# Optimizing a Trainium2 kernel written in Bass

```python
import numpy as np
import jax
import jax.numpy as jnp

def _softmax(x, axis=-1):
    return jax.nn.softmax(x, axis=axis)

def _gelu(x):
    return jax.nn.gelu(x, approximate=True)

def _silu(x):
    return jax.nn.silu(x)

def _sigmoid(x):
    return jax.nn.sigmoid(x)

def _layernorm(x, axis=-1, eps=1e-05):
    m = jnp.mean(x, axis=axis, keepdims=True)
    v = jnp.var(x, axis=axis, keepdims=True)
    return (x - m) / jnp.sqrt(v + eps)

def _scatter_add(tgt, idx, src, axis=0):
    return tgt.at[idx].add(src)

def _segment_sum(src, seg, n):
    return jax.ops.segment_sum(src, seg, n)
kernel_name = 'mk_decoder_preln_d2_seqx_r4_c74ec9'

def setup_inputs(seed: int=0):
    np.random.seed(seed)
    _w = jnp.asarray

    def _rec_inputs():
        import jax
        import jax.numpy as jnp
        _rk = jax.random.key(seed)
        x = 7.22e-05 + 1 * jax.random.normal(jax.random.fold_in(_rk, 1), (32, 112, 256), jnp.float32)
        _lenS = 112 - jax.random.randint(jax.random.fold_in(_rk, 7), (32,), 0, max(1, 112 // 4) + 1, jnp.int32)
        _lenS2 = 375 - jax.random.randint(jax.random.fold_in(_rk, 8), (32,), 0, max(1, 375 // 4) + 1, jnp.int32)
        _ctx_768P = jax.random.normal(jax.random.fold_in(_rk, 11), (32, 16, 192), jnp.float32)
        _ctx_768c = jax.random.dirichlet(jax.random.fold_in(_rk, 511), 0.3 * jnp.ones((16,), jnp.float32), (32, 375))
        _ctx_768t = jnp.einsum('bsk,bkd->bsd', _ctx_768c, _ctx_768P)
        _ctx_768t = _ctx_768t * jax.lax.rsqrt(jnp.mean(jnp.square(_ctx_768t)) + 1e-12) * 0.953939
        ctx_768 = 2.09791e-05 + 1.00001 * (_ctx_768t + 0.3 * jax.random.normal(jax.random.fold_in(_rk, 611), (32, 375, 192), jnp.float32))
        return (x, ctx_768)
    x, ctx_768 = _rec_inputs()

    def _L0_attn_setup():
        import jax, jax.numpy as jnp
        import numpy as np
        RSQRT2 = 2 ** (-0.5)
        B, S, D_IN = (2, 1024, 256)
        H, D_HEAD = (8, 64)
        QK_DIM = H * D_HEAD
        V_DIM = H * D_HEAD
        OUT_DIM = D_IN
        LN_EPS = 1e-05

        def _layernorm(y, gamma, beta):
            mu = jnp.mean(y, axis=-1, keepdims=True)
            var = jnp.mean(jnp.square(y - mu), axis=-1, keepdims=True)
            return (y - mu) * jax.lax.rsqrt(var + LN_EPS) * gamma + beta
        key = jax.random.key(seed)
        ks = jax.random.split(key, 8)

        def lecun(k, fan_in, shape):
            return jax.random.normal(k, shape, dtype=jnp.float32) * (1.0 / np.sqrt(fan_in))
        return {'x': jax.random.normal(ks[0], (B, S, D_IN), dtype=jnp.float32), 'W_qk': lecun(ks[1], D_IN, (D_IN, 2 * QK_DIM)), 'b_qk': jnp.zeros((2 * QK_DIM,), jnp.float32), 'W_v': lecun(ks[2], D_IN, (D_IN, V_DIM)), 'b_v': jnp.zeros((V_DIM,), jnp.float32), 'W_out': lecun(ks[3], V_DIM, (V_DIM, OUT_DIM)), 'b_out': jnp.zeros((OUT_DIM,), jnp.float32), 'ln_gamma': jnp.ones((OUT_DIM,), jnp.float32), 'ln_beta': jnp.zeros((OUT_DIM,), jnp.float32)}
    _L0_attn_all = _L0_attn_setup()
    _L0_attn_in = {k: v for k, v in _L0_attn_all.items() if k in ('W_qk', 'b_qk', 'W_v', 'b_v', 'W_out', 'b_out', 'ln_gamma', 'ln_beta')}
    del _L0_attn_all

    def _L0_xattn_setup():
        import jax, jax.numpy as jnp
        import numpy as np
        IN_DIM = 256
        CTX_DIM = 192
        NUM_HEADS = 16
        HEAD_DIM = IN_DIM // NUM_HEADS
        SCALE = 1.0 / float(np.sqrt(HEAD_DIM))
        key = jax.random.key(seed)
        ks = jax.random.split(key, 10)
        B, NQ, NKV = (8, 256, 128)
        s_in = 1.0 / float(np.sqrt(IN_DIM))
        s_ctx = 1.0 / float(np.sqrt(CTX_DIM))
        return {'x': jax.random.normal(ks[0], (B, NQ, IN_DIM), dtype=jnp.float32), 'context': jax.random.normal(ks[1], (B, NKV, CTX_DIM), dtype=jnp.float32), 'Wq': jax.random.normal(ks[2], (IN_DIM, IN_DIM), dtype=jnp.float32) * s_in, 'bq': jax.random.normal(ks[3], (IN_DIM,), dtype=jnp.float32) * 0.01, 'Wk': jax.random.normal(ks[4], (IN_DIM, CTX_DIM), dtype=jnp.float32) * s_ctx, 'bk': jax.random.normal(ks[5], (IN_DIM,), dtype=jnp.float32) * 0.01, 'Wv': jax.random.normal(ks[6], (IN_DIM, CTX_DIM), dtype=jnp.float32) * s_ctx, 'bv': jax.random.normal(ks[7], (IN_DIM,), dtype=jnp.float32) * 0.01, 'Wo': jax.random.normal(ks[8], (IN_DIM, IN_DIM), dtype=jnp.float32) * s_in, 'bo': jax.random.normal(ks[9], (IN_DIM,), dtype=jnp.float32) * 0.01}
    _L0_xattn_all = _L0_xattn_setup()
    _L0_xattn_in = {k: v for k, v in _L0_xattn_all.items() if k in ('Wq', 'bq', 'Wk', 'bk', 'Wv', 'bv', 'Wo', 'bo')}
    del _L0_xattn_all

    def _L0_ffn_setup():
        import jax, jax.numpy as jnp
        import numpy as np
        B, T, D = (2, 512, 256)
        E, K, FF = (8, 2, 1024)

        def _reference_tuple_inner(x, gate_w, gate_b, w1, b1, w2, b2):
            n_experts = w1.shape[0]
            gate_logits = x @ gate_w + gate_b
            topk_vals, topk_idx = jax.lax.top_k(gate_logits, K)
            topk_w = jax.nn.softmax(topk_vals, axis=-1)
            onehot = jax.nn.one_hot(topk_idx, n_experts, dtype=x.dtype)
            comb = jnp.sum(onehot * topk_w[..., None], axis=2)
            h = jax.nn.gelu(jnp.einsum('btd,edf->ebtf', x, w1) + b1[:, None, None, :], approximate=False)
            y = jnp.einsum('ebtf,efd->ebtd', h, w2) + b2[:, None, None, :]
            output = jnp.einsum('ebtd,bte->btd', y, comb)
            expert_counts = jnp.sum(onehot, axis=(0, 1, 2)).astype(jnp.float32)
            return (output, gate_logits, topk_idx, expert_counts)
        key = jax.random.key(seed)
        ks = jax.random.split(key, 4)
        scale = 0.02
        return {'x': jax.random.normal(ks[0], (B, T, D), jnp.float32), 'gate_w': jax.random.normal(ks[1], (D, E), jnp.float32) * scale, 'gate_b': jnp.zeros((E,), jnp.float32), 'w1': jax.random.normal(ks[2], (E, D, FF), jnp.float32) * scale, 'b1': jnp.zeros((E, FF), jnp.float32), 'w2': jax.random.normal(ks[3], (E, FF, D), jnp.float32) * scale, 'b2': jnp.zeros((E, D), jnp.float32)}
    _L0_ffn_all = _L0_ffn_setup()
    _L0_ffn_in = {k: v for k, v in _L0_ffn_all.items() if k in ('gate_w', 'gate_b', 'w1', 'b1', 'w2', 'b2')}
    del _L0_ffn_all

    def _L1_attn_setup():
        import jax, jax.numpy as jnp
        import numpy as np
        D = 256
        E = 2 * D
        S = 128
        LN_EPS = 1e-05
        key = jax.random.key(seed)
        ks = jax.random.split(key, 4)
        bs, seq_len = (4, 512)
        x = jax.random.normal(ks[0], (bs, seq_len, D), dtype=jnp.float32)
        W_in = jax.random.normal(ks[1], (D, 2 * E + S), dtype=jnp.float32) / np.sqrt(D)
        b_in = jnp.zeros((2 * E + S,), dtype=jnp.float32)
        W_out = jax.random.normal(ks[2], (E, D), dtype=jnp.float32) / np.sqrt(E)
        b_out = jnp.zeros((D,), dtype=jnp.float32)
        ln_g = jnp.ones((D,), dtype=jnp.float32)
        ln_b = jnp.zeros((D,), dtype=jnp.float32)
        gamma_q = jnp.ones((S,), dtype=jnp.float32)
        beta_q = jnp.zeros((S,), dtype=jnp.float32)
        gamma_k = jnp.ones((S,), dtype=jnp.float32)
        beta_k = jnp.zeros((S,), dtype=jnp.float32)
        return {'x': x, 'ln_g': ln_g, 'ln_b': ln_b, 'W_in': W_in, 'b_in': b_in, 'W_out': W_out, 'b_out': b_out, 'gamma_q': gamma_q, 'beta_q': beta_q, 'gamma_k': gamma_k, 'beta_k': beta_k}
    _L1_attn_all = _L1_attn_setup()
    _L1_attn_in = {k: v for k, v in _L1_attn_all.items() if k in ('ln_g', 'ln_b', 'W_in', 'b_in', 'W_out', 'b_out', 'gamma_q', 'beta_q', 'gamma_k', 'beta_k')}
    del _L1_attn_all

    def _L1_xattn_setup():
        import jax, jax.numpy as jnp
        import numpy as np
        D = 256
        L = 192
        H = 16
        EPS = 1e-05

        def layer_norm(x, g, b):
            mu = jnp.mean(x, axis=-1, keepdims=True)
            var = jnp.var(x, axis=-1, keepdims=True)
            return (x - mu) * jax.lax.rsqrt(var + EPS) * g + b
        key = jax.random.key(seed)
        ks = jax.random.split(key, 8)
        B, T, N = (4, 1024, 128)
        sq = lambda d: 1.0 / np.sqrt(d)
        return {'x': jax.random.normal(ks[0], (B, T, D), jnp.float32), 'xf': jax.random.normal(ks[1], (B, N, L), jnp.float32), 'norm_g': jnp.ones((D,), jnp.float32), 'norm_b': jnp.zeros((D,), jnp.float32), 'tnorm_g': jnp.ones((L,), jnp.float32), 'tnorm_b': jnp.zeros((L,), jnp.float32), 'Wq': jax.random.normal(ks[2], (D, D), jnp.float32) * sq(D), 'bq': jnp.zeros((D,), jnp.float32), 'Wk': jax.random.normal(ks[3], (L, D), jnp.float32) * sq(L), 'bk': jnp.zeros((D,), jnp.float32), 'Wv': jax.random.normal(ks[4], (L, D), jnp.float32) * sq(L), 'bv': jnp.zeros((D,), jnp.float32)}
    _L1_xattn_all = _L1_xattn_setup()
    _L1_xattn_in = {k: v for k, v in _L1_xattn_all.items() if k in ('norm_g', 'norm_b', 'tnorm_g', 'tnorm_b', 'Wq', 'bq', 'Wk', 'bk', 'Wv', 'bv')}
    del _L1_xattn_all

    def _L1_ffn_setup():
        import jax, jax.numpy as jnp
        import numpy as np
        B, T, D, E, H, K = (4, 512, 256, 8, 512, 2)
        key = jax.random.key(seed)
        k0, k1, k2, k3 = jax.random.split(key, 4)
        x = jax.random.normal(k0, (B, T, D), dtype=jnp.float32)
        router_w = jax.random.normal(k1, (E, D), dtype=jnp.float32) * D ** (-0.5)
        w1 = jax.random.normal(k2, (E, D, H), dtype=jnp.float32) * D ** (-0.5)
        w2 = jax.random.normal(k3, (E, H, D), dtype=jnp.float32) * H ** (-0.5)
        return {'x': x, 'router_w': router_w, 'w1': w1, 'w2': w2}
    _L1_ffn_all = _L1_ffn_setup()
    _L1_ffn_in = {k: v for k, v in _L1_ffn_all.items() if k in ('router_w', 'w1', 'w2')}
    del _L1_ffn_all
    return {'x': x, 'ctx_768': ctx_768, 'L0_attn_W_qk': _L0_attn_in['W_qk'], 'L0_attn_b_qk': _L0_attn_in['b_qk'], 'L0_attn_W_v': _L0_attn_in['W_v'], 'L0_attn_b_v': _L0_attn_in['b_v'], 'L0_attn_W_out': _L0_attn_in['W_out'], 'L0_attn_b_out': _L0_attn_in['b_out'], 'L0_attn_ln_gamma': _L0_attn_in['ln_gamma'], 'L0_attn_ln_beta': _L0_attn_in['ln_beta'], 'L0_xattn_Wq': _L0_xattn_in['Wq'], 'L0_xattn_bq': _L0_xattn_in['bq'], 'L0_xattn_Wk': _L0_xattn_in['Wk'], 'L0_xattn_bk': _L0_xattn_in['bk'], 'L0_xattn_Wv': _L0_xattn_in['Wv'], 'L0_xattn_bv': _L0_xattn_in['bv'], 'L0_xattn_Wo': _L0_xattn_in['Wo'], 'L0_xattn_bo': _L0_xattn_in['bo'], 'L0_ffn_gate_w': _L0_ffn_in['gate_w'], 'L0_ffn_gate_b': _L0_ffn_in['gate_b'], 'L0_ffn_w1': _L0_ffn_in['w1'], 'L0_ffn_b1': _L0_ffn_in['b1'], 'L0_ffn_w2': _L0_ffn_in['w2'], 'L0_ffn_b2': _L0_ffn_in['b2'], 'L1_attn_ln_g': _L1_attn_in['ln_g'], 'L1_attn_ln_b': _L1_attn_in['ln_b'], 'L1_attn_W_in': _L1_attn_in['W_in'], 'L1_attn_b_in': _L1_attn_in['b_in'], 'L1_attn_W_out': _L1_attn_in['W_out'], 'L1_attn_b_out': _L1_attn_in['b_out'], 'L1_attn_gamma_q': _L1_attn_in['gamma_q'], 'L1_attn_beta_q': _L1_attn_in['beta_q'], 'L1_attn_gamma_k': _L1_attn_in['gamma_k'], 'L1_attn_beta_k': _L1_attn_in['beta_k'], 'L1_xattn_norm_g': _L1_xattn_in['norm_g'], 'L1_xattn_norm_b': _L1_xattn_in['norm_b'], 'L1_xattn_tnorm_g': _L1_xattn_in['tnorm_g'], 'L1_xattn_tnorm_b': _L1_xattn_in['tnorm_b'], 'L1_xattn_Wq': _L1_xattn_in['Wq'], 'L1_xattn_bq': _L1_xattn_in['bq'], 'L1_xattn_Wk': _L1_xattn_in['Wk'], 'L1_xattn_bk': _L1_xattn_in['bk'], 'L1_xattn_Wv': _L1_xattn_in['Wv'], 'L1_xattn_bv': _L1_xattn_in['bv'], 'L1_ffn_router_w': _L1_ffn_in['router_w'], 'L1_ffn_w1': _L1_ffn_in['w1'], 'L1_ffn_w2': _L1_ffn_in['w2']}

def reference(x, ctx_768, L0_attn_W_qk, L0_attn_b_qk, L0_attn_W_v, L0_attn_b_v, L0_attn_W_out, L0_attn_b_out, L0_attn_ln_gamma, L0_attn_ln_beta, L0_xattn_Wq, L0_xattn_bq, L0_xattn_Wk, L0_xattn_bk, L0_xattn_Wv, L0_xattn_bv, L0_xattn_Wo, L0_xattn_bo, L0_ffn_gate_w, L0_ffn_gate_b, L0_ffn_w1, L0_ffn_b1, L0_ffn_w2, L0_ffn_b2, L1_attn_ln_g, L1_attn_ln_b, L1_attn_W_in, L1_attn_b_in, L1_attn_W_out, L1_attn_b_out, L1_attn_gamma_q, L1_attn_beta_q, L1_attn_gamma_k, L1_attn_beta_k, L1_xattn_norm_g, L1_xattn_norm_b, L1_xattn_tnorm_g, L1_xattn_tnorm_b, L1_xattn_Wq, L1_xattn_bq, L1_xattn_Wk, L1_xattn_bk, L1_xattn_Wv, L1_xattn_bv, L1_ffn_router_w, L1_ffn_w1, L1_ffn_w2):
    import jax
    import jax.numpy as jnp

    def _L0_attn_ref(x, W_qk, b_qk, W_v, b_v, W_out, b_out, ln_gamma, ln_beta):
        import jax, jax.numpy as jnp
        import numpy as np
        RSQRT2 = 2 ** (-0.5)
        B, S, D_IN = (2, 1024, 256)
        H, D_HEAD = (8, 64)
        QK_DIM = H * D_HEAD
        V_DIM = H * D_HEAD
        OUT_DIM = D_IN
        LN_EPS = 1e-05

        def _layernorm(y, gamma, beta):
            mu = jnp.mean(y, axis=-1, keepdims=True)
            var = jnp.mean(jnp.square(y - mu), axis=-1, keepdims=True)
            return (y - mu) * jax.lax.rsqrt(var + LN_EPS) * gamma + beta
        b, s, _ = x.shape
        scale = D_HEAD ** (-0.5)
        qk = x @ W_qk + b_qk
        qk = qk.reshape(b, s, H, D_HEAD, 2)
        q, k = (qk[..., 0], qk[..., 1])
        v = (x @ W_v + b_v).reshape(b, s, H, D_HEAD)
        sim = jnp.einsum('bihd,bjhd->bhij', q, k) * scale
        attn = jax.nn.softmax(sim, axis=-1)
        o = jnp.einsum('bhij,bjhd->bihd', attn, v)
        o = o.reshape(b, s, V_DIM)
        y = _layernorm(o @ W_out + b_out, ln_gamma, ln_beta)
        return (y + x) * RSQRT2

    def _L0_xattn_ref(x, context, Wq, bq, Wk, bk, Wv, bv, Wo, bo):
        import jax, jax.numpy as jnp
        import numpy as np
        IN_DIM = 256
        CTX_DIM = 192
        NUM_HEADS = 16
        HEAD_DIM = IN_DIM // NUM_HEADS
        SCALE = 1.0 / float(np.sqrt(HEAD_DIM))
        q = x @ Wq.T + bq
        k = context @ Wk.T + bk
        v = context @ Wv.T + bv
        B, NQ, _ = q.shape
        NKV = k.shape[1]
        q = q.reshape(B, NQ, NUM_HEADS, HEAD_DIM)
        k = k.reshape(B, NKV, NUM_HEADS, HEAD_DIM)
        v = v.reshape(B, NKV, NUM_HEADS, HEAD_DIM)
        attn = jnp.einsum('bihd,bjhd->bhij', q, k) * SCALE
        attn = jax.nn.softmax(attn, axis=-1)
        out = jnp.einsum('bhij,bjhd->bihd', attn, v)
        out = out.reshape(B, NQ, IN_DIM)
        return out @ Wo.T + bo

    def _L0_ffn_ref(x, gate_w, gate_b, w1, b1, w2, b2):
        import jax, jax.numpy as jnp
        import numpy as np
        B, T, D = (2, 512, 256)
        E, K, FF = (8, 2, 1024)

        def _reference_tuple_inner(x, gate_w, gate_b, w1, b1, w2, b2):
            n_experts = w1.shape[0]
            gate_logits = x @ gate_w + gate_b
            topk_vals, topk_idx = jax.lax.top_k(gate_logits, K)
            topk_w = jax.nn.softmax(topk_vals, axis=-1)
            onehot = jax.nn.one_hot(topk_idx, n_experts, dtype=x.dtype)
            comb = jnp.sum(onehot * topk_w[..., None], axis=2)
            h = jax.nn.gelu(jnp.einsum('btd,edf->ebtf', x, w1) + b1[:, None, None, :], approximate=False)
            y = jnp.einsum('ebtf,efd->ebtd', h, w2) + b2[:, None, None, :]
            output = jnp.einsum('ebtd,bte->btd', y, comb)
            expert_counts = jnp.sum(onehot, axis=(0, 1, 2)).astype(jnp.float32)
            return (output, gate_logits, topk_idx, expert_counts)
        return _reference_tuple_inner(x, gate_w, gate_b, w1, b1, w2, b2)[0]

    def _L1_attn_ref(x, ln_g, ln_b, W_in, b_in, W_out, b_out, gamma_q, beta_q, gamma_k, beta_k):
        import jax, jax.numpy as jnp
        import numpy as np
        D = 256
        E = 2 * D
        S = 128
        LN_EPS = 1e-05
        seq_len = x.shape[1]
        mu = jnp.mean(x, axis=-1, keepdims=True)
        var = jnp.mean(jnp.square(x - mu), axis=-1, keepdims=True)
        xn = (x - mu) * jax.lax.rsqrt(var + LN_EPS) * ln_g + ln_b
        uvz = jax.nn.silu(jnp.einsum('bld,df->blf', xn, W_in) + b_in)
        u, v, z = (uvz[..., :E], uvz[..., E:2 * E], uvz[..., 2 * E:])
        q = z * gamma_q + beta_q
        k = z * gamma_k + beta_k
        attn = jnp.einsum('bqs,bks->bqk', q, k) / seq_len
        attn = jnp.square(jax.nn.relu(attn))
        out = u * jnp.einsum('bqk,bke->bqe', attn, v)
        return x + jnp.einsum('ble,ed->bld', out, W_out) + b_out

    def _L1_xattn_ref(x, xf, norm_g, norm_b, tnorm_g, tnorm_b, Wq, bq, Wk, bk, Wv, bv):
        import jax, jax.numpy as jnp
        import numpy as np
        D = 256
        L = 192
        H = 16
        EPS = 1e-05

        def layer_norm(x, g, b):
            mu = jnp.mean(x, axis=-1, keepdims=True)
            var = jnp.var(x, axis=-1, keepdims=True)
            return (x - mu) * jax.lax.rsqrt(var + EPS) * g + b
        B, T, _ = x.shape
        N = xf.shape[1]
        hd = D // H
        xn = layer_norm(x, norm_g, norm_b)
        xfn = layer_norm(xf, tnorm_g, tnorm_b)
        q = (xn @ Wq + bq).reshape(B, T, H, hd)
        k = (xfn @ Wk + bk).reshape(B, N, H, hd)
        v = (xfn @ Wv + bv).reshape(B, N, H, hd)
        scores = jnp.einsum('bthd,bnhd->bhtn', q, k) / jnp.sqrt(jnp.float32(hd))
        w = jax.nn.softmax(scores, axis=-1)
        y = jnp.einsum('bhtn,bnhd->bthd', w, v).reshape(B, T, D)
        return y

    def _L1_ffn_ref(x, router_w, w1, w2):
        import jax, jax.numpy as jnp
        import numpy as np
        B, T, D, E, H, K = (4, 512, 256, 8, 512, 2)
        Bb, Tt, Dd = x.shape
        N = Bb * Tt
        logits = jnp.einsum('btd,ed->bte', x, router_w)
        top_vals, top_idx = jax.lax.top_k(logits, K)
        top_w = jax.nn.softmax(top_vals, axis=-1)
        xf = x.reshape(N, Dd)
        h = jnp.einsum('nd,edh->enh', xf, w1)
        h = jnp.square(jax.nn.relu(h))
        y = jnp.einsum('enh,ehd->end', h, w2)
        idx_f = top_idx.reshape(N, K)
        w_f = top_w.reshape(N, K)
        y_sel = y[idx_f, jnp.arange(N)[:, None]]
        out = jnp.einsum('nk,nkd->nd', w_f, y_sel)
        return out.reshape(Bb, Tt, Dd)
    x = x + _L0_attn_ref(_layernorm(x, axis=-1), L0_attn_W_qk, L0_attn_b_qk, L0_attn_W_v, L0_attn_b_v, L0_attn_W_out, L0_attn_b_out, L0_attn_ln_gamma, L0_attn_ln_beta)
    x = x + _L0_xattn_ref(_layernorm(x, axis=-1), ctx_768, L0_xattn_Wq, L0_xattn_bq, L0_xattn_Wk, L0_xattn_bk, L0_xattn_Wv, L0_xattn_bv, L0_xattn_Wo, L0_xattn_bo)
    x = x + _L0_ffn_ref(_layernorm(x, axis=-1), L0_ffn_gate_w, L0_ffn_gate_b, L0_ffn_w1, L0_ffn_b1, L0_ffn_w2, L0_ffn_b2)
    x = x + _L1_attn_ref(_layernorm(x, axis=-1), L1_attn_ln_g, L1_attn_ln_b, L1_attn_W_in, L1_attn_b_in, L1_attn_W_out, L1_attn_b_out, L1_attn_gamma_q, L1_attn_beta_q, L1_attn_gamma_k, L1_attn_beta_k)
    x = x + _L1_xattn_ref(_layernorm(x, axis=-1), ctx_768, L1_xattn_norm_g, L1_xattn_norm_b, L1_xattn_tnorm_g, L1_xattn_tnorm_b, L1_xattn_Wq, L1_xattn_bq, L1_xattn_Wk, L1_xattn_bk, L1_xattn_Wv, L1_xattn_bv)
    x = x + _L1_ffn_ref(_layernorm(x, axis=-1), L1_ffn_router_w, L1_ffn_w1, L1_ffn_w2)
    return x

_drawn_inputs = setup_inputs


def setup_inputs(seed=0):
    import zlib

    import numpy as np

    out = dict(_drawn_inputs(seed))
    spreads = {'L0_attn_b_qk': (0.0, 0.1),
     'L0_attn_b_v': (0.0, 0.1),
     'L0_attn_b_out': (0.0, 0.1),
     'L0_attn_ln_gamma': (1.0, 0.2),
     'L0_attn_ln_beta': (0.0, 0.1),
     'L0_ffn_gate_b': (0.0, 0.1),
     'L0_ffn_b1': (0.0, 0.301),
     'L0_ffn_b2': (0.0, 0.1),
     'L1_attn_ln_g': (1.0, 0.2),
     'L1_attn_ln_b': (0.0, 0.1),
     'L1_attn_b_in': (0.0, 0.1),
     'L1_attn_b_out': (0.0, 0.1),
     'L1_attn_gamma_q': (1.0, 0.2),
     'L1_attn_beta_q': (0.0, 0.332),
     'L1_attn_gamma_k': (1.0, 0.2),
     'L1_attn_beta_k': (0.0, 0.292),
     'L1_xattn_norm_g': (1.0, 0.534),
     'L1_xattn_norm_b': (0.0, 0.393),
     'L1_xattn_tnorm_g': (1.0, 0.2),
     'L1_xattn_tnorm_b': (0.0, 0.1),
     'L1_xattn_bq': (0.0, 0.44),
     'L1_xattn_bk': (0.0, 2.0),
     'L1_xattn_bv': (0.0, 0.1)}
    factors = {'L0_xattn_bq': 21.63, 'L0_xattn_bk': 64.0, 'L0_xattn_bv': 3.221, 'L0_xattn_bo': 4.187}
    for name, (base, spread) in spreads.items():
        noise = np.random.default_rng([zlib.crc32(name.encode()), seed]).standard_normal(out[name].shape)
        drawn = base * np.exp(spread * noise) if base else spread * noise
        out[name] = jnp.asarray(drawn.astype(out[name].dtype))
    for name, factor in factors.items():
        out[name] = (out[name] * factor).astype(out[name].dtype)
    return out
```

```python
from contextlib import ExitStack

import numpy as np

import concourse.bass as bass
from concourse import mybir

ALU = mybir.AluOpType
ACT = mybir.ActivationFunctionType
F32 = mybir.dt.float32
AX_X = mybir.AxisListType.X

P = 128
EPS = 1e-5
GROUP = 4
ONE = 1
LAST_STAGE = 6


def wide(ap, axis, n):
    shape = list(ap.shape)
    shape[axis] = n
    return ap.broadcast_to(shape)


class Parts:
    pass


class Chain:

    def __init__(self, eng, sem, before=0, length=None):
        self.eng, self.sem, self.before, self.length, self.n = eng, sem, before, length, 0

    def __call__(self, ins):
        self.n += 1
        ins.then_inc(self.sem, 1)
        self.eng.wait_ge(self.sem, self.before + self.n)

    def close(self):
        assert self.length == self.n, (self.length, self.n)


def decoder(nc, d, out):
    B, T, D = d["x"].shape
    NG = B // GROUP
    GT = GROUP * T
    KD = D // P
    NKV = d["ctx_768"].shape[1]
    DC = d["ctx_768"].shape[2]
    KB = 125
    NJ = NKV // KB
    C1 = DC - P
    XH, XD = 16, D // 16
    AH, AD = 8, 64
    E = 8

    ctx = ExitStack()
    with ctx:
        def sb(name, shape, dt=F32):
            return ctx.enter_context(nc.sbuf_tensor(name, shape, dt))

        stage_sems = []

        def sem(name):
            stage_sems.append(nc.alloc_semaphore(name=name))
            return stage_sems[-1]

        counts = []

        def count(name):
            counts.append(sem(name))
            return counts[-1]

        def start_counts():
            for s in counts:
                nc.gpsimd.sem_inc(s, ONE)
            counts.clear()
            nc.all_engine_barrier()

        def end_stage():
            nc.clear_and_free_semaphores(list(stage_sems))
            nc.all_engine_barrier()
            stage_sems.clear()

        bank = [ctx.enter_context(nc.psum_tensor(f"bank{i}", [P, 512], F32)) for i in range(8)]

        x = sb("x_res", [T, B, D])
        mv = sb("x_mean_var", [T, B, 2])
        rstd = sb("x_rstd", [T, B])
        ident = sb("ident", [P, P])
        norm_tmp = sb("norm_tmp", [T, 3, B])
        stat6 = sb("stat6", [T, B, 6])
        scratch = sb("scratch", [P, GROUP])

        w = Parts()
        w.q = sb("w_q", [P, KD, AH * AD])
        w.k = sb("w_k", [P, KD, AH * AD])
        w.v = sb("w_v", [P, KD, AH * AD])
        w.o = sb("w_o", [P, 4, D])
        w.bq = sb("w_bq", [P, 4])
        w.bk = sb("w_bk", [P, 4])
        w.bv = sb("w_bv", [P, 4])
        w.bo = sb("w_bo", [T, D])
        w.ln_g = sb("w_ln_g", [T, D])
        w.ln_b = sb("w_ln_b", [T, D])
        w.in_ = sb("w_in", [P, KD, 1152])
        w.out = sb("w_out", [P, 4, D])
        w.b_in_u = sb("w_b_in_u", [P, 9])
        w.b_in_v = sb("w_b_in_v", [T, 512])
        w.b_out = sb("w_b_out", [T, D])
        w.gq = sb("w_gq", [P, 4])
        w.ln_gb = sb("w_ln_gb", [P, 2 * KD])
        w.ln_b_wide = sb("w_ln_b_wide", [P, KD, T])
        xa = []
        for n in range(2):
            a = Parts()
            a.wq = sb(f"x{n}_wq", [P, KD, D])
            a.wk = sb(f"x{n}_wk", [P, 2, D])
            a.wv = sb(f"x{n}_wv", [P, 2, D])
            a.bq = sb(f"x{n}_bq", [P, 1, KD])
            a.bk = sb(f"x{n}_bk", [P, KD])
            a.bv = sb(f"x{n}_bv", [P, D])
            xa.append(a)
        xa[0].wo = sb("x0_wo", [P, KD, D])
        xa[0].bo = sb("x0_bo", [T, D])
        xa[1].gb = sb("x1_gb", [P, 8])
        xa[1].b_wide = sb("x1_b_wide", [P, 4, P])
        head_mask = sb("head_mask", [P, P // XD])

        FOLD_WIDE = KD + 2
        loads = sem("setup_loads")
        const_ready = sem("const_ready")
        fold_chain = sem("fold_chain")
        fold_ps = sem("fold_ps")

        def cols(ap, k):
            return ap if k > 1 else ap.rearrange("(p k) -> p k", k=1)

        def rows(ap, parts):
            return ap.partition_broadcast(parts)

        setup_loads = [
            (w.q[:], d["L0_Wq"].rearrange("(k p) n -> p k n", p=P)),
            (w.k[:], d["L0_Wk"].rearrange("(k p) n -> p k n", p=P)),
            (w.v[:], d["L0_attn_W_v"].rearrange("(k p) n -> p k n", p=P)),
            (w.o[:], d["L0_attn_W_out"].rearrange("(k p) n -> p k n", p=P)),
            (w.bq[:], cols(d["L0_bq"], 4)),
            (w.bk[:], cols(d["L0_bk"], 4)),
            (w.bv[:], cols(d["L0_attn_b_v"], 4)),
            (w.bo[:], rows(d["L0_attn_b_out"], T)),
            (w.ln_g[:], rows(d["L0_attn_ln_gamma"], T)),
            (w.ln_b[:], rows(d["L0_attn_ln_beta"], T)),
            (w.in_[:], d["L1_attn_W_in"].rearrange("(k p) n -> p k n", p=P)),
            (w.out[:], d["L1_attn_W_out"].rearrange("(k p) n -> p k n", p=P)),
            (w.b_in_u[:], cols(d["L1_b_in_cols"], 9)),
            (w.b_in_v[:], rows(d["L1_attn_b_in"][512:1024], T)),
            (w.b_out[:], rows(d["L1_attn_b_out"], T)),
            (w.gq[:, 0:1], cols(d["L1_attn_gamma_q"], 1)),
            (w.gq[:, 1:2], cols(d["L1_attn_beta_q"], 1)),
            (w.gq[:, 2:3], cols(d["L1_attn_gamma_k"], 1)),
            (w.gq[:, 3:4], cols(d["L1_attn_beta_k"], 1)),
            (w.ln_gb[:, 0:KD], cols(d["L1_attn_ln_g"], KD)),
            (w.ln_gb[:, KD:2 * KD], cols(d["L1_attn_ln_b"], KD)),
            (xa[0].wq[:], d["L0_xWq_T"].rearrange("(k p) n -> p k n", p=P)),
            (xa[0].wk[:, 0, :], d["L0_xWk_T"][0:P, :]),
            (xa[0].wk[0:C1, 1, :], d["L0_xWk_T"][P:DC, :]),
            (xa[0].wv[:, 0, :], d["L0_xWv_T"][0:P, :]),
            (xa[0].wv[0:C1, 1, :], d["L0_xWv_T"][P:DC, :]),
            (xa[0].wo[:], d["L0_xWo_T"].rearrange("(k p) n -> p k n", p=P)),
            (xa[0].bq[:, 0, :], cols(d["L0_xattn_bq"], KD)),
            (xa[0].bk[:], cols(d["L0_xattn_bk"], KD)),
            (xa[0].bv[:], rows(d["L0_xattn_bv"], P)),
            (xa[0].bo[:], rows(d["L0_xattn_bo"], T)),
            (xa[1].wq[:], d["L1_xattn_Wq"].rearrange("(k p) n -> p k n", p=P)),
            (xa[1].wk[:, 0, :], d["L1_xattn_Wk"][0:P, :]),
            (xa[1].wk[0:C1, 1, :], d["L1_xattn_Wk"][P:DC, :]),
            (xa[1].wv[:, 0, :], d["L1_xattn_Wv"][0:P, :]),
            (xa[1].wv[0:C1, 1, :], d["L1_xattn_Wv"][P:DC, :]),
            (xa[1].bq[:, 0, :], cols(d["L1_xattn_bq"], KD)),
            (xa[1].bk[:], cols(d["L1_xattn_bk"], KD)),
            (xa[1].bv[:], rows(d["L1_xattn_bv"], P)),
            (xa[1].gb[:, 0:KD], cols(d["L1_xattn_norm_g"], KD)),
            (xa[1].gb[:, KD:2 * KD], cols(d["L1_xattn_norm_b"], KD)),
            (xa[1].gb[:, 4:5], cols(d["L1_xattn_tnorm_g"][0:P], 1)),
            (xa[1].gb[0:C1, 5:6], d["L1_xattn_tnorm_g"][P:DC].rearrange("(p a) -> p a", a=1)),
            (xa[1].gb[:, 6:7], cols(d["L1_xattn_tnorm_b"][0:P], 1)),
            (xa[1].gb[0:C1, 7:8], d["L1_xattn_tnorm_b"][P:DC].rearrange("(p a) -> p a", a=1)),
            (x[:], d["x"].rearrange("b t d -> t b d")),
        ]

        def residual_stats(dve, b, col=None):
            if col is not None:
                dve.memset(scratch[0:T, col:col + 1], 0.0)
            dve.bn_stats(stat6[:, b, :], x[:, b, :])

        with nc.Block() as block:
            @block.sync
            def _(sp):
                for dst, src in setup_loads:
                    sp.dma_start(dst, src).then_inc(loads, 16)

            @block.gpsimd
            def _(pool):
                made = Chain(pool, const_ready)
                made(pool.memset(ident[:], 0.0))
                made(pool.affine_select(out=ident[:], in_=ident[:], compare_op=ALU.not_equal, fill=1.0,
                                        base=0, pattern=[[-1, P]], channel_multiplier=1))
                made(pool.memset(head_mask[:], XD ** -0.5))
                made(pool.affine_select(out=head_mask[:], in_=head_mask[:], compare_op=ALU.is_ge, fill=0.0,
                                        base=0, pattern=[[-XD, P // XD]], channel_multiplier=1))
                made(pool.affine_select(out=head_mask[:], in_=head_mask[:], compare_op=ALU.is_ge, fill=0.0,
                                        base=XD - 1, pattern=[[XD, P // XD]], channel_multiplier=-1))

            @block.vector
            def _(dve):
                fold = Chain(dve, fold_chain)
                dve.wait_ge(loads, 16 * len(setup_loads))
                dve.wait_ge(const_ready, 5)
                for k in range(KD):
                    fold(dve.tensor_scalar(w.ln_b_wide[:, k, :], ident[:, 0:T], 0.0,
                                           w.ln_gb[:, KD + k:KD + k + 1], ALU.mult, ALU.add))
                for k in range(2):
                    n = P if k == 0 else C1
                    fold(dve.tensor_scalar(xa[1].b_wide[0:n, 2 + k, :], ident[0:n, :], 0.0,
                                           xa[1].gb[0:n, 6 + k:7 + k], ALU.mult, ALU.add))
                assert fold.n == FOLD_WIDE
                dve.wait_ge(fold_ps, 1)
                fold(dve.tensor_tensor(w.bo[:], w.bo[:], bank[0][0:T, 0:D], ALU.add))
                fold(dve.tensor_tensor(w.b_in_v[:], w.b_in_v[:], bank[1][0:T, :], ALU.add))
                fold(dve.tensor_tensor(w.b_in_u[:], w.b_in_u[:], bank[2][:, 0:9], ALU.add))
                fold(dve.tensor_tensor(xa[1].bq[:, 0, :], xa[1].bq[:, 0, :], bank[2][:, 16:16 + KD], ALU.add))
                fold(dve.tensor_tensor(xa[1].bk[:], xa[1].bk[:], bank[2][:, 32:32 + KD], ALU.add))
                fold(dve.tensor_tensor(xa[1].bv[:], xa[1].bv[:], bank[3][:, 0:D], ALU.add))
                for k in range(KD):
                    fold(dve.tensor_scalar(w.in_[:, k, :], w.in_[:, k, :], w.ln_gb[:, k:k + 1], None, ALU.mult))
                    fold(dve.tensor_scalar(xa[1].wq[:, k, :], xa[1].wq[:, k, :], xa[1].gb[:, k:k + 1], None,
                                           ALU.mult))
                    n = P if k == 0 else C1
                    for wt in (xa[1].wk, xa[1].wv):
                        fold(dve.tensor_scalar(wt[0:n, k, :], wt[0:n, k, :], xa[1].gb[0:n, 4 + k:5 + k], None,
                                               ALU.mult))
                for b in range(B):
                    residual_stats(dve, b)

            @block.tensor
            def _(pe):
                pe.wait_ge(loads, 16 * len(setup_loads))
                pe.wait_ge(fold_chain, FOLD_WIDE)
                for k in range(4):
                    pe.matmul(bank[0][0:T, 0:D], wide(w.bv[:, k:k + 1], 1, T), w.o[:, k, :],
                              start=(k == 0), stop=(k == 3))
                for k in range(KD):
                    pe.matmul(bank[1][0:T, :], w.ln_b_wide[:, k, :], w.in_[:, k, 512:1024],
                              start=(k == 0), stop=(k == KD - 1))
                for m in range(9):
                    for k in range(KD):
                        pe.matmul(bank[2][:, m:m + 1], w.in_[:, k, m * P:(m + 1) * P],
                                  w.ln_gb[:, KD + k:KD + k + 1], start=(k == 0), stop=(k == KD - 1))
                for m in range(KD):
                    for k in range(KD):
                        pe.matmul(bank[2][:, 16 + m:17 + m], xa[1].wq[:, k, m * P:(m + 1) * P],
                                  xa[1].gb[:, KD + k:KD + k + 1], start=(k == 0), stop=(k == KD - 1))
                    for k in range(2):
                        n = P if k == 0 else C1
                        pe.matmul(bank[2][:, 32 + m:33 + m], xa[1].wk[0:n, k, m * P:(m + 1) * P],
                                  xa[1].gb[0:n, 6 + k:7 + k], start=(k == 0), stop=(k == 1))
                for k in range(2):
                    n = P if k == 0 else C1
                    last = pe.matmul(bank[3][:, 0:D], xa[1].b_wide[0:n, 2 + k, :], xa[1].wv[0:n, k, :],
                                     start=(k == 0), stop=(k == 1))
                last.then_inc(fold_ps, 1)

        def mean_var(dve, chain, six, stats, tmp, width):
            chain(dve.tensor_tensor(tmp[:, 0, :], six[:, :, 1], six[:, :, 4], ALU.add))
            chain(dve.tensor_tensor(tmp[:, 1, :], six[:, :, 1], six[:, :, 4], ALU.subtract))
            chain(dve.tensor_tensor(tmp[:, 2, :], six[:, :, 2], six[:, :, 5], ALU.add))
            chain(dve.tensor_scalar(stats[:, :, 0], tmp[:, 0, :], 0.5, None, ALU.mult))
            chain(dve.tensor_tensor(tmp[:, 1, :], tmp[:, 1, :], tmp[:, 1, :], ALU.mult))
            chain(dve.tensor_scalar(tmp[:, 1, :], tmp[:, 1, :], 0.25, None, ALU.mult))
            chain(dve.tensor_scalar(tmp[:, 2, :], tmp[:, 2, :], 1.0 / width, None, ALU.mult))
            chain(dve.tensor_tensor(stats[:, :, 1], tmp[:, 1, :], tmp[:, 2, :], ALU.add))

        def make_rstd_dve(dve, chain, std_ready, std_asked, stats, rs, tmp, double, six=None, width=D):
            if six is not None:
                mean_var(dve, chain, six, stats, tmp, width)
            chain(dve.tensor_scalar(tmp[:, 0, :], stats[:, :, 1], 1.0 + EPS if double else 1.0,
                                    EPS * EPS if double else EPS, ALU.mult, ALU.add))
            dve.sem_inc(std_asked, 1)
            dve.wait_ge(std_ready, 1)
            chain(dve.reciprocal(tmp[:, 2, :], tmp[:, 1, :]))
            chain(dve.tensor_tensor(tmp[:, 1, :], tmp[:, 2, :], tmp[:, 2, :], ALU.mult))
            chain(dve.tensor_tensor(tmp[:, 1, :], tmp[:, 1, :], tmp[:, 0, :], ALU.mult))
            chain(dve.tensor_scalar(tmp[:, 1, :], tmp[:, 1, :], -0.5, 1.5, ALU.mult, ALU.add))
            chain(dve.tensor_tensor(rs, tmp[:, 2, :], tmp[:, 1, :], ALU.mult))

        def make_rstd_act(act, std_ready, std_asked, tmp):
            act.wait_ge(std_asked, 1)
            act.activation(tmp[:, 1, :], tmp[:, 0, :], ACT.Sqrt).then_inc(std_ready, 1)

        env = Parts()
        env.nc, env.d, env.B, env.T, env.D, env.NG, env.GT, env.KD = (
            nc, d, B, T, D, NG, GT, KD)
        env.NKV, env.DC, env.KB, env.NJ, env.C1, env.XH, env.XD, env.AH = (
            NKV, DC, KB, NJ, C1, XH, XD, AH)
        env.AD, env.E, env.bank, env.x, env.mv, env.rstd, env.ident, env.norm_tmp = (
            AD, E, bank, x, mv, rstd, ident, norm_tmp)
        env.stat6, env.scratch, env.head_mask, env.w, env.xa, env.sem, env.count, env.start_counts = (
            stat6, scratch, head_mask, w, xa, sem, count, start_counts)
        env.residual_stats, env.make_rstd_dve, env.make_rstd_act = (
            residual_stats, make_rstd_dve, make_rstd_act)
        end_stage()
        stages = [self_attention, lambda e: cross_attention(e, 0), lambda e: experts(e, 0),
                  gated_attention, lambda e: cross_attention(e, 1), lambda e: experts(e, 1)]
        for stage in stages[:LAST_STAGE]:
            stage(env)
            end_stage()

        stored = sem("out_stored")
        with nc.Block() as block:
            @block.sync
            def _(sp):
                sp.dma_start(out.rearrange("b t d -> t b d"), x[:]).then_inc(stored, 16)
                sp.wait_ge(stored, 16)


def self_attention(e):
    nc, sem, bank, x, mv, rstd, ident, w = e.nc, e.sem, e.bank, e.x, e.mv, e.rstd, e.ident, e.w
    T, D, B, NG, GT, KD, H, HD = e.T, e.D, e.B, e.NG, e.GT, e.KD, e.AH, e.AD
    UNITS = GROUP * 2
    HU = H // 2
    with ExitStack() as st:
        def sb(name, shape):
            return st.enter_context(nc.sbuf_tensor(name, shape, F32))

        y_all = sb("sa_y", [T, B, D])
        y_mv = sb("sa_y_mv", [T, B, 2])
        y_rstd = sb("sa_y_rstd", [T, B])
        y_tmp = sb("sa_y_tmp", [T, 3, B])
        y_stat = sb("sa_y_stat", [T, B, 6])
        xn = sb("sa_xn", [T, GROUP, D])
        xnT = sb("sa_xnT", [P, KD, GT])
        qT = sb("sa_qT", [P, 4, GT])
        kT = sb("sa_kT", [P, 4, GT])
        v = sb("sa_v", [T, GROUP, H, HD + 1])
        mx = sb("sa_max", [T, 2, HU])
        prob = sb("sa_prob", [T, 2, HU, T])
        probT = sb("sa_probT", [T, 2, HU, T])
        rinv = sb("sa_rinv", [T, 2, HU])
        o = sb("sa_o", [T, 2, H, HD])
        oT = sb("sa_oT", [P, 2, 4, T])

        count, flag = e.count, sem
        std_asked, std_ready = flag("sa_std_asked"), flag("sa_std_ready")
        pre = flag("sa_pre")
        xn_ready = count("sa_xn_ready")
        xT_ps = count("sa_xT_ps")
        xT_ready = count("sa_xT_ready")
        qk_ps = count("sa_qk_ps")
        q_ready, k_ready = count("sa_q_ready"), count("sa_k_ready")
        v_ps, v_ready = count("sa_v_ps"), count("sa_v_ready")
        s_ps = count("sa_scores_ps")
        mx_done = count("sa_max_done")
        shifted = count("sa_shifted")
        exp_done = count("sa_exp_done")
        pT_ps, pT_ready = count("sa_probT_ps"), count("sa_probT_ready")
        pv_ps = count("sa_pv_ps")
        rinv_done = count("sa_rinv_done")
        o_ready = count("sa_o_ready")
        oT_ps, oT_ready = count("sa_oT_ps"), count("sa_oT_ready")
        y_ps, y_done = count("sa_y_ps"), count("sa_y_done")

        e.start_counts()
        with nc.Block() as block:
            @block.tensor
            def _(pe):
                with pe.Fori(0, NG) as g:
                    pe.wait_ge(xn_ready, ONE + g * GROUP + GROUP)
                    for k in range(KD):
                        for s in range(GROUP):
                            last = pe.transpose(bank[k][:, s * T:(s + 1) * T], xn[:, s, k * P:(k + 1) * P],
                                                ident[0:T, 0:T])
                        last.then_inc(xT_ps, 1)
                    for m in range(4):
                        for side, (wt, ready) in enumerate(((w.q, q_ready), (w.k, k_ready))):
                            if m == 0 and side == 0:
                                pe.wait_ge(xT_ready, ONE + g * 2 + 2)
                            if m > 0:
                                pe.wait_ge(ready, ONE + g * 4 + m)
                            for k in range(KD):
                                last = pe.matmul(bank[2 + side][:, 0:GT], wt[:, k, m * P:(m + 1) * P],
                                                 xnT[:, k, :], start=(k == 0), stop=(k == KD - 1))
                            last.then_inc(qk_ps, 1)
                    for s in range(GROUP):
                        if s >= 2:
                            pe.wait_ge(v_ready, ONE + g * GROUP + s - 1)
                        for k in range(KD):
                            last = pe.matmul(bank[s % 2][0:T, :], xnT[:, k, s * T:(s + 1) * T], w.v[:, k, :],
                                             start=(k == 0), stop=(k == KD - 1))
                        last.then_inc(v_ps, 1)
                    pe.wait_ge(q_ready, ONE + g * 4 + 4)
                    pe.wait_ge(k_ready, ONE + g * 4 + 4)

                    def scores(u):
                        s = u // 2
                        if u >= 2:
                            pe.wait_ge(shifted, ONE + g * UNITS + u - 1)
                        for i in range(HU):
                            h = 2 * i + u % 2
                            p0 = HD * (h % 2)
                            last = pe.matmul(bank[4 + u % 2][0:T, i * T:(i + 1) * T],
                                             qT[p0:p0 + HD, h // 2, s * T:(s + 1) * T],
                                             kT[p0:p0 + HD, h // 2, s * T:(s + 1) * T], start=True, stop=True)
                        last.then_inc(s_ps, 1)

                    def turn_prob(u):
                        pe.wait_ge(exp_done, ONE + g * UNITS + u + 1)
                        if u < 2:
                            pe.wait_ge(v_ready, ONE + g * GROUP + 4)
                        for i in range(HU):
                            last = pe.transpose(bank[u % 2][0:T, i * T:(i + 1) * T], prob[:, u % 2, i, :],
                                                ident[0:T, 0:T])
                        last.then_inc(pT_ps, 1)

                    def values(u):
                        s = u // 2
                        pe.wait_ge(pT_ready, ONE + g * UNITS + u + 1)
                        if u >= 2:
                            pe.wait_ge(o_ready, ONE + g * UNITS + u - 1)
                        for i in range(HU):
                            h = 2 * i + u % 2
                            last = pe.matmul(bank[2 + u % 2][0:T, i * (HD + 1):(i + 1) * (HD + 1)],
                                             probT[:, u % 2, i, :], v[:, s, h, :], start=True, stop=True)
                        last.then_inc(pv_ps, 1)

                    def turn_out(s):
                        pe.wait_ge(o_ready, ONE + g * UNITS + 2 * s + 2)
                        ov = o[:, s % 2].rearrange("t h e -> t (h e)")
                        for k in range(4):
                            last = pe.transpose(bank[6][:, k * T:(k + 1) * T], ov[:, k * P:(k + 1) * P],
                                                ident[0:T, 0:T])
                        last.then_inc(oT_ps, 1)

                    def project(s):
                        pe.wait_ge(oT_ready, ONE + g * GROUP + s + 1)
                        pe.wait_ge(y_done, ONE + g * GROUP + s)
                        for k in range(4):
                            last = pe.matmul(bank[7][0:T, 0:D], oT[:, s % 2, k, :], w.o[:, k, :],
                                             start=(k == 0), stop=(k == 3))
                        last.then_inc(y_ps, 1)

                    scores(0)
                    scores(1)
                    for u in range(UNITS):
                        turn_prob(u)
                        if u + 2 < UNITS:
                            scores(u + 2)
                        values(u)
                        if u % 2 == 1 and u >= 3:
                            turn_out((u - 3) // 2)
                        if u % 2 == 0 and u >= 4:
                            project((u - 4) // 2)
                    project(GROUP - 2)
                    turn_out(GROUP - 1)
                    project(GROUP - 1)

            @block.scalar
            def _(act):
                e.make_rstd_act(act, std_ready, std_asked, e.norm_tmp)
                with act.Fori(0, NG) as g:
                    for k in range(KD):
                        act.wait_ge(xT_ps, ONE + g * 2 + k + 1)
                        act.wait_ge(v_ps, ONE + g * GROUP)
                        act.activation(xnT[:, k, :], bank[k][:, 0:GT], ACT.Copy).then_inc(xT_ready, 1)
                    for m in range(4):
                        act.wait_ge(qk_ps, ONE + g * 8 + 2 * m + 1)
                        act.wait_ge(s_ps, ONE + g * UNITS)
                        act.activation(qT[:, m, :], bank[2][:, 0:GT], ACT.Identity,
                                       bias=w.bq[:, m:m + 1]).then_inc(q_ready, 1)

                    def exp(u):
                        act.wait_ge(shifted, ONE + g * UNITS + u + 1)
                        act.activation(prob[:, u % 2], prob[:, u % 2], ACT.Exp,
                                       scale=HD ** -0.5).then_inc(exp_done, 1)

                    def copy_probT(u):
                        act.wait_ge(pT_ps, ONE + g * UNITS + u + 1)
                        if u >= 2:
                            act.wait_ge(pv_ps, ONE + g * UNITS + u - 1)
                        else:
                            act.wait_ge(pv_ps, ONE + g * UNITS)
                        act.activation(probT[:, u % 2].rearrange("t a b -> t (a b)"), bank[u % 2][0:T, 0:HU * T],
                                       ACT.Copy).then_inc(pT_ready, 1)

                    def copy_oT(s):
                        act.wait_ge(oT_ps, ONE + g * GROUP + s + 1)
                        if s >= 2:
                            act.wait_ge(y_ps, ONE + g * GROUP + s - 1)
                        else:
                            act.wait_ge(y_ps, ONE + g * GROUP)
                        act.activation(oT[:, s % 2].rearrange("p a b -> p (a b)"), bank[6][:, 0:4 * T],
                                       ACT.Copy).then_inc(oT_ready, 1)

                    exp(0)
                    for u in range(UNITS):
                        if u + 1 < UNITS:
                            exp(u + 1)
                        copy_probT(u)
                        if u % 2 == 1 and u >= 3:
                            copy_oT((u - 3) // 2)
                    copy_oT(GROUP - 1)

            @block.vector
            def _(dve):
                chain = Chain(dve, pre)
                e.make_rstd_dve(dve, chain, std_ready, std_asked, mv, rstd[:], e.norm_tmp, False, e.stat6)
                chain(dve.memset(v[:, :, :, HD:HD + 1], 1.0))
                with dve.Fori(0, NG) as g:
                    dve.wait_ge(xT_ps, ONE + g * 2)
                    for s in range(GROUP):
                        b = g * GROUP + s
                        dve.tensor_scalar(xn[:, s, :], x[:, b, :], mv[:, b, 0:1], rstd[:, bass.ds(b, 1)],
                                          ALU.subtract, ALU.mult).then_inc(xn_ready, 1)
                    for m in range(4):
                        dve.wait_ge(qk_ps, ONE + g * 8 + 2 * m + 2)
                        dve.wait_ge(s_ps, ONE + g * UNITS)
                        dve.tensor_scalar(kT[:, m, :], bank[3][:, 0:GT], w.bk[:, m:m + 1], None,
                                          ALU.add).then_inc(k_ready, 1)
                    for s in range(GROUP):
                        dve.wait_ge(v_ps, ONE + g * GROUP + s + 1)
                        dve.wait_ge(pv_ps, ONE + g * UNITS)
                        dve.tensor_copy(v[:, s, :, 0:HD],
                                        bank[s % 2][0:T, :].rearrange("t (h e) -> t h e", e=HD))\
                           .then_inc(v_ready, 1)

                    def shift(u):
                        dve.wait_ge(s_ps, ONE + g * UNITS + u + 1)
                        sc = bank[4 + u % 2][0:T, 0:HU * T].rearrange("t (h k) -> t h k", k=T)
                        dve.tensor_reduce(mx[:, u % 2, :], sc, AX_X, ALU.max).then_inc(mx_done, 1)
                        dve.wait_ge(mx_done, ONE + g * UNITS + u + 1)
                        if u >= 2:
                            dve.wait_ge(pT_ps, ONE + g * UNITS + u - 1)
                        else:
                            dve.wait_ge(pT_ps, ONE + g * UNITS)
                        dve.tensor_tensor(prob[:, u % 2], sc, wide(mx[:, u % 2, :].unsqueeze(2), 2, T),
                                          ALU.subtract).then_inc(shifted, 1)

                    def normalise(u):
                        s = u // 2
                        pv = bank[2 + u % 2][0:T, 0:HU * (HD + 1)].rearrange("t (h e) -> t h e", e=HD + 1)
                        dve.wait_ge(pv_ps, ONE + g * UNITS + u + 1)
                        dve.reciprocal(rinv[:, u % 2, :], pv[:, :, HD]).then_inc(rinv_done, 1)
                        dve.wait_ge(rinv_done, ONE + g * UNITS + u + 1)
                        if s >= 2:
                            dve.wait_ge(oT_ps, ONE + g * GROUP + s - 1)
                        else:
                            dve.wait_ge(oT_ps, ONE + g * GROUP)
                        dve.tensor_tensor(o[:, s % 2, u % 2::2, :], pv[:, :, 0:HD],
                                          wide(rinv[:, u % 2, :].unsqueeze(2), 2, HD), ALU.mult)\
                           .then_inc(o_ready, 1)

                    def keep_y(s):
                        dve.wait_ge(y_ps, ONE + g * GROUP + s + 1)
                        dve.tensor_tensor(y_all[:, g * GROUP + s, :], bank[7][0:T, 0:D], w.bo[:],
                                          ALU.add).then_inc(y_done, 1)

                    shift(0)
                    shift(1)
                    for u in range(UNITS):
                        if u + 2 < UNITS:
                            shift(u + 2)
                        normalise(u)
                        if u % 2 == 0 and u >= 4:
                            keep_y((u - 4) // 2)
                    keep_y(GROUP - 2)
                    keep_y(GROUP - 1)

        y_asked, y_std = flag("sa_y_std_asked"), flag("sa_y_std")
        ychain = flag("sa_y_chain")
        loop_chain = flag("sa_fin_chain")
        with nc.Block() as block:
            @block.scalar
            def _(act):
                e.make_rstd_act(act, y_std, y_asked, y_tmp)

            @block.vector
            def _(dve):
                chain = Chain(dve, ychain)
                for b in range(B):
                    last = dve.bn_stats(y_stat[:, b, :], y_all[:, b, :])
                chain(last)
                e.make_rstd_dve(dve, chain, y_std, y_asked, y_mv, y_rstd[:], y_tmp, False, y_stat)
                with dve.Fori(0, NG) as g:
                    n = 2 * GROUP + 4
                    link = Chain(dve, loop_chain, g * n, n)
                    for s in range(GROUP):
                        b = g * GROUP + s
                        yb = y_all[:, b, :]
                        link(dve.tensor_scalar(yb, yb, y_mv[:, b, 0:1], y_rstd[:, bass.ds(b, 1)],
                                               ALU.subtract, ALU.mult))
                        link(dve.tensor_scalar(xn[:, s, :], x[:, b, :], mv[:, b, 0:1], rstd[:, bass.ds(b, 1)],
                                               ALU.subtract, ALU.mult))
                    yg = y_all[:, bass.ds(g * GROUP, GROUP), :]
                    xg = x[:, bass.ds(g * GROUP, GROUP), :]
                    link(dve.tensor_tensor(yg, yg, wide(w.ln_g[:].unsqueeze(1), 1, GROUP), ALU.mult))
                    link(dve.tensor_tensor(yg, yg, wide(w.ln_b[:].unsqueeze(1), 1, GROUP), ALU.add))
                    link(dve.tensor_tensor(yg, yg, xn[:], ALU.add))
                    link(dve.scalar_tensor_tensor(out=xg, in0=yg, scalar=2.0 ** -0.5, in1=xg, op0=ALU.mult,
                                                  op1=ALU.add))
                    for s in range(GROUP):
                        e.residual_stats(dve, g * GROUP + s, s)
                    link.close()


def cross_attention(e, layer):
    nc, sem, bank, x, mv, rstd, ident, d = e.nc, e.sem, e.bank, e.x, e.mv, e.rstd, e.ident, e.d
    T, D, B, NG, KD, H, HD = e.T, e.D, e.B, e.NG, e.KD, e.XH, e.XD
    KB, NJ, NKV, DC, C1 = e.KB, e.NJ, e.NKV, e.DC, e.C1
    a = e.xa[layer]
    n_ = f"x{layer}_"
    JOB = (bank[0], bank[4])
    SCORE = (bank[5], bank[6], bank[7])
    PT = (bank[2], bank[3])
    PV = bank[1]
    NH = GROUP * H
    AHEAD = 2
    with ExitStack() as st:
        def sb(name, shape):
            return st.enter_context(nc.sbuf_tensor(n_ + name, shape, F32))

        def count(name):
            return e.count(n_ + name)

        def flag(name):
            return sem(n_ + name)

        ctxT = sb("ctxT", [P, 2, 2, NKV])
        xn = sb("xn", [T, 2, D])
        xnT = sb("xnT", [P, 2, KD, T])
        qT = sb("qT", [P, 2, H, T])
        kT = sb("kT", [P, 2, KD, NKV])
        v = sb("v", [KB, 2, NJ, H, HD + 1])
        mx = sb("neg_max", [T, 4])
        prob = sb("prob", [T, 4, NKV])
        probT = sb("probT", [KB, 4, NJ, T])
        rinv = sb("rinv", [T, 2, H])
        o = sb("o", [T, 2, H, HD])
        oT = sb("oT", [P, 2, KD, T])
        y = sb("y", [T, 2, D])
        if layer == 1:
            cnat = sb("cnat", [KB, 2, NJ, DC])
            cmv = sb("cmv", [KB, B * NJ, 2])
            crstd = sb("crstd", [KB, B * NJ])
            ctmp = sb("ctmp", [KB, 3, B * NJ])
            cstat = sb("cstat", [KB, B * NJ, 6])

        std_asked, std_ready, pre = flag("std_asked"), flag("std_ready"), flag("pre")
        ctx_loaded = [flag("ctx_even"), flag("ctx_odd")]
        cn_ready, cT_ps, cT0_ready, cT1_ready = count("cn_ready"), count("cT_ps"), count("cT0_ready"), count("cT1_ready")
        xn_ready, xT_ps, xT_ready = count("xn_ready"), count("xT_ps"), count("xT_ready")
        q_ps, q_ready = count("q_ps"), count("q_ready")
        k_ps, k0_ready, k1_ready = count("k_ps"), count("k0_ready"), count("k1_ready")
        v_ps, v01_ready, v2_ready = count("v_ps"), count("v01_ready"), count("v2_ready")
        s_ps, max_done, exp_done = count("scores_ps"), count("max_done"), count("exp_done")
        pT_ps, pT_act, pT_dve = count("probT_ps"), count("probT_act"), count("probT_dve")
        pv_ps, rinv_done, o_ready, o_biased = count("pv_ps"), count("rinv_done"), count("o_ready"), count("o_biased")
        oT_ps, oT_ready, y_ps, y_read = count("oT_ps"), count("oT_ready"), count("y_ps"), count("y_read")
        tail = flag("tail")

        if layer == 1:
            c_asked, c_std, c_chain, c_dma = flag("c_std_asked"), flag("c_std"), flag("c_chain"), flag("c_dma")
            c_dma2, c_read = flag("c_dma_odd"), count("c_read")
            e.start_counts()
            with nc.Block() as block:
                @block.sync
                def _(sp):
                    with sp.Fori(0, B // 2) as i:
                        for r in range(2):
                            sp.wait_ge(c_read, ONE + i * 2)
                            sp.dma_start(cnat[:, r], d["ctx_768"][bass.ds(i * 2 + r, 1)].rearrange(
                                "b (j p) c -> p (b j) c", p=KB)).then_inc((c_dma, c_dma2)[r], 16)

                @block.scalar
                def _(act):
                    e.make_rstd_act(act, c_std, c_asked, ctmp)

                @block.vector
                def _(dve):
                    with dve.Fori(0, B // 2) as i:
                        for r in range(2):
                            dve.wait_ge(c_read, ONE + i * 2)
                            dve.wait_ge((c_dma, c_dma2)[r], i * 16 + 16)
                            dve.memset(e.scratch[:, r:r + 1], 0.0)
                            for j in range(NJ):
                                last = dve.bn_stats(cstat[:, (i * 2 + r) * NJ + j, :], cnat[:, r, j, :])
                            last.then_inc(c_read, 1)
                    dve.wait_ge(c_read, ONE + B)
                    chain = Chain(dve, c_chain)
                    e.make_rstd_dve(dve, chain, c_std, c_asked, cmv, crstd[:], ctmp, False, cstat, DC)

        e.start_counts()
        with nc.Block() as block:
            @block.sync
            def _(sp):
                with sp.Fori(0, NG) as g:
                    for s in range(GROUP):
                        b = g * GROUP + s
                        r = s % 2
                        if layer == 0:
                            sp.wait_ge(v_ps, ONE + g * (2 * GROUP) + (2 * (s - 1) if s >= 2 else 0))
                            sp.dma_start(ctxT[:, r, 0, :], d["ctx_T"][0:P, bass.ds(b, 1), :].rearrange(
                                "c b k -> c (b k)")).then_inc(ctx_loaded[r], 16)
                            sp.dma_start(ctxT[0:C1, r, 1, :], d["ctx_T"][P:DC, bass.ds(b, 1), :].rearrange(
                                "c b k -> c (b k)")).then_inc(ctx_loaded[r], 16)
                        else:
                            sp.wait_ge(cT_ps, ONE + g * (2 * GROUP) + (2 * (s - 1) if s >= 2 else 0))
                            sp.dma_start(cnat[:, r], d["ctx_768"][bass.ds(b, 1)].rearrange(
                                "b (j p) c -> p (b j) c", p=KB)).then_inc(ctx_loaded[r], 16)

            @block.tensor
            def _(pe):
                with pe.Fori(0, NG) as g:
                    def job(s, j):
                        b = g * GROUP + s
                        r = s % 2
                        to = JOB[j % 2]
                        if j in (0, 1) and layer == 1:
                            if j == 0:
                                pe.wait_ge(cn_ready, ONE + b + 1)
                                pe.wait_ge(v01_ready, ONE + b)
                                pe.wait_ge(v2_ready, ONE + b)
                            n = P if j == 0 else C1
                            for c in range(NJ):
                                last = pe.transpose(to[0:n, c * KB:(c + 1) * KB], cnat[:, r, c, j * P:j * P + n],
                                                    ident[0:KB, 0:KB])
                            last.then_inc(cT_ps, 1)
                        if j == 2:
                            pe.wait_ge(xn_ready, ONE + b + 1)
                            if layer == 1:
                                pe.wait_ge(cT0_ready, ONE + b + 1)
                            else:
                                pe.wait_ge(v01_ready, ONE + b)
                            for k in range(KD):
                                last = pe.transpose(to[:, k * T:(k + 1) * T], xn[:, r, k * P:(k + 1) * P],
                                                    ident[0:T, 0:T])
                            last.then_inc(xT_ps, 1)
                        if j == 3:
                            pe.wait_ge(xT_ready, ONE + b + 1)
                            if layer == 1:
                                pe.wait_ge(cT1_ready, ONE + b + 1)
                            else:
                                pe.wait_ge(v2_ready, ONE + b)
                            for m in range(KD):
                                for k in range(KD):
                                    last = pe.matmul(to[:, m * T:(m + 1) * T], a.wq[:, k, m * P:(m + 1) * P],
                                                     xnT[:, r, k, :], start=(k == 0), stop=(k == KD - 1))
                            last.then_inc(q_ps, 1)
                        if j in (4, 5):
                            m = j - 4
                            if j == 4 and layer == 0:
                                pe.wait_ge(ctx_loaded[r], g * (16 * GROUP) + 32 * (s // 2 + 1))
                            if j == 5:
                                pe.wait_ge(q_ready, ONE + b + 1)
                            for k in range(2):
                                n = P if k == 0 else C1
                                last = pe.matmul(to[:, 0:NKV], a.wk[0:n, k, m * P:(m + 1) * P],
                                                 ctxT[0:n, r, k, :], start=(k == 0), stop=(k == 1))
                            last.then_inc(k_ps, 1)
                        if j in (6, 7):
                            pe.wait_ge(k0_ready if j == 6 else k1_ready, ONE + b + 1)
                            for c in (range(2) if j == 6 else range(2, NJ)):
                                for k in range(2):
                                    n = P if k == 0 else C1
                                    at = c % 2 * D
                                    last = pe.matmul(to[0:KB, at:at + D], ctxT[0:n, r, k, c * KB:(c + 1) * KB],
                                                     a.wv[0:n, k, :], start=(k == 0), stop=(k == 1))
                            last.then_inc(v_ps, 1)

                    def scores(i):
                        s, h = divmod(i, H)
                        r = s % 2
                        b = g * GROUP + s
                        if h == 0:
                            pe.wait_ge(q_ready, ONE + b + 1)
                            pe.wait_ge(k0_ready, ONE + b + 1)
                            pe.wait_ge(k1_ready, ONE + b + 1)
                        pe.wait_ge(exp_done, ONE + g * NH + (i - 2 if i >= 3 else 0))
                        pe.matmul(SCORE[i % 3][0:T, 0:NKV], qT[:, r, h, :], kT[:, r, h // (P // HD), :],
                                  start=True, stop=True).then_inc(s_ps, 1)

                    def turn_prob(i):
                        pe.wait_ge(exp_done, ONE + g * NH + i + 1)
                        half = g * (NH // 2) + (i // 2 if i >= 2 else 0)
                        pe.wait_ge(pT_dve if i % 2 else pT_act, ONE + half)
                        for c in range(NJ):
                            last = pe.transpose(PT[i % 2][0:KB, c * T:(c + 1) * T],
                                                prob[:, i % 4, c * KB:(c + 1) * KB], ident[0:T, 0:T])
                        last.then_inc(pT_ps, 1)

                    def values(i):
                        s, h = divmod(i, H)
                        if h == 0:
                            pe.wait_ge(v01_ready, ONE + g * GROUP + s + 1)
                            pe.wait_ge(v2_ready, ONE + g * GROUP + s + 1)
                            pe.wait_ge(o_ready, ONE + g * GROUP + s)
                        pe.wait_ge(pT_dve if i % 2 else pT_act, ONE + g * (NH // 2) + i // 2 + 1)
                        for c in range(NJ):
                            last = pe.matmul(PV[0:T, h * (HD + 1):(h + 1) * (HD + 1)], probT[:, i % 4, c, :],
                                             v[:, s % 2, c, h, :], start=(c == 0), stop=(c == NJ - 1))
                        last.then_inc(pv_ps, 1)

                    def turn_out(s):
                        pe.wait_ge(o_biased, ONE + g * GROUP + s + 1)
                        ov = o[:, s % 2].rearrange("t h e -> t (h e)")
                        for k in range(KD):
                            last = pe.transpose(bank[0][:, k * T:(k + 1) * T], ov[:, k * P:(k + 1) * P],
                                                ident[0:T, 0:T])
                        last.then_inc(oT_ps, 1)

                    def project(s):
                        pe.wait_ge(oT_ready, ONE + g * GROUP + s + 1)
                        for k in range(KD):
                            last = pe.matmul(bank[4][0:T, 0:D], oT[:, s % 2, k, :], a.wo[:, k, :],
                                             start=(k == 0), stop=(k == KD - 1))
                        last.then_inc(y_ps, 1)

                    first = 0 if layer == 1 else 2
                    for j in range(first, 8):
                        job(0, j)
                    for i in range(NH + AHEAD + 1):
                        if i < NH:
                            scores(i)
                        if 0 <= i - AHEAD < NH:
                            turn_prob(i - AHEAD)
                        if i - AHEAD - 1 >= 0:
                            values(i - AHEAD - 1)
                        s, h = divmod(i, H)
                        if layer == 0 and h == 4 and s >= 1:
                            pe.wait_ge(v01_ready, ONE + g * GROUP + s + 1)
                            turn_out(s - 1)
                        if layer == 0 and h == 5 and s >= 1:
                            pe.wait_ge(v2_ready, ONE + g * GROUP + s + 1)
                            project(s - 1)
                        if s < GROUP - 1 and 7 <= h < 15 and h - 7 >= first:
                            if layer == 0 and s >= 1 and h - 7 == first:
                                pe.wait_ge(oT_ready, ONE + g * GROUP + s)
                                pe.wait_ge(y_read, ONE + g * GROUP + s)
                            job(s + 1, h - 7)
                    if layer == 0:
                        turn_out(GROUP - 1)
                        pe.wait_ge(y_read, ONE + g * GROUP + GROUP - 1)
                        project(GROUP - 1)
                        pe.wait_ge(y_read, ONE + g * GROUP + GROUP)

            @block.scalar
            def _(act):
                e.make_rstd_act(act, std_ready, std_asked, e.norm_tmp)
                with act.Fori(0, NG) as g:
                    def copies(s, j):
                        b = g * GROUP + s
                        r = s % 2
                        if j == 0 and layer == 1:
                            act.wait_ge(cT_ps, ONE + g * (2 * GROUP) + 2 * s + 1)
                            act.wait_ge(v_ps, ONE + g * (2 * GROUP) + (2 * (s - 1) if s >= 2 else 0))
                            act.activation(ctxT[:, r, 0, :], JOB[0][:, 0:NKV], ACT.Copy).then_inc(cT0_ready, 1)
                        if j == 2:
                            act.wait_ge(xT_ps, ONE + b + 1)
                            act.activation(xnT[:, r].rearrange("p k t -> p (k t)"), JOB[0][:, 0:KD * T],
                                           ACT.Copy).then_inc(xT_ready, 1)
                        if j == 4:
                            act.wait_ge(k_ps, ONE + g * (2 * GROUP) + 2 * s + 1)
                            act.wait_ge(s_ps, ONE + g * NH + (H * (s - 1) if s >= 2 else 0))
                            act.activation(kT[:, r, 0, :], JOB[0][:, 0:NKV], ACT.Identity,
                                           bias=a.bk[:, 0:1]).then_inc(k0_ready, 1)
                        if j == 6:
                            act.wait_ge(v_ps, ONE + g * (2 * GROUP) + 2 * s + 1)
                            act.wait_ge(pv_ps, ONE + g * NH + (H * (s - 1) if s >= 2 else 0))
                            act.activation(v[:, r, 0:2, :, 0:HD],
                                           JOB[0][0:KB, :].rearrange("p (c h e) -> p c h e", c=2, e=HD),
                                           ACT.Copy).then_inc(v01_ready, 1)

                    def exp(i):
                        act.wait_ge(max_done, ONE + g * NH + i + 1)
                        act.wait_ge(pT_ps, ONE + g * NH + (i - 3 if i >= 4 else 0))
                        act.activation(prob[:, i % 4, :], SCORE[i % 3][0:T, 0:NKV], ACT.Exp,
                                       bias=mx[:, i % 4:i % 4 + 1]).then_inc(exp_done, 1)

                    def copy_probT(i):
                        act.wait_ge(pT_ps, ONE + g * NH + i + 1)
                        act.wait_ge(pv_ps, ONE + g * NH + (i - 3 if i >= 4 else 0))
                        act.activation(probT[:, i % 4].rearrange("k c t -> k (c t)"), PT[0][0:KB, 0:NJ * T],
                                       ACT.Copy).then_inc(pT_act, 1)

                    def copy_oT(s):
                        act.wait_ge(oT_ps, ONE + g * GROUP + s + 1)
                        act.wait_ge(y_ps, ONE + g * GROUP + max(s - 1, 0))
                        act.activation(oT[:, s % 2].rearrange("p k t -> p (k t)"), bank[0][:, 0:KD * T],
                                       ACT.Copy).then_inc(oT_ready, 1)

                    for j in range(8):
                        copies(0, j)
                    for i in range(NH + AHEAD + 1):
                        if i < NH:
                            exp(i)
                        if 0 <= i - AHEAD < NH and (i - AHEAD) % 2 == 0:
                            copy_probT(i - AHEAD)
                        s, h = divmod(i, H)
                        if layer == 0 and h == 4 and s >= 1:
                            copy_oT(s - 1)
                        if s < GROUP - 1 and 7 <= h < 15:
                            copies(s + 1, h - 7)
                    if layer == 0:
                        copy_oT(GROUP - 1)

            @block.vector
            def _(dve):
                chain = Chain(dve, pre)
                e.make_rstd_dve(dve, chain, std_ready, std_asked, mv, rstd[:], e.norm_tmp, layer == 1, e.stat6)
                chain(dve.memset(v[:, :, :, :, HD:HD + 1], 1.0))
                n_tail = 1
                with dve.Fori(0, NG) as g:
                    link = Chain(dve, tail, g * GROUP * n_tail, GROUP * n_tail)

                    def norm_context(s):
                        b = g * GROUP + s
                        r = s % 2
                        dve.wait_ge(ctx_loaded[r], g * (8 * GROUP) + 16 * (s // 2 + 1))
                        for c in range(NJ):
                            row = b * NJ + c
                            last = dve.tensor_scalar(cnat[:, r, c, :], cnat[:, r, c, :], cmv[:, row, 0:1],
                                                     crstd[:, bass.ds(row, 1)], ALU.subtract, ALU.mult)
                        last.then_inc(cn_ready, 1)

                    def copies(s, j):
                        b = g * GROUP + s
                        r = s % 2
                        if j == 1:
                            dve.wait_ge(xT_ps, ONE + g * GROUP + max(s - 1, 0))
                            dve.tensor_scalar(xn[:, r, :], x[:, b, :], mv[:, b, 0:1], rstd[:, bass.ds(b, 1)],
                                              ALU.subtract, ALU.mult).then_inc(xn_ready, 1)
                            if layer == 1:
                                dve.wait_ge(cT_ps, ONE + g * (2 * GROUP) + 2 * s + 2)
                                dve.wait_ge(v_ps, ONE + g * (2 * GROUP) + (2 * (s - 1) if s >= 2 else 0))
                                dve.tensor_copy(ctxT[0:C1, r, 1, :], JOB[1][0:C1, 0:NKV]).then_inc(cT1_ready, 1)
                        if j == 3:
                            dve.wait_ge(q_ps, ONE + b + 1)
                            dve.wait_ge(s_ps, ONE + g * NH + (H * (s - 1) if s >= 2 else 0))
                            for m in range(KD):
                                for h in range(P // HD):
                                    last = dve.tensor_scalar(qT[:, r, m * (P // HD) + h, :],
                                                             JOB[1][:, m * T:(m + 1) * T], a.bq[:, 0, m:m + 1],
                                                             e.head_mask[:, h:h + 1], ALU.add, ALU.mult)
                            last.then_inc(q_ready, 1)
                        if j == 5:
                            dve.wait_ge(k_ps, ONE + g * (2 * GROUP) + 2 * s + 2)
                            dve.wait_ge(s_ps, ONE + g * NH + (H * (s - 1) if s >= 2 else 0))
                            dve.tensor_scalar(kT[:, r, 1, :], JOB[1][:, 0:NKV], a.bk[:, 1:2], None,
                                              ALU.add).then_inc(k1_ready, 1)
                        if j == 7:
                            dve.wait_ge(v_ps, ONE + g * (2 * GROUP) + 2 * s + 2)
                            dve.wait_ge(pv_ps, ONE + g * NH + (H * (s - 1) if s >= 2 else 0))
                            dve.tensor_copy(v[:, r, 2, :, 0:HD],
                                            JOB[1][0:KB, 0:D].rearrange("p (h e) -> p h e", e=HD))\
                               .then_inc(v2_ready, 1)

                    def neg_max(i):
                        dve.wait_ge(s_ps, ONE + g * NH + i + 1)
                        dve.wait_ge(exp_done, ONE + g * NH + (i - 3 if i >= 4 else 0))
                        dve.tensor_reduce(mx[:, i % 4:i % 4 + 1], SCORE[i % 3][0:T, 0:NKV], AX_X, ALU.max,
                                          negate=True).then_inc(max_done, 1)

                    def copy_probT(i):
                        dve.wait_ge(pT_ps, ONE + g * NH + i + 1)
                        dve.wait_ge(pv_ps, ONE + g * NH + (i - 3 if i >= 4 else 0))
                        dve.tensor_copy(probT[:, i % 4].rearrange("k c t -> k (c t)"), PT[1][0:KB, 0:NJ * T])\
                           .then_inc(pT_dve, 1)

                    def normalise(s):
                        b = g * GROUP + s
                        pv = PV[0:T, 0:H * (HD + 1)].rearrange("t (h e) -> t h e", e=HD + 1)
                        dve.wait_ge(pv_ps, ONE + g * NH + H * (s + 1))
                        dve.reciprocal(rinv[:, s % 2, :], pv[:, :, HD]).then_inc(rinv_done, 1)
                        dve.wait_ge(rinv_done, ONE + b + 1)
                        if layer == 0:
                            dve.wait_ge(oT_ps, ONE + g * GROUP + max(s - 1, 0))
                        dve.tensor_tensor(o[:, s % 2], pv[:, :, 0:HD], wide(rinv[:, s % 2, :].unsqueeze(2), 2, HD),
                                          ALU.mult).then_inc(o_ready, 1)
                        dve.wait_ge(o_ready, ONE + b + 1)
                        ov = o[:, s % 2].rearrange("t h e -> t (h e)")
                        dve.tensor_tensor(ov, ov, a.bv[0:T, :], ALU.add).then_inc(o_biased, 1)
                        if layer == 1:
                            dve.wait_ge(o_biased, ONE + b + 1)
                            link(dve.tensor_tensor(x[:, b, :], x[:, b, :], ov, ALU.add))
                            e.residual_stats(dve, b, s)

                    def add_y(s):
                        b = g * GROUP + s
                        dve.wait_ge(y_ps, ONE + b + 1)
                        dve.tensor_tensor(y[:, s % 2, :], bank[4][0:T, 0:D], a.bo[:], ALU.add).then_inc(y_read, 1)
                        dve.wait_ge(y_read, ONE + b + 1)
                        link(dve.tensor_tensor(x[:, b, :], x[:, b, :], y[:, s % 2, :], ALU.add))
                        e.residual_stats(dve, b, s)

                    if layer == 1:
                        norm_context(0)
                    for j in range(8):
                        copies(0, j)
                    neg_max(0)
                    for i in range(NH + AHEAD + 1):
                        if i + 1 < NH:
                            neg_max(i + 1)
                        if 0 <= i - AHEAD < NH and (i - AHEAD) % 2 == 1:
                            copy_probT(i - AHEAD)
                        s, h = divmod(i, H)
                        if h == AHEAD and s >= 1:
                            normalise(s - 1)
                        if layer == 0 and h == 5 and s >= 1:
                            add_y(s - 1)
                        if layer == 1 and h == 5 and s < GROUP - 1:
                            norm_context(s + 1)
                        if s < GROUP - 1 and 7 <= h < 15:
                            copies(s + 1, h - 7)
                    if layer == 0:
                        add_y(GROUP - 1)
                    link.close()


def experts(e, layer):
    nc, sem, bank, x, mv, rstd, ident, d = e.nc, e.sem, e.bank, e.x, e.mv, e.rstd, e.ident, e.d
    T, D, B, NG, GT, KD, E = e.T, e.D, e.B, e.NG, e.GT, e.KD, e.E
    n_ = f"f{layer}_"
    w1_d, w2_d = d[f"L{layer}_ffn_w1"], d[f"L{layer}_ffn_w2"]
    FF = w1_d.shape[2]
    NF = FF // P
    BIG = 3.0e38
    with ExitStack() as st:
        def sb(name, shape):
            return st.enter_context(nc.sbuf_tensor(n_ + name, shape, F32))

        def count(name):
            return e.count(n_ + name)

        def flag(name):
            return sem(n_ + name)

        xT = sb("xT", [P, KD, B * T])
        xTg = sb("xTg", [P, KD, GT])
        xn = sb("xn", [T, GROUP, D])
        gw = sb("gate_w", [P, KD, E])
        gb = sb("gate_b", [T, E])
        b1 = sb("b1", [P, E, NF])
        b2 = sb("b2", [E, D])
        logit = sb("logit", [T, B, E])
        iota = sb("iota", [T, E])
        t0, one1, one2 = sb("t0", [T, B, E]), sb("one1", [T, B, E]), sb("one2", [T, B, E])
        top = sb("top", [T, 6, B])
        comb = sb("comb", [T, B, E])
        combG = sb("combG", [T, GROUP, E])
        combT = sb("combT", [E, GROUP, T])
        w1 = sb("w1", [P, 2, KD, FF])
        w2 = sb("w2", [P, 2, NF, D])
        hT = sb("hT", [P, NF, GT])

        gate_loads, std_asked, std_ready, pre = flag("gate_loads"), flag("std_asked"), flag("std_ready"), flag("pre")
        w_loaded = [flag("w_even"), flag("w_odd")]
        xn_ready, xT_ps, xT_ready, xT_kept = count("xn_ready"), count("xT_ps"), count("xT_ready"), count("xT_kept")
        logit_ps, logit_read = count("logit_ps"), count("logit_read")
        iota_made, exp_asked, exp_done = count("iota_made"), count("exp_asked"), count("exp_done")
        top_chain = flag("top_chain")

        e.start_counts()
        with nc.Block() as block:
            @block.sync
            def _(sp):
                gate = d["L0_ffn_gate_w"] if layer == 0 else d["router_T"]
                with nc.allow_non_contiguous_dma(reason="eight columns of the gate"):
                    sp.dma_start(gw[:], gate.rearrange("(k p) n -> p k n", p=P)).then_inc(gate_loads, 16)
                if layer == 0:
                    sp.dma_start(gb[:], d["L0_ffn_gate_b"].partition_broadcast(T)).then_inc(gate_loads, 16)
                    sp.dma_start(b1[:], d["L0_b1_cols"]).then_inc(gate_loads, 16)
                    sp.dma_start(b2[:], d["L0_ffn_b2"]).then_inc(gate_loads, 16)
                for r in range(2):
                    sp.dma_start(w1[:, r], w1_d[r].rearrange("(k p) f -> p k f", p=P)).then_inc(w_loaded[r], 16)
                    sp.dma_start(w2[:, r], w2_d[r].rearrange("(k p) n -> p k n", p=P)).then_inc(w_loaded[r], 16)

            @block.gpsimd
            def _(pool):
                for i in range(E):
                    pool.memset(iota[:, i:i + 1], float(i)).then_inc(iota_made, 1)
                with pool.Fori(0, NG) as g:
                    pool.wait_ge(xT_ready, ONE + g * 2 + 2)
                    pool.tensor_copy(xT[:, :, bass.ds(g * GT, GT)], xTg[:]).then_inc(xT_kept, 1)

            @block.tensor
            def _(pe):
                pe.wait_ge(gate_loads, 16 * (4 if layer == 0 else 1))
                with pe.Fori(0, NG) as g:
                    pe.wait_ge(xn_ready, ONE + g * GROUP + GROUP)
                    for k in range(KD):
                        for s in range(GROUP):
                            last = pe.transpose(bank[k][:, s * T:(s + 1) * T], xn[:, s, k * P:(k + 1) * P],
                                                ident[0:T, 0:T])
                        last.then_inc(xT_ps, 1)
                    pe.wait_ge(xT_ready, ONE + g * 2 + 2)
                    pe.wait_ge(logit_read, ONE + g)
                    for s in range(GROUP):
                        for k in range(KD):
                            last = pe.matmul(bank[2][0:T, s * E:(s + 1) * E], xTg[:, k, s * T:(s + 1) * T],
                                             gw[:, k, :], start=(k == 0), stop=(k == KD - 1))
                    last.then_inc(logit_ps, 1)

            @block.scalar
            def _(act):
                e.make_rstd_act(act, std_ready, std_asked, e.norm_tmp)
                with act.Fori(0, NG) as g:
                    for k in range(KD):
                        act.wait_ge(xT_ps, ONE + g * 2 + k + 1)
                        act.wait_ge(logit_ps, ONE + g)
                        act.wait_ge(xT_kept, ONE + g)
                        act.activation(xTg[:, k, :], bank[k][:, 0:GT], ACT.Copy).then_inc(xT_ready, 1)
                act.wait_ge(exp_asked, ONE + 1)
                act.activation(top[:, 2, :], top[:, 2, :], ACT.Exp).then_inc(exp_done, 1)

            @block.vector
            def _(dve):
                chain = Chain(dve, pre)
                e.make_rstd_dve(dve, chain, std_ready, std_asked, mv, rstd[:], e.norm_tmp, False, e.stat6)
                dve.wait_ge(gate_loads, 16 * (4 if layer == 0 else 1))
                with dve.Fori(0, NG) as g:
                    dve.wait_ge(xT_ps, ONE + g * 2)
                    for s in range(GROUP):
                        b = g * GROUP + s
                        dve.tensor_scalar(xn[:, s, :], x[:, b, :], mv[:, b, 0:1], rstd[:, bass.ds(b, 1)],
                                          ALU.subtract, ALU.mult).then_inc(xn_ready, 1)
                    dve.wait_ge(logit_ps, ONE + g + 1)
                    lg = logit[:, bass.ds(g * GROUP, GROUP), :]
                    ps = bank[2][0:T, 0:GROUP * E].rearrange("t (s n) -> t s n", n=E)
                    if layer == 0:
                        dve.tensor_tensor(lg, ps, wide(gb[:].unsqueeze(1), 1, GROUP), ALU.add).then_inc(logit_read, 1)
                    else:
                        dve.tensor_copy(lg, ps).then_inc(logit_read, 1)
                dve.wait_ge(logit_read, ONE + NG)
                dve.wait_ge(iota_made, ONE + E)
                link = Chain(dve, top_chain)
                iw = wide(iota[:].unsqueeze(1), 1, B)

                def over_experts(row):
                    return wide(top[:, row, :].unsqueeze(2), 2, E)

                def first_of_max(values, value, index, onehot):
                    link(dve.tensor_reduce(top[:, value, :], values, AX_X, ALU.max))
                    link(dve.tensor_tensor(t0[:], values, over_experts(value), ALU.is_equal))
                    link(dve.tensor_scalar(t0[:], t0[:], -float(E), float(E), ALU.mult, ALU.add))
                    link(dve.tensor_tensor(t0[:], t0[:], iw, ALU.add))
                    link(dve.tensor_reduce(top[:, index, :], t0[:], AX_X, ALU.min))
                    link(dve.tensor_tensor(onehot[:], iw, over_experts(index), ALU.is_equal))

                first_of_max(logit[:], 0, 1, one1)
                link(dve.scalar_tensor_tensor(out=logit[:], in0=one1[:], scalar=-BIG, in1=logit[:], op0=ALU.mult,
                                              op1=ALU.add))
                first_of_max(logit[:], 3, 4, one2)
                link(dve.tensor_tensor(top[:, 2, :], top[:, 3, :], top[:, 0, :], ALU.subtract))
                dve.sem_inc(exp_asked, 1)
                dve.wait_ge(exp_done, ONE + 1)
                link(dve.tensor_scalar(top[:, 5, :], top[:, 2, :], 1.0, None, ALU.add))
                link(dve.reciprocal(top[:, 5, :], top[:, 5, :]))
                link(dve.tensor_tensor(one1[:], one1[:], over_experts(5), ALU.mult))
                link(dve.tensor_tensor(top[:, 5, :], top[:, 5, :], top[:, 2, :], ALU.mult))
                link(dve.tensor_tensor(one2[:], one2[:], over_experts(5), ALU.mult))
                link(dve.tensor_tensor(comb[:], one1[:], one2[:], ALU.add))

        down_ps = count("down_ps")
        up_ps, h_raw, h_ready = count("up_ps"), count("h_raw"), count("h_ready")
        acc_done = count("acc_done")
        combG_ready, combT_ps, combT_ready = count("combG_ready"), count("combT_ps"), count("combT_ready")
        b2_ps, b2_added = count("b2_ps"), count("b2_added")
        e.start_counts()
        with nc.Block() as block:
            @block.sync
            def _(sp):
                with sp.Fori(1, E // 2) as i:
                    for r in range(2):
                        sp.wait_ge(down_ps, ONE + (i * 2 + r - 1) * (NG * GROUP))
                        sp.dma_start(w1[:, r], w1_d[bass.ds(i * 2 + r, 1)].rearrange("o (k p) f -> p (o k) f", p=P))\
                          .then_inc(w_loaded[r], 16)
                        sp.dma_start(w2[:, r], w2_d[bass.ds(i * 2 + r, 1)].rearrange("o (k p) n -> p (o k) n", p=P))\
                          .then_inc(w_loaded[r], 16)

            @block.tensor
            def _(pe):
                if layer == 0:
                    with pe.Fori(0, NG) as g:
                        pe.wait_ge(combG_ready, ONE + g + 1)
                        for s in range(GROUP):
                            last = pe.transpose(bank[0][0:E, s * T:(s + 1) * T], combG[:, s, :], ident[0:T, 0:T])
                        last.then_inc(combT_ps, 1)
                        pe.wait_ge(combT_ready, ONE + g + 1)
                        pe.wait_ge(b2_added, ONE + g * GROUP)
                        for s in range(GROUP):
                            pe.matmul(bank[4 + s][0:T, 0:D], combT[:, s, :], b2[:], start=True,
                                      stop=True).then_inc(b2_ps, 1)
                    pe.wait_ge(b2_added, ONE + NG * GROUP)
                with pe.Fori(0, E // 2) as i:
                    for r in range(2):
                        with pe.Fori(0, NG) as g:
                            pe.wait_ge(w_loaded[r], i * 32 + 32)
                            n = (i * 2 + r) * NG + g
                            for f in range(NF):
                                pe.wait_ge(h_raw, ONE + n * NF + (f - 3 if f >= 4 else 0))
                                for k in range(KD):
                                    last = pe.matmul(bank[f % 4][:, 0:GT], w1[:, r, k, f * P:(f + 1) * P],
                                                     xT[:, k, bass.ds(g * GT, GT)], start=(k == 0),
                                                     stop=(k == KD - 1))
                                last.then_inc(up_ps, 1)
                            for s in range(GROUP):
                                if s == 0:
                                    pe.wait_ge(acc_done, ONE + n * GROUP)
                                for f in range(NF):
                                    if s == 0:
                                        pe.wait_ge(h_raw if layer == 0 else h_ready, ONE + n * NF + f + 1)
                                    last = pe.matmul(bank[4 + s][0:T, 0:D], hT[:, f, s * T:(s + 1) * T],
                                                     w2[:, r, f, :], start=(f == 0), stop=(f == NF - 1))
                                last.then_inc(down_ps, 1)

            @block.scalar
            def _(act):
                if layer == 0:
                    with act.Fori(0, NG) as g:
                        act.wait_ge(combT_ps, ONE + g + 1)
                        act.wait_ge(b2_ps, ONE + g * GROUP)
                        act.activation(combT[:].rearrange("n s t -> n (s t)"), bank[0][0:E, 0:GT],
                                       ACT.Copy).then_inc(combT_ready, 1)
                with act.Fori(0, E) as i:
                    with act.Fori(0, NG) as g:
                        n = i * NG + g
                        for f in range(NF):
                            act.wait_ge(up_ps, ONE + n * NF + f + 1)
                            act.wait_ge(down_ps, ONE + n * GROUP)
                            if layer == 0:
                                act.activation(hT[:, f, :], bank[f % 4][:, 0:GT], ACT.Gelu,
                                               bias=b1[:, i, f:f + 1]).then_inc(h_raw, 1)
                            else:
                                act.activation(hT[:, f, :], bank[f % 4][:, 0:GT], ACT.Relu).then_inc(h_raw, 1)

            @block.vector
            def _(dve):
                if layer == 0:
                    with dve.Fori(0, NG) as g:
                        dve.wait_ge(combT_ps, ONE + g)
                        dve.tensor_copy(combG[:], comb[:, bass.ds(g * GROUP, GROUP), :]).then_inc(combG_ready, 1)
                        for s in range(GROUP):
                            b = g * GROUP + s
                            dve.wait_ge(b2_ps, ONE + b + 1)
                            dve.tensor_tensor(x[:, b, :], x[:, b, :], bank[4 + s][0:T, 0:D], ALU.add)\
                               .then_inc(b2_added, 1)
                    dve.wait_ge(b2_added, ONE + NG * GROUP)
                with dve.Fori(0, E) as i:
                    with dve.Fori(0, NG) as g:
                        n = i * NG + g
                        if layer == 1:
                            for f in range(NF):
                                dve.wait_ge(h_raw, ONE + n * NF + f + 1)
                                dve.tensor_tensor(hT[:, f, :], hT[:, f, :], hT[:, f, :], ALU.mult)\
                                   .then_inc(h_ready, 1)
                        dve.wait_ge(acc_done, ONE + n * GROUP)
                        for s in range(GROUP):
                            b = g * GROUP + s
                            dve.wait_ge(down_ps, ONE + n * GROUP + s + 1)
                            dve.scalar_tensor_tensor(out=x[:, b, :], in0=bank[4 + s][0:T, 0:D],
                                                     scalar=comb[:, b, bass.ds(i, 1)], in1=x[:, b, :], op0=ALU.mult,
                                                     op1=ALU.add).then_inc(acc_done, 1)
                dve.wait_ge(acc_done, ONE + E * NG * GROUP)
                if layer == 0:
                    for b in range(B):
                        e.residual_stats(dve, b)


def gated_attention(e):
    nc, sem, bank, x, mv, rstd, ident, w = e.nc, e.sem, e.bank, e.x, e.mv, e.rstd, e.ident, e.w
    T, D, B, NG, GT, KD = e.T, e.D, e.B, e.NG, e.GT, e.KD
    EE = 512
    NE = EE // P
    with ExitStack() as st:
        def sb(name, shape):
            return st.enter_context(nc.sbuf_tensor("ga_" + name, shape, F32))

        def count(name):
            return e.count("ga_" + name)

        def flag(name):
            return sem("ga_" + name)

        rstd1 = sb("rstd1", [T, B])
        xn = sb("xn", [T, GROUP, D])
        xn1 = sb("xn1", [T, GROUP, D])
        xnT = sb("xnT", [P, KD, GT])
        uT = sb("uT", [P, NE, GT])
        zT = sb("zT", [P, GT])
        qT, kT = sb("qT", [P, GT]), sb("kT", [P, GT])
        v = sb("v", [T, GROUP, EE])
        aT = sb("aT", [T, GT])
        hT = sb("hT", [P, NE, GT])

        asked1, std1, asked2, std2, pre = flag("asked1"), flag("std1"), flag("asked2"), flag("std2"), flag("pre")
        xn_ready, xT_ps, xT_ready = count("xn_ready"), count("xT_ps"), count("xT_ready")
        xn1_ready, xn1_based = count("xn1_ready"), count("xn1_based")
        uz_ps, z_ready, u_ready = count("uz_ps"), count("z_ready"), count("u_ready")
        qk_ready = count("qk_ready")
        v_ps, v_biased, v_ready = count("v_ps"), count("v_biased"), count("v_ready")
        a_ps, a_relu, a_ready = count("a_ps"), count("a_relu"), count("a_ready")
        av_ps, h_ready, y_ps = count("av_ps"), count("h_ready"), count("y_ps")
        tail = flag("tail")

        e.start_counts()
        with nc.Block() as block:
            @block.tensor
            def _(pe):
                with pe.Fori(0, NG) as g:
                    pe.wait_ge(xn_ready, ONE + g * GROUP + GROUP)
                    for k in range(KD):
                        for s in range(GROUP):
                            last = pe.transpose(bank[k][:, s * T:(s + 1) * T], xn[:, s, k * P:(k + 1) * P],
                                                ident[0:T, 0:T])
                        last.then_inc(xT_ps, 1)
                    pe.wait_ge(xT_ready, ONE + g * 2 + 2)
                    def up(to, m):
                        for k in range(KD):
                            last = pe.matmul(to[:, 0:GT], w.in_[:, k, m * P:(m + 1) * P], xnT[:, k, :],
                                             start=(k == 0), stop=(k == KD - 1))
                        last.then_inc(uz_ps, 1)
                    up(bank[2], 2 * NE)
                    for s in range(GROUP):
                        if s >= 2:
                            pe.wait_ge(v_biased, ONE + g * GROUP + s - 1)
                        for k in range(KD):
                            last = pe.matmul(bank[4 + s % 2][0:T, :], xnT[:, k, s * T:(s + 1) * T],
                                             w.in_[:, k, EE:2 * EE], start=(k == 0), stop=(k == KD - 1))
                        last.then_inc(v_ps, 1)
                        if s >= 2:
                            pe.wait_ge(u_ready, ONE + g * NE + s - 1)
                        up(bank[6 + s % 2], s)
                    pe.wait_ge(qk_ready, ONE + g * 2 + 2)
                    for s in range(GROUP):
                        at = slice(s * T, (s + 1) * T)
                        last = pe.matmul(bank[3][0:T, at], kT[:, at], qT[:, at], start=True, stop=True)
                    last.then_inc(a_ps, 1)
                    pe.wait_ge(a_ready, ONE + g + 1)
                    pe.wait_ge(v_ready, ONE + g * GROUP + GROUP)
                    pe.wait_ge(v_biased, ONE + g * GROUP + GROUP)
                    pe.wait_ge(u_ready, ONE + g * NE + NE)
                    for m in range(NE):
                        for s in range(GROUP):
                            at = slice(s * T, (s + 1) * T)
                            last = pe.matmul(bank[4 + m][:, at], v[:, s, m * P:(m + 1) * P], aT[:, at],
                                             start=True, stop=True)
                        last.then_inc(av_ps, 1)
                    for s in range(GROUP):
                        if s >= 2:
                            pe.wait_ge(tail, g * (2 * GROUP) + 2 * (s - 2) + 1)
                        for m in range(NE):
                            if s == 0:
                                pe.wait_ge(h_ready, ONE + g * NE + m + 1)
                            last = pe.matmul(bank[s % 2][0:T, 0:D], hT[:, m, s * T:(s + 1) * T], w.out[:, m, :],
                                             start=(m == 0), stop=(m == NE - 1))
                        last.then_inc(y_ps, 1)
                    pe.wait_ge(tail, g * (2 * GROUP) + 2 * (GROUP - 1) + 1)

            @block.scalar
            def _(act):
                e.make_rstd_act(act, std1, asked1, e.norm_tmp)
                e.make_rstd_act(act, std2, asked2, e.norm_tmp)
                with act.Fori(0, NG) as g:
                    for k in range(KD):
                        act.wait_ge(xT_ps, ONE + g * 2 + k + 1)
                        act.wait_ge(uz_ps, ONE + g * (NE + 1))
                        act.activation(xnT[:, k, :], bank[k][:, 0:GT], ACT.Copy).then_inc(xT_ready, 1)
                    act.wait_ge(uz_ps, ONE + g * (NE + 1) + 1)
                    act.wait_ge(qk_ready, ONE + g * 2)
                    act.activation(zT[:], bank[2][:, 0:GT], ACT.Silu, bias=w.b_in_u[:, 8:9]).then_inc(z_ready, 1)
                    for s in range(GROUP):
                        act.wait_ge(v_biased, ONE + g * GROUP + s + 1)
                        act.activation(v[:, s, :], v[:, s, :], ACT.Silu).then_inc(v_ready, 1)
                        act.wait_ge(uz_ps, ONE + g * (NE + 1) + s + 2)
                        act.wait_ge(h_ready, ONE + g * NE)
                        act.activation(uT[:, s, :], bank[6 + s % 2][:, 0:GT], ACT.Silu,
                                       bias=w.b_in_u[:, s:s + 1]).then_inc(u_ready, 1)
                    act.wait_ge(a_ps, ONE + g + 1)
                    act.activation(aT[:], bank[3][0:T, 0:GT], ACT.Relu, scale=1.0 / T).then_inc(a_relu, 1)

            @block.gpsimd
            def _(pool):
                with pool.Fori(0, NG) as g:
                    pool.wait_ge(xn1_ready, ONE + g * GROUP + GROUP)
                    pool.tensor_tensor(xn1[:], xn1[:], wide(w.b_out[:].unsqueeze(1), 1, GROUP), ALU.add)\
                        .then_inc(xn1_based, 1)

            @block.vector
            def _(dve):
                chain = Chain(dve, pre)
                e.make_rstd_dve(dve, chain, std1, asked1, mv, rstd1[:], e.norm_tmp, False, e.stat6)
                e.make_rstd_dve(dve, chain, std2, asked2, mv, rstd[:], e.norm_tmp, True)
                with dve.Fori(0, NG) as g:
                    dve.wait_ge(xT_ps, ONE + g * 2)
                    for s in range(GROUP):
                        b = g * GROUP + s
                        dve.tensor_scalar(xn[:, s, :], x[:, b, :], mv[:, b, 0:1], rstd[:, bass.ds(b, 1)],
                                          ALU.subtract, ALU.mult).then_inc(xn_ready, 1)
                    for s in range(GROUP):
                        b = g * GROUP + s
                        dve.tensor_scalar(xn1[:, s, :], x[:, b, :], mv[:, b, 0:1], rstd1[:, bass.ds(b, 1)],
                                          ALU.subtract, ALU.mult).then_inc(xn1_ready, 1)
                    for s in range(GROUP):
                        dve.wait_ge(v_ps, ONE + g * GROUP + s + 1)
                        dve.wait_ge(av_ps, ONE + g * NE)
                        dve.tensor_tensor(v[:, s, :], bank[4 + s % 2][0:T, :], w.b_in_v[:], ALU.add)\
                           .then_inc(v_biased, 1)
                        if s == 1:
                            dve.wait_ge(z_ready, ONE + g + 1)
                            dve.wait_ge(a_ps, ONE + g)
                            dve.tensor_scalar(qT[:], zT[:], w.gq[:, 0:1], w.gq[:, 1:2], ALU.mult,
                                              ALU.add).then_inc(qk_ready, 1)
                            dve.tensor_scalar(kT[:], zT[:], w.gq[:, 2:3], w.gq[:, 3:4], ALU.mult,
                                              ALU.add).then_inc(qk_ready, 1)
                    dve.wait_ge(a_relu, ONE + g + 1)
                    dve.tensor_tensor(aT[:], aT[:], aT[:], ALU.mult).then_inc(a_ready, 1)
                    for m in range(NE):
                        dve.wait_ge(av_ps, ONE + g * NE + m + 1)
                        dve.wait_ge(u_ready, ONE + g * NE + m + 1)
                        dve.tensor_tensor(hT[:, m, :], bank[4 + m][:, 0:GT], uT[:, m, :], ALU.mult)\
                           .then_inc(h_ready, 1)
                    dve.wait_ge(xn1_based, ONE + g + 1)
                    link = Chain(dve, tail, g * (2 * GROUP), 2 * GROUP)
                    for s in range(GROUP):
                        b = g * GROUP + s
                        dve.wait_ge(y_ps, ONE + b + 1)
                        link(dve.tensor_tensor(xn1[:, s, :], xn1[:, s, :], bank[s % 2][0:T, 0:D], ALU.add))
                        link(dve.tensor_tensor(x[:, b, :], x[:, b, :], xn1[:, s, :], ALU.add))
                        e.residual_stats(dve, b, s)
                    link.close()


def kernel(**inputs):
    import concourse.bacc as bacc
    from concourse.bass_utils import run_bass_kernel_spmd

    a = {k: np.asarray(v) for k, v in inputs.items()}
    a["L0_Wq"], a["L0_Wk"] = a["L0_attn_W_qk"][:, 0::2], a["L0_attn_W_qk"][:, 1::2]
    a["L0_bq"], a["L0_bk"] = a["L0_attn_b_qk"][0::2], a["L0_attn_b_qk"][1::2]
    for n in "qkvo":
        a[f"L0_xW{n}_T"] = a.pop(f"L0_xattn_W{n}").T
    a["router_T"] = a.pop("L1_ffn_router_w").T
    a["ctx_T"] = a["ctx_768"].transpose(2, 0, 1)
    del a["L0_attn_W_qk"], a["L0_attn_b_qk"]
    for name in ("L0_bq", "L0_bk", "L0_attn_b_v", "L1_attn_ln_g", "L1_attn_ln_b", "L0_xattn_bq", "L0_xattn_bk",
                 "L1_xattn_bq", "L1_xattn_bk", "L1_xattn_norm_g", "L1_xattn_norm_b"):
        a[name] = a[name].reshape(-1, P).T
    a["L0_b1_cols"] = a["L0_ffn_b1"].reshape(8, -1, P).transpose(2, 0, 1)
    a["L1_b_in_cols"] = a["L1_attn_b_in"].reshape(-1, P).T
    a = {k: np.ascontiguousarray(v) for k, v in a.items()}

    nc = bacc.Bacc("TRN2", target_bir_lowering=False, num_devices=1)
    d = {k: nc.dram_tensor(f"in_{k}", v.shape, mybir.dt.from_np(v.dtype), kind="ExternalInput").ap()
         for k, v in a.items()}
    out = nc.dram_tensor("out_x", a["x"].shape, F32, kind="ExternalOutput").ap()
    decoder(nc, d, out)
    r = run_bass_kernel_spmd(nc, [{f"in_{k}": v for k, v in a.items()}], core_ids=[0])
    return r.results[0]["out_x"]
```

```python
from contextlib import ExitStack

import numpy as np

import concourse.bass as bass
from concourse import mybir

ALU = mybir.AluOpType
ACT = mybir.ActivationFunctionType
F32 = mybir.dt.float32
AX_X = mybir.AxisListType.X

P = 128
EPS = 1e-5
GROUP = 4
ONE = 1
TWO = 2
LAST_STAGE = 6


def wide(ap, axis, n):
    shape = list(ap.shape)
    shape[axis] = n
    return ap.broadcast_to(shape)


class Parts:
    pass


class Chain:

    def __init__(self, eng, sem, before=0, length=None):
        self.eng, self.sem, self.before, self.length, self.n = eng, sem, before, length, 0

    def __call__(self, ins):
        self.n += 1
        ins.then_inc(self.sem, 1)
        self.eng.wait_ge(self.sem, self.before + self.n)

    def close(self):
        assert self.length == self.n, (self.length, self.n)


def decoder(nc, d, out):
    B, T, D = d["x"].shape
    NG = B // GROUP
    GT = GROUP * T
    KD = D // P
    NKV = d["ctx_768"].shape[1]
    DC = d["ctx_768"].shape[2]
    KB = 125
    NJ = NKV // KB
    C1 = DC - P
    XH, XD = 16, D // 16
    AH, AD = 8, 64
    E = 8
    SLOTS = 2 * P
    NT = (2 * B * T - E) // SLOTS + E

    ctx = ExitStack()
    with ctx:
        def sb(name, shape, dt=F32):
            return ctx.enter_context(nc.sbuf_tensor(name, shape, dt))

        stage_sems = []

        def sem(name):
            stage_sems.append(nc.alloc_semaphore(name=name))
            return stage_sems[-1]

        counts = []

        def count(name, start=ONE):
            counts.append((sem(name), start))
            return counts[-1][0]

        def start_counts():
            for s, start in counts:
                nc.gpsimd.sem_inc(s, start)
            counts.clear()
            nc.all_engine_barrier()

        def end_stage():
            nc.clear_and_free_semaphores(list(stage_sems))
            nc.all_engine_barrier()
            stage_sems.clear()

        bank = [ctx.enter_context(nc.psum_tensor(f"bank{i}", [P, 512], F32)) for i in range(8)]

        x = sb("x_res", [T, B, D])
        mv = sb("x_mean_var", [T, B, 2])
        rstd = sb("x_rstd", [T, B])
        ident = sb("ident", [P, P])
        norm_tmp = sb("norm_tmp", [T, 3, B])
        stat6 = sb("stat6", [T, B, 6])
        scratch = sb("scratch", [P, GROUP])

        w = Parts()
        w.q = sb("w_q", [P, KD, AH * AD])
        w.k = sb("w_k", [P, KD, AH * AD])
        w.v = sb("w_v", [P, KD, AH * AD])
        w.o = sb("w_o", [P, 4, D])
        w.bq = sb("w_bq", [P, 4])
        w.bk = sb("w_bk", [P, 4])
        w.bv = sb("w_bv", [P, 4])
        w.bo = sb("w_bo", [T, D])
        w.ln_g = sb("w_ln_g", [T, D])
        w.ln_b = sb("w_ln_b", [T, D])
        w.in_ = sb("w_in", [P, KD, 1152])
        w.out = sb("w_out", [P, 4, D])
        w.b_in_u = sb("w_b_in_u", [P, 9])
        w.b_in_v = sb("w_b_in_v", [T, 512])
        w.b_out = sb("w_b_out", [T, D])
        w.gq = sb("w_gq", [P, 4])
        w.ln_gb = sb("w_ln_gb", [P, 2 * KD])
        w.ln_b_wide = sb("w_ln_b_wide", [P, KD, T])
        xa = []
        for n in range(2):
            a = Parts()
            a.wq = sb(f"x{n}_wq", [P, KD, D])
            a.wk = sb(f"x{n}_wk", [P, 2, D])
            a.wv = sb(f"x{n}_wv", [P, 2, D])
            a.bq = sb(f"x{n}_bq", [P, 1, KD])
            a.bk = sb(f"x{n}_bk", [P, KD])
            a.bv = sb(f"x{n}_bv", [P, D])
            xa.append(a)
        xa[0].wo = sb("x0_wo", [P, KD, D])
        xa[0].bo = sb("x0_bo", [T, D])
        xa[1].gb = sb("x1_gb", [P, 8])
        xa[1].b_wide = sb("x1_b_wide", [P, 4, P])
        head_mask = sb("head_mask", [P, P // XD])

        FOLD_WIDE = KD + 2
        loads = sem("setup_loads")
        const_ready = sem("const_ready")
        fold_chain = sem("fold_chain")
        fold_ps = sem("fold_ps")

        def cols(ap, k):
            return ap if k > 1 else ap.rearrange("(p k) -> p k", k=1)

        def rows(ap, parts):
            return ap.partition_broadcast(parts)

        setup_loads = [
            (w.q[:], d["L0_Wq"].rearrange("(k p) n -> p k n", p=P)),
            (w.k[:], d["L0_Wk"].rearrange("(k p) n -> p k n", p=P)),
            (w.v[:], d["L0_attn_W_v"].rearrange("(k p) n -> p k n", p=P)),
            (w.o[:], d["L0_attn_W_out"].rearrange("(k p) n -> p k n", p=P)),
            (w.bq[:], cols(d["L0_bq"], 4)),
            (w.bk[:], cols(d["L0_bk"], 4)),
            (w.bv[:], cols(d["L0_attn_b_v"], 4)),
            (w.bo[:], rows(d["L0_attn_b_out"], T)),
            (w.ln_g[:], rows(d["L0_attn_ln_gamma"], T)),
            (w.ln_b[:], rows(d["L0_attn_ln_beta"], T)),
            (w.in_[:], d["L1_attn_W_in"].rearrange("(k p) n -> p k n", p=P)),
            (w.out[:], d["L1_attn_W_out"].rearrange("(k p) n -> p k n", p=P)),
            (w.b_in_u[:], cols(d["L1_b_in_cols"], 9)),
            (w.b_in_v[:], rows(d["L1_attn_b_in"][512:1024], T)),
            (w.b_out[:], rows(d["L1_attn_b_out"], T)),
            (w.gq[:, 0:1], cols(d["L1_attn_gamma_q"], 1)),
            (w.gq[:, 1:2], cols(d["L1_attn_beta_q"], 1)),
            (w.gq[:, 2:3], cols(d["L1_attn_gamma_k"], 1)),
            (w.gq[:, 3:4], cols(d["L1_attn_beta_k"], 1)),
            (w.ln_gb[:, 0:KD], cols(d["L1_attn_ln_g"], KD)),
            (w.ln_gb[:, KD:2 * KD], cols(d["L1_attn_ln_b"], KD)),
            (xa[0].wq[:], d["L0_xWq_T"].rearrange("(k p) n -> p k n", p=P)),
            (xa[0].wk[:, 0, :], d["L0_xWk_T"][0:P, :]),
            (xa[0].wk[0:C1, 1, :], d["L0_xWk_T"][P:DC, :]),
            (xa[0].wv[:, 0, :], d["L0_xWv_T"][0:P, :]),
            (xa[0].wv[0:C1, 1, :], d["L0_xWv_T"][P:DC, :]),
            (xa[0].wo[:], d["L0_xWo_T"].rearrange("(k p) n -> p k n", p=P)),
            (xa[0].bq[:, 0, :], cols(d["L0_xattn_bq"], KD)),
            (xa[0].bk[:], cols(d["L0_xattn_bk"], KD)),
            (xa[0].bv[:], rows(d["L0_xattn_bv"], P)),
            (xa[0].bo[:], rows(d["L0_xattn_bo"], T)),
            (xa[1].wq[:], d["L1_xattn_Wq"].rearrange("(k p) n -> p k n", p=P)),
            (xa[1].wk[:, 0, :], d["L1_xattn_Wk"][0:P, :]),
            (xa[1].wk[0:C1, 1, :], d["L1_xattn_Wk"][P:DC, :]),
            (xa[1].wv[:, 0, :], d["L1_xattn_Wv"][0:P, :]),
            (xa[1].wv[0:C1, 1, :], d["L1_xattn_Wv"][P:DC, :]),
            (xa[1].bq[:, 0, :], cols(d["L1_xattn_bq"], KD)),
            (xa[1].bk[:], cols(d["L1_xattn_bk"], KD)),
            (xa[1].bv[:], rows(d["L1_xattn_bv"], P)),
            (xa[1].gb[:, 0:KD], cols(d["L1_xattn_norm_g"], KD)),
            (xa[1].gb[:, KD:2 * KD], cols(d["L1_xattn_norm_b"], KD)),
            (xa[1].gb[:, 4:5], cols(d["L1_xattn_tnorm_g"][0:P], 1)),
            (xa[1].gb[0:C1, 5:6], d["L1_xattn_tnorm_g"][P:DC].rearrange("(p a) -> p a", a=1)),
            (xa[1].gb[:, 6:7], cols(d["L1_xattn_tnorm_b"][0:P], 1)),
            (xa[1].gb[0:C1, 7:8], d["L1_xattn_tnorm_b"][P:DC].rearrange("(p a) -> p a", a=1)),
            (x[:], d["x"].rearrange("b t d -> t b d")),
        ]

        def residual_stats(dve, b, col=None):
            if col is not None:
                dve.memset(scratch[0:T, col:col + 1], 0.0)
            dve.bn_stats(stat6[:, b, :], x[:, b, :])

        with nc.Block() as block:
            @block.sync
            def _(sp):
                for dst, src in setup_loads:
                    sp.dma_start(dst, src).then_inc(loads, 16)

            @block.gpsimd
            def _(pool):
                made = Chain(pool, const_ready)
                made(pool.memset(ident[:], 0.0))
                made(pool.affine_select(out=ident[:], in_=ident[:], compare_op=ALU.not_equal, fill=1.0,
                                        base=0, pattern=[[-1, P]], channel_multiplier=1))
                made(pool.memset(head_mask[:], XD ** -0.5))
                made(pool.affine_select(out=head_mask[:], in_=head_mask[:], compare_op=ALU.is_ge, fill=0.0,
                                        base=0, pattern=[[-XD, P // XD]], channel_multiplier=1))
                made(pool.affine_select(out=head_mask[:], in_=head_mask[:], compare_op=ALU.is_ge, fill=0.0,
                                        base=XD - 1, pattern=[[XD, P // XD]], channel_multiplier=-1))

            @block.vector
            def _(dve):
                fold = Chain(dve, fold_chain)
                dve.wait_ge(loads, 16 * len(setup_loads))
                dve.wait_ge(const_ready, 5)
                for k in range(KD):
                    fold(dve.tensor_scalar(w.ln_b_wide[:, k, :], ident[:, 0:T], 0.0,
                                           w.ln_gb[:, KD + k:KD + k + 1], ALU.mult, ALU.add))
                for k in range(2):
                    n = P if k == 0 else C1
                    fold(dve.tensor_scalar(xa[1].b_wide[0:n, 2 + k, :], ident[0:n, :], 0.0,
                                           xa[1].gb[0:n, 6 + k:7 + k], ALU.mult, ALU.add))
                assert fold.n == FOLD_WIDE
                dve.wait_ge(fold_ps, 1)
                fold(dve.tensor_tensor(w.bo[:], w.bo[:], bank[0][0:T, 0:D], ALU.add))
                fold(dve.tensor_tensor(w.b_in_v[:], w.b_in_v[:], bank[1][0:T, :], ALU.add))
                fold(dve.tensor_tensor(w.b_in_u[:], w.b_in_u[:], bank[2][:, 0:9], ALU.add))
                fold(dve.tensor_tensor(xa[1].bq[:, 0, :], xa[1].bq[:, 0, :], bank[2][:, 16:16 + KD], ALU.add))
                fold(dve.tensor_tensor(xa[1].bk[:], xa[1].bk[:], bank[2][:, 32:32 + KD], ALU.add))
                fold(dve.tensor_tensor(xa[1].bv[:], xa[1].bv[:], bank[3][:, 0:D], ALU.add))
                for k in range(KD):
                    fold(dve.tensor_scalar(w.in_[:, k, :], w.in_[:, k, :], w.ln_gb[:, k:k + 1], None, ALU.mult))
                    fold(dve.tensor_scalar(xa[1].wq[:, k, :], xa[1].wq[:, k, :], xa[1].gb[:, k:k + 1], None,
                                           ALU.mult))
                    n = P if k == 0 else C1
                    for wt in (xa[1].wk, xa[1].wv):
                        fold(dve.tensor_scalar(wt[0:n, k, :], wt[0:n, k, :], xa[1].gb[0:n, 4 + k:5 + k], None,
                                               ALU.mult))
                for b in range(B):
                    residual_stats(dve, b)

            @block.tensor
            def _(pe):
                pe.wait_ge(loads, 16 * len(setup_loads))
                pe.wait_ge(fold_chain, FOLD_WIDE)
                for k in range(4):
                    pe.matmul(bank[0][0:T, 0:D], wide(w.bv[:, k:k + 1], 1, T), w.o[:, k, :],
                              start=(k == 0), stop=(k == 3))
                for k in range(KD):
                    pe.matmul(bank[1][0:T, :], w.ln_b_wide[:, k, :], w.in_[:, k, 512:1024],
                              start=(k == 0), stop=(k == KD - 1))
                for m in range(9):
                    for k in range(KD):
                        pe.matmul(bank[2][:, m:m + 1], w.in_[:, k, m * P:(m + 1) * P],
                                  w.ln_gb[:, KD + k:KD + k + 1], start=(k == 0), stop=(k == KD - 1))
                for m in range(KD):
                    for k in range(KD):
                        pe.matmul(bank[2][:, 16 + m:17 + m], xa[1].wq[:, k, m * P:(m + 1) * P],
                                  xa[1].gb[:, KD + k:KD + k + 1], start=(k == 0), stop=(k == KD - 1))
                    for k in range(2):
                        n = P if k == 0 else C1
                        pe.matmul(bank[2][:, 32 + m:33 + m], xa[1].wk[0:n, k, m * P:(m + 1) * P],
                                  xa[1].gb[0:n, 6 + k:7 + k], start=(k == 0), stop=(k == 1))
                for k in range(2):
                    n = P if k == 0 else C1
                    last = pe.matmul(bank[3][:, 0:D], xa[1].b_wide[0:n, 2 + k, :], xa[1].wv[0:n, k, :],
                                     start=(k == 0), stop=(k == 1))
                last.then_inc(fold_ps, 1)

        def mean_var(dve, chain, six, stats, tmp, width):
            chain(dve.tensor_tensor(tmp[:, 0, :], six[:, :, 1], six[:, :, 4], ALU.add))
            chain(dve.tensor_tensor(tmp[:, 1, :], six[:, :, 1], six[:, :, 4], ALU.subtract))
            chain(dve.tensor_tensor(tmp[:, 2, :], six[:, :, 2], six[:, :, 5], ALU.add))
            chain(dve.tensor_scalar(stats[:, :, 0], tmp[:, 0, :], 0.5, None, ALU.mult))
            chain(dve.tensor_tensor(tmp[:, 1, :], tmp[:, 1, :], tmp[:, 1, :], ALU.mult))
            chain(dve.tensor_scalar(tmp[:, 1, :], tmp[:, 1, :], 0.25, None, ALU.mult))
            chain(dve.tensor_scalar(tmp[:, 2, :], tmp[:, 2, :], 1.0 / width, None, ALU.mult))
            chain(dve.tensor_tensor(stats[:, :, 1], tmp[:, 1, :], tmp[:, 2, :], ALU.add))

        def make_rstd_dve(dve, chain, std_ready, std_asked, stats, rs, tmp, double, six=None, width=D):
            if six is not None:
                mean_var(dve, chain, six, stats, tmp, width)
            chain(dve.tensor_scalar(tmp[:, 0, :], stats[:, :, 1], 1.0 + EPS if double else 1.0,
                                    EPS * EPS if double else EPS, ALU.mult, ALU.add))
            dve.sem_inc(std_asked, 1)
            dve.wait_ge(std_ready, 1)
            chain(dve.reciprocal(tmp[:, 2, :], tmp[:, 1, :]))
            chain(dve.tensor_tensor(tmp[:, 1, :], tmp[:, 2, :], tmp[:, 2, :], ALU.mult))
            chain(dve.tensor_tensor(tmp[:, 1, :], tmp[:, 1, :], tmp[:, 0, :], ALU.mult))
            chain(dve.tensor_scalar(tmp[:, 1, :], tmp[:, 1, :], -0.5, 1.5, ALU.mult, ALU.add))
            chain(dve.tensor_tensor(rs, tmp[:, 2, :], tmp[:, 1, :], ALU.mult))

        def make_rstd_act(act, std_ready, std_asked, tmp):
            act.wait_ge(std_asked, 1)
            act.activation(tmp[:, 1, :], tmp[:, 0, :], ACT.Sqrt).then_inc(std_ready, 1)

        env = Parts()
        env.nc, env.d, env.B, env.T, env.D, env.NG, env.GT, env.KD = (
            nc, d, B, T, D, NG, GT, KD)
        env.NKV, env.DC, env.KB, env.NJ, env.C1, env.XH, env.XD, env.AH = (
            NKV, DC, KB, NJ, C1, XH, XD, AH)
        env.AD, env.E, env.bank, env.x, env.mv, env.rstd, env.ident, env.norm_tmp = (
            AD, E, bank, x, mv, rstd, ident, norm_tmp)
        env.stat6, env.scratch, env.head_mask, env.w, env.xa, env.sem, env.count, env.start_counts = (
            stat6, scratch, head_mask, w, xa, sem, count, start_counts)
        env.residual_stats, env.make_rstd_dve, env.make_rstd_act = (
            residual_stats, make_rstd_dve, make_rstd_act)
        slot_x = nc.dram_tensor("slot_x", [NT * SLOTS, D], F32, kind="Internal").ap()
        slot_y = nc.dram_tensor("slot_y", [NT * SLOTS, D], F32, kind="Internal").ap()
        env.slot_x, env.slot_y, env.SLOTS, env.NT = slot_x, slot_y, SLOTS, NT
        end_stage()
        stages = [self_attention, lambda e: cross_attention(e, 0), lambda e: experts(e, 0),
                  gated_attention, lambda e: cross_attention(e, 1), lambda e: experts(e, 1)]
        for stage in stages[:LAST_STAGE]:
            stage(env)
            end_stage()

        stored = sem("out_stored")
        with nc.Block() as block:
            @block.sync
            def _(sp):
                sp.dma_start(out.rearrange("b t d -> t b d"), x[:]).then_inc(stored, 16)
                sp.wait_ge(stored, 16)


def self_attention(e):
    nc, sem, bank, x, mv, rstd, ident, w = e.nc, e.sem, e.bank, e.x, e.mv, e.rstd, e.ident, e.w
    T, D, B, NG, GT, KD, H, HD = e.T, e.D, e.B, e.NG, e.GT, e.KD, e.AH, e.AD
    UNITS = GROUP * 2
    HU = H // 2
    with ExitStack() as st:
        def sb(name, shape):
            return st.enter_context(nc.sbuf_tensor(name, shape, F32))

        y_all = sb("sa_y", [T, B, D])
        y_mv = sb("sa_y_mv", [T, B, 2])
        y_rstd = sb("sa_y_rstd", [T, B])
        y_tmp = sb("sa_y_tmp", [T, 3, B])
        y_stat = sb("sa_y_stat", [T, B, 6])
        xn = sb("sa_xn", [T, GROUP, D])
        xnT = sb("sa_xnT", [P, KD, GT])
        qT = sb("sa_qT", [P, 4, GT])
        kT = sb("sa_kT", [P, 4, GT])
        v = sb("sa_v", [T, GROUP, H, HD + 1])
        mx = sb("sa_max", [T, 2, HU])
        prob = sb("sa_prob", [T, 2, HU, T])
        probT = sb("sa_probT", [T, 2, HU, T])
        rinv = sb("sa_rinv", [T, 2, HU])
        o = sb("sa_o", [T, 2, H, HD])
        oT = sb("sa_oT", [P, 2, 4, T])

        count, flag = e.count, sem
        std_asked, std_ready = flag("sa_std_asked"), flag("sa_std_ready")
        pre = flag("sa_pre")
        xn_ready = count("sa_xn_ready")
        xT_ps = count("sa_xT_ps")
        xT_ready = count("sa_xT_ready")
        qk_ps = count("sa_qk_ps")
        q_ready, k_ready = count("sa_q_ready"), count("sa_k_ready")
        v_ps, v_ready = count("sa_v_ps"), count("sa_v_ready")
        s_ps = count("sa_scores_ps")
        mx_done = count("sa_max_done")
        shifted = count("sa_shifted")
        exp_done = count("sa_exp_done")
        pT_ps, pT_ready = count("sa_probT_ps"), count("sa_probT_ready")
        pv_ps = count("sa_pv_ps")
        rinv_done = count("sa_rinv_done")
        o_ready = count("sa_o_ready")
        oT_ps, oT_ready = count("sa_oT_ps"), count("sa_oT_ready")
        y_ps, y_done = count("sa_y_ps"), count("sa_y_done")

        e.start_counts()
        with nc.Block() as block:
            @block.tensor
            def _(pe):
                with pe.Fori(0, NG) as g:
                    pe.wait_ge(xn_ready, ONE + g * GROUP + GROUP)
                    for k in range(KD):
                        for s in range(GROUP):
                            last = pe.transpose(bank[k][:, s * T:(s + 1) * T], xn[:, s, k * P:(k + 1) * P],
                                                ident[0:T, 0:T])
                        last.then_inc(xT_ps, 1)
                    for m in range(4):
                        for side, (wt, ready) in enumerate(((w.q, q_ready), (w.k, k_ready))):
                            if m == 0 and side == 0:
                                pe.wait_ge(xT_ready, ONE + g * 2 + 2)
                            if m > 0:
                                pe.wait_ge(ready, ONE + g * 4 + m)
                            for k in range(KD):
                                last = pe.matmul(bank[2 + side][:, 0:GT], wt[:, k, m * P:(m + 1) * P],
                                                 xnT[:, k, :], start=(k == 0), stop=(k == KD - 1))
                            last.then_inc(qk_ps, 1)
                    for s in range(GROUP):
                        if s >= 2:
                            pe.wait_ge(v_ready, ONE + g * GROUP + s - 1)
                        for k in range(KD):
                            last = pe.matmul(bank[s % 2][0:T, :], xnT[:, k, s * T:(s + 1) * T], w.v[:, k, :],
                                             start=(k == 0), stop=(k == KD - 1))
                        last.then_inc(v_ps, 1)
                    pe.wait_ge(q_ready, ONE + g * 4 + 4)
                    pe.wait_ge(k_ready, ONE + g * 4 + 4)

                    def scores(u):
                        s = u // 2
                        if u >= 2:
                            pe.wait_ge(shifted, ONE + g * UNITS + u - 1)
                        for i in range(HU):
                            h = 2 * i + u % 2
                            p0 = HD * (h % 2)
                            last = pe.matmul(bank[4 + u % 2][0:T, i * T:(i + 1) * T],
                                             qT[p0:p0 + HD, h // 2, s * T:(s + 1) * T],
                                             kT[p0:p0 + HD, h // 2, s * T:(s + 1) * T], start=True, stop=True)
                        last.then_inc(s_ps, 1)

                    def turn_prob(u):
                        pe.wait_ge(exp_done, ONE + g * UNITS + u + 1)
                        if u < 2:
                            pe.wait_ge(v_ready, ONE + g * GROUP + 4)
                        for i in range(HU):
                            last = pe.transpose(bank[u % 2][0:T, i * T:(i + 1) * T], prob[:, u % 2, i, :],
                                                ident[0:T, 0:T])
                        last.then_inc(pT_ps, 1)

                    def values(u):
                        s = u // 2
                        pe.wait_ge(pT_ready, ONE + g * UNITS + u + 1)
                        if u >= 2:
                            pe.wait_ge(o_ready, ONE + g * UNITS + u - 1)
                        for i in range(HU):
                            h = 2 * i + u % 2
                            last = pe.matmul(bank[2 + u % 2][0:T, i * (HD + 1):(i + 1) * (HD + 1)],
                                             probT[:, u % 2, i, :], v[:, s, h, :], start=True, stop=True)
                        last.then_inc(pv_ps, 1)

                    def turn_out(s):
                        pe.wait_ge(o_ready, ONE + g * UNITS + 2 * s + 2)
                        ov = o[:, s % 2].rearrange("t h e -> t (h e)")
                        for k in range(4):
                            last = pe.transpose(bank[6][:, k * T:(k + 1) * T], ov[:, k * P:(k + 1) * P],
                                                ident[0:T, 0:T])
                        last.then_inc(oT_ps, 1)

                    def project(s):
                        pe.wait_ge(oT_ready, ONE + g * GROUP + s + 1)
                        pe.wait_ge(y_done, ONE + g * GROUP + s)
                        for k in range(4):
                            last = pe.matmul(bank[7][0:T, 0:D], oT[:, s % 2, k, :], w.o[:, k, :],
                                             start=(k == 0), stop=(k == 3))
                        last.then_inc(y_ps, 1)

                    scores(0)
                    scores(1)
                    for u in range(UNITS):
                        turn_prob(u)
                        if u + 2 < UNITS:
                            scores(u + 2)
                        values(u)
                        if u % 2 == 1 and u >= 3:
                            turn_out((u - 3) // 2)
                        if u % 2 == 0 and u >= 4:
                            project((u - 4) // 2)
                    project(GROUP - 2)
                    turn_out(GROUP - 1)
                    project(GROUP - 1)

            @block.scalar
            def _(act):
                e.make_rstd_act(act, std_ready, std_asked, e.norm_tmp)
                with act.Fori(0, NG) as g:
                    for k in range(KD):
                        act.wait_ge(xT_ps, ONE + g * 2 + k + 1)
                        act.wait_ge(v_ps, ONE + g * GROUP)
                        act.activation(xnT[:, k, :], bank[k][:, 0:GT], ACT.Copy).then_inc(xT_ready, 1)
                    for m in range(4):
                        act.wait_ge(qk_ps, ONE + g * 8 + 2 * m + 1)
                        act.wait_ge(s_ps, ONE + g * UNITS)
                        act.activation(qT[:, m, :], bank[2][:, 0:GT], ACT.Identity,
                                       bias=w.bq[:, m:m + 1]).then_inc(q_ready, 1)

                    def exp(u):
                        act.wait_ge(shifted, ONE + g * UNITS + u + 1)
                        act.activation(prob[:, u % 2], prob[:, u % 2], ACT.Exp,
                                       scale=HD ** -0.5).then_inc(exp_done, 1)

                    def copy_probT(u):
                        act.wait_ge(pT_ps, ONE + g * UNITS + u + 1)
                        if u >= 2:
                            act.wait_ge(pv_ps, ONE + g * UNITS + u - 1)
                        else:
                            act.wait_ge(pv_ps, ONE + g * UNITS)
                        act.activation(probT[:, u % 2].rearrange("t a b -> t (a b)"), bank[u % 2][0:T, 0:HU * T],
                                       ACT.Copy).then_inc(pT_ready, 1)

                    def copy_oT(s):
                        act.wait_ge(oT_ps, ONE + g * GROUP + s + 1)
                        if s >= 2:
                            act.wait_ge(y_ps, ONE + g * GROUP + s - 1)
                        else:
                            act.wait_ge(y_ps, ONE + g * GROUP)
                        act.activation(oT[:, s % 2].rearrange("p a b -> p (a b)"), bank[6][:, 0:4 * T],
                                       ACT.Copy).then_inc(oT_ready, 1)

                    exp(0)
                    for u in range(UNITS):
                        if u + 1 < UNITS:
                            exp(u + 1)
                        copy_probT(u)
                        if u % 2 == 1 and u >= 3:
                            copy_oT((u - 3) // 2)
                    copy_oT(GROUP - 1)

            @block.vector
            def _(dve):
                chain = Chain(dve, pre)
                e.make_rstd_dve(dve, chain, std_ready, std_asked, mv, rstd[:], e.norm_tmp, False, e.stat6)
                chain(dve.memset(v[:, :, :, HD:HD + 1], 1.0))
                with dve.Fori(0, NG) as g:
                    dve.wait_ge(xT_ps, ONE + g * 2)
                    for s in range(GROUP):
                        b = g * GROUP + s
                        dve.tensor_scalar(xn[:, s, :], x[:, b, :], mv[:, b, 0:1], rstd[:, bass.ds(b, 1)],
                                          ALU.subtract, ALU.mult).then_inc(xn_ready, 1)
                    for m in range(4):
                        dve.wait_ge(qk_ps, ONE + g * 8 + 2 * m + 2)
                        dve.wait_ge(s_ps, ONE + g * UNITS)
                        dve.tensor_scalar(kT[:, m, :], bank[3][:, 0:GT], w.bk[:, m:m + 1], None,
                                          ALU.add).then_inc(k_ready, 1)
                    for s in range(GROUP):
                        dve.wait_ge(v_ps, ONE + g * GROUP + s + 1)
                        dve.wait_ge(pv_ps, ONE + g * UNITS)
                        dve.tensor_copy(v[:, s, :, 0:HD],
                                        bank[s % 2][0:T, :].rearrange("t (h e) -> t h e", e=HD))\
                           .then_inc(v_ready, 1)

                    def shift(u):
                        dve.wait_ge(s_ps, ONE + g * UNITS + u + 1)
                        sc = bank[4 + u % 2][0:T, 0:HU * T].rearrange("t (h k) -> t h k", k=T)
                        dve.tensor_reduce(mx[:, u % 2, :], sc, AX_X, ALU.max).then_inc(mx_done, 1)
                        dve.wait_ge(mx_done, ONE + g * UNITS + u + 1)
                        if u >= 2:
                            dve.wait_ge(pT_ps, ONE + g * UNITS + u - 1)
                        else:
                            dve.wait_ge(pT_ps, ONE + g * UNITS)
                        dve.tensor_tensor(prob[:, u % 2], sc, wide(mx[:, u % 2, :].unsqueeze(2), 2, T),
                                          ALU.subtract).then_inc(shifted, 1)

                    def normalise(u):
                        s = u // 2
                        pv = bank[2 + u % 2][0:T, 0:HU * (HD + 1)].rearrange("t (h e) -> t h e", e=HD + 1)
                        dve.wait_ge(pv_ps, ONE + g * UNITS + u + 1)
                        dve.reciprocal(rinv[:, u % 2, :], pv[:, :, HD]).then_inc(rinv_done, 1)
                        dve.wait_ge(rinv_done, ONE + g * UNITS + u + 1)
                        if s >= 2:
                            dve.wait_ge(oT_ps, ONE + g * GROUP + s - 1)
                        else:
                            dve.wait_ge(oT_ps, ONE + g * GROUP)
                        dve.tensor_tensor(o[:, s % 2, u % 2::2, :], pv[:, :, 0:HD],
                                          wide(rinv[:, u % 2, :].unsqueeze(2), 2, HD), ALU.mult)\
                           .then_inc(o_ready, 1)

                    def keep_y(s):
                        dve.wait_ge(y_ps, ONE + g * GROUP + s + 1)
                        dve.tensor_tensor(y_all[:, g * GROUP + s, :], bank[7][0:T, 0:D], w.bo[:],
                                          ALU.add).then_inc(y_done, 1)

                    shift(0)
                    shift(1)
                    for u in range(UNITS):
                        if u + 2 < UNITS:
                            shift(u + 2)
                        normalise(u)
                        if u % 2 == 0 and u >= 4:
                            keep_y((u - 4) // 2)
                    keep_y(GROUP - 2)
                    keep_y(GROUP - 1)

        y_asked, y_std = flag("sa_y_std_asked"), flag("sa_y_std")
        ychain = flag("sa_y_chain")
        loop_chain = flag("sa_fin_chain")
        with nc.Block() as block:
            @block.scalar
            def _(act):
                e.make_rstd_act(act, y_std, y_asked, y_tmp)

            @block.vector
            def _(dve):
                chain = Chain(dve, ychain)
                for b in range(B):
                    last = dve.bn_stats(y_stat[:, b, :], y_all[:, b, :])
                chain(last)
                e.make_rstd_dve(dve, chain, y_std, y_asked, y_mv, y_rstd[:], y_tmp, False, y_stat)
                with dve.Fori(0, NG) as g:
                    n = 2 * GROUP + 4
                    link = Chain(dve, loop_chain, g * n, n)
                    for s in range(GROUP):
                        b = g * GROUP + s
                        yb = y_all[:, b, :]
                        link(dve.tensor_scalar(yb, yb, y_mv[:, b, 0:1], y_rstd[:, bass.ds(b, 1)],
                                               ALU.subtract, ALU.mult))
                        link(dve.tensor_scalar(xn[:, s, :], x[:, b, :], mv[:, b, 0:1], rstd[:, bass.ds(b, 1)],
                                               ALU.subtract, ALU.mult))
                    yg = y_all[:, bass.ds(g * GROUP, GROUP), :]
                    xg = x[:, bass.ds(g * GROUP, GROUP), :]
                    link(dve.tensor_tensor(yg, yg, wide(w.ln_g[:].unsqueeze(1), 1, GROUP), ALU.mult))
                    link(dve.tensor_tensor(yg, yg, wide(w.ln_b[:].unsqueeze(1), 1, GROUP), ALU.add))
                    link(dve.tensor_tensor(yg, yg, xn[:], ALU.add))
                    link(dve.scalar_tensor_tensor(out=xg, in0=yg, scalar=2.0 ** -0.5, in1=xg, op0=ALU.mult,
                                                  op1=ALU.add))
                    for s in range(GROUP):
                        e.residual_stats(dve, g * GROUP + s, s)
                    link.close()


def cross_attention(e, layer):
    nc, sem, bank, x, mv, rstd, ident, d = e.nc, e.sem, e.bank, e.x, e.mv, e.rstd, e.ident, e.d
    T, D, B, NG, KD, H, HD = e.T, e.D, e.B, e.NG, e.KD, e.XH, e.XD
    KB, NJ, NKV, DC, C1 = e.KB, e.NJ, e.NKV, e.DC, e.C1
    a = e.xa[layer]
    n_ = f"x{layer}_"
    JOB = (bank[0], bank[4])
    SCORE = (bank[5], bank[6], bank[7])
    PT = (bank[2], bank[3])
    PV = bank[1]
    NH = GROUP * H
    AHEAD = 2
    with ExitStack() as st:
        def sb(name, shape):
            return st.enter_context(nc.sbuf_tensor(n_ + name, shape, F32))

        def count(name):
            return e.count(n_ + name)

        def flag(name):
            return sem(n_ + name)

        ctxT = sb("ctxT", [P, 2, 2, NKV])
        xn = sb("xn", [T, 2, D])
        xnT = sb("xnT", [P, 2, KD, T])
        qT = sb("qT", [P, 2, H, T])
        kT = sb("kT", [P, 2, KD, NKV])
        v = sb("v", [KB, 2, NJ, H, HD + 1])
        mx = sb("neg_max", [T, 4])
        prob = sb("prob", [T, 4, NKV])
        probT = sb("probT", [KB, 4, NJ, T])
        rinv = sb("rinv", [T, 2, H])
        o = sb("o", [T, 2, H, HD])
        oT = sb("oT", [P, 2, KD, T])
        y = sb("y", [T, 2, D])
        if layer == 1:
            cnat = sb("cnat", [KB, 2, NJ, DC])
            cmv = sb("cmv", [KB, B * NJ, 2])
            crstd = sb("crstd", [KB, B * NJ])
            ctmp = sb("ctmp", [KB, 3, B * NJ])
            cstat = sb("cstat", [KB, B * NJ, 6])

        std_asked, std_ready, pre = flag("std_asked"), flag("std_ready"), flag("pre")
        ctx_loaded = [flag("ctx_even"), flag("ctx_odd")]
        cn_ready, cT_ps, cT0_ready, cT1_ready = count("cn_ready"), count("cT_ps"), count("cT0_ready"), count("cT1_ready")
        xn_ready, xT_ps, xT_ready = count("xn_ready"), count("xT_ps"), count("xT_ready")
        q_ps, q_ready = count("q_ps"), count("q_ready")
        k_ps, k0_ready, k1_ready = count("k_ps"), count("k0_ready"), count("k1_ready")
        v_ps, v01_ready, v2_ready = count("v_ps"), count("v01_ready"), count("v2_ready")
        s_ps, max_done, exp_done = count("scores_ps"), count("max_done"), count("exp_done")
        pT_ps, pT_act, pT_dve = count("probT_ps"), count("probT_act"), count("probT_dve")
        pv_ps, rinv_done, o_ready, o_biased = count("pv_ps"), count("rinv_done"), count("o_ready"), count("o_biased")
        oT_ps, oT_ready, y_ps, y_read = count("oT_ps"), count("oT_ready"), count("y_ps"), count("y_read")
        tail = flag("tail")

        if layer == 1:
            c_asked, c_std, c_chain, c_dma = flag("c_std_asked"), flag("c_std"), flag("c_chain"), flag("c_dma")
            c_dma2, c_read = flag("c_dma_odd"), count("c_read")
            e.start_counts()
            with nc.Block() as block:
                @block.sync
                def _(sp):
                    with sp.Fori(0, B // 2) as i:
                        for r in range(2):
                            sp.wait_ge(c_read, ONE + i * 2)
                            sp.dma_start(cnat[:, r], d["ctx_768"][bass.ds(i * 2 + r, 1)].rearrange(
                                "b (j p) c -> p (b j) c", p=KB)).then_inc((c_dma, c_dma2)[r], 16)

                @block.scalar
                def _(act):
                    e.make_rstd_act(act, c_std, c_asked, ctmp)

                @block.vector
                def _(dve):
                    with dve.Fori(0, B // 2) as i:
                        for r in range(2):
                            dve.wait_ge(c_read, ONE + i * 2)
                            dve.wait_ge((c_dma, c_dma2)[r], i * 16 + 16)
                            dve.memset(e.scratch[:, r:r + 1], 0.0)
                            for j in range(NJ):
                                last = dve.bn_stats(cstat[:, (i * 2 + r) * NJ + j, :], cnat[:, r, j, :])
                            last.then_inc(c_read, 1)
                    dve.wait_ge(c_read, ONE + B)
                    chain = Chain(dve, c_chain)
                    e.make_rstd_dve(dve, chain, c_std, c_asked, cmv, crstd[:], ctmp, False, cstat, DC)

        e.start_counts()
        with nc.Block() as block:
            @block.sync
            def _(sp):
                with sp.Fori(0, NG) as g:
                    for s in range(GROUP):
                        b = g * GROUP + s
                        r = s % 2
                        if layer == 0:
                            sp.wait_ge(v_ps, ONE + g * (2 * GROUP) + (2 * (s - 1) if s >= 2 else 0))
                            sp.dma_start(ctxT[:, r, 0, :], d["ctx_T"][0:P, bass.ds(b, 1), :].rearrange(
                                "c b k -> c (b k)")).then_inc(ctx_loaded[r], 16)
                            sp.dma_start(ctxT[0:C1, r, 1, :], d["ctx_T"][P:DC, bass.ds(b, 1), :].rearrange(
                                "c b k -> c (b k)")).then_inc(ctx_loaded[r], 16)
                        else:
                            sp.wait_ge(cT_ps, ONE + g * (2 * GROUP) + (2 * (s - 1) if s >= 2 else 0))
                            sp.dma_start(cnat[:, r], d["ctx_768"][bass.ds(b, 1)].rearrange(
                                "b (j p) c -> p (b j) c", p=KB)).then_inc(ctx_loaded[r], 16)

            @block.tensor
            def _(pe):
                with pe.Fori(0, NG) as g:
                    def job(s, j):
                        b = g * GROUP + s
                        r = s % 2
                        to = JOB[j % 2]
                        if j in (0, 1) and layer == 1:
                            if j == 0:
                                pe.wait_ge(cn_ready, ONE + b + 1)
                                pe.wait_ge(v01_ready, ONE + b)
                                pe.wait_ge(v2_ready, ONE + b)
                            n = P if j == 0 else C1
                            for c in range(NJ):
                                last = pe.transpose(to[0:n, c * KB:(c + 1) * KB], cnat[:, r, c, j * P:j * P + n],
                                                    ident[0:KB, 0:KB])
                            last.then_inc(cT_ps, 1)
                        if j == 2:
                            pe.wait_ge(xn_ready, ONE + b + 1)
                            if layer == 1:
                                pe.wait_ge(cT0_ready, ONE + b + 1)
                            else:
                                pe.wait_ge(v01_ready, ONE + b)
                            for k in range(KD):
                                last = pe.transpose(to[:, k * T:(k + 1) * T], xn[:, r, k * P:(k + 1) * P],
                                                    ident[0:T, 0:T])
                            last.then_inc(xT_ps, 1)
                        if j == 3:
                            pe.wait_ge(xT_ready, ONE + b + 1)
                            if layer == 1:
                                pe.wait_ge(cT1_ready, ONE + b + 1)
                            else:
                                pe.wait_ge(v2_ready, ONE + b)
                            for m in range(KD):
                                for k in range(KD):
                                    last = pe.matmul(to[:, m * T:(m + 1) * T], a.wq[:, k, m * P:(m + 1) * P],
                                                     xnT[:, r, k, :], start=(k == 0), stop=(k == KD - 1))
                            last.then_inc(q_ps, 1)
                        if j in (4, 5):
                            m = j - 4
                            if j == 4 and layer == 0:
                                pe.wait_ge(ctx_loaded[r], g * (16 * GROUP) + 32 * (s // 2 + 1))
                            if j == 5:
                                pe.wait_ge(q_ready, ONE + b + 1)
                            for k in range(2):
                                n = P if k == 0 else C1
                                last = pe.matmul(to[:, 0:NKV], a.wk[0:n, k, m * P:(m + 1) * P],
                                                 ctxT[0:n, r, k, :], start=(k == 0), stop=(k == 1))
                            last.then_inc(k_ps, 1)
                        if j in (6, 7):
                            pe.wait_ge(k0_ready if j == 6 else k1_ready, ONE + b + 1)
                            for c in (range(2) if j == 6 else range(2, NJ)):
                                for k in range(2):
                                    n = P if k == 0 else C1
                                    at = c % 2 * D
                                    last = pe.matmul(to[0:KB, at:at + D], ctxT[0:n, r, k, c * KB:(c + 1) * KB],
                                                     a.wv[0:n, k, :], start=(k == 0), stop=(k == 1))
                            last.then_inc(v_ps, 1)

                    def scores(i):
                        s, h = divmod(i, H)
                        r = s % 2
                        b = g * GROUP + s
                        if h == 0:
                            pe.wait_ge(q_ready, ONE + b + 1)
                            pe.wait_ge(k0_ready, ONE + b + 1)
                            pe.wait_ge(k1_ready, ONE + b + 1)
                        pe.wait_ge(exp_done, ONE + g * NH + (i - 2 if i >= 3 else 0))
                        pe.matmul(SCORE[i % 3][0:T, 0:NKV], qT[:, r, h, :], kT[:, r, h // (P // HD), :],
                                  start=True, stop=True).then_inc(s_ps, 1)

                    def turn_prob(i):
                        pe.wait_ge(exp_done, ONE + g * NH + i + 1)
                        half = g * (NH // 2) + (i // 2 if i >= 2 else 0)
                        pe.wait_ge(pT_dve if i % 2 else pT_act, ONE + half)
                        for c in range(NJ):
                            last = pe.transpose(PT[i % 2][0:KB, c * T:(c + 1) * T],
                                                prob[:, i % 4, c * KB:(c + 1) * KB], ident[0:T, 0:T])
                        last.then_inc(pT_ps, 1)

                    def values(i):
                        s, h = divmod(i, H)
                        if h == 0:
                            pe.wait_ge(v01_ready, ONE + g * GROUP + s + 1)
                            pe.wait_ge(v2_ready, ONE + g * GROUP + s + 1)
                            pe.wait_ge(o_ready, ONE + g * GROUP + s)
                        pe.wait_ge(pT_dve if i % 2 else pT_act, ONE + g * (NH // 2) + i // 2 + 1)
                        for c in range(NJ):
                            last = pe.matmul(PV[0:T, h * (HD + 1):(h + 1) * (HD + 1)], probT[:, i % 4, c, :],
                                             v[:, s % 2, c, h, :], start=(c == 0), stop=(c == NJ - 1))
                        last.then_inc(pv_ps, 1)

                    def turn_out(s):
                        pe.wait_ge(o_biased, ONE + g * GROUP + s + 1)
                        ov = o[:, s % 2].rearrange("t h e -> t (h e)")
                        for k in range(KD):
                            last = pe.transpose(bank[0][:, k * T:(k + 1) * T], ov[:, k * P:(k + 1) * P],
                                                ident[0:T, 0:T])
                        last.then_inc(oT_ps, 1)

                    def project(s):
                        pe.wait_ge(oT_ready, ONE + g * GROUP + s + 1)
                        for k in range(KD):
                            last = pe.matmul(bank[4][0:T, 0:D], oT[:, s % 2, k, :], a.wo[:, k, :],
                                             start=(k == 0), stop=(k == KD - 1))
                        last.then_inc(y_ps, 1)

                    first = 0 if layer == 1 else 2
                    for j in range(first, 8):
                        job(0, j)
                    for i in range(NH + AHEAD + 1):
                        if i < NH:
                            scores(i)
                        if 0 <= i - AHEAD < NH:
                            turn_prob(i - AHEAD)
                        if i - AHEAD - 1 >= 0:
                            values(i - AHEAD - 1)
                        s, h = divmod(i, H)
                        if layer == 0 and h == 4 and s >= 1:
                            pe.wait_ge(v01_ready, ONE + g * GROUP + s + 1)
                            turn_out(s - 1)
                        if layer == 0 and h == 5 and s >= 1:
                            pe.wait_ge(v2_ready, ONE + g * GROUP + s + 1)
                            project(s - 1)
                        if s < GROUP - 1 and 7 <= h < 15 and h - 7 >= first:
                            if layer == 0 and s >= 1 and h - 7 == first:
                                pe.wait_ge(oT_ready, ONE + g * GROUP + s)
                                pe.wait_ge(y_read, ONE + g * GROUP + s)
                            job(s + 1, h - 7)
                    if layer == 0:
                        turn_out(GROUP - 1)
                        pe.wait_ge(y_read, ONE + g * GROUP + GROUP - 1)
                        project(GROUP - 1)
                        pe.wait_ge(y_read, ONE + g * GROUP + GROUP)

            @block.scalar
            def _(act):
                e.make_rstd_act(act, std_ready, std_asked, e.norm_tmp)
                with act.Fori(0, NG) as g:
                    def copies(s, j):
                        b = g * GROUP + s
                        r = s % 2
                        if j == 0 and layer == 1:
                            act.wait_ge(cT_ps, ONE + g * (2 * GROUP) + 2 * s + 1)
                            act.wait_ge(v_ps, ONE + g * (2 * GROUP) + (2 * (s - 1) if s >= 2 else 0))
                            act.activation(ctxT[:, r, 0, :], JOB[0][:, 0:NKV], ACT.Copy).then_inc(cT0_ready, 1)
                        if j == 2:
                            act.wait_ge(xT_ps, ONE + b + 1)
                            act.activation(xnT[:, r].rearrange("p k t -> p (k t)"), JOB[0][:, 0:KD * T],
                                           ACT.Copy).then_inc(xT_ready, 1)
                        if j == 4:
                            act.wait_ge(k_ps, ONE + g * (2 * GROUP) + 2 * s + 1)
                            act.wait_ge(s_ps, ONE + g * NH + (H * (s - 1) if s >= 2 else 0))
                            act.activation(kT[:, r, 0, :], JOB[0][:, 0:NKV], ACT.Identity,
                                           bias=a.bk[:, 0:1]).then_inc(k0_ready, 1)
                        if j == 6:
                            act.wait_ge(v_ps, ONE + g * (2 * GROUP) + 2 * s + 1)
                            act.wait_ge(pv_ps, ONE + g * NH + (H * (s - 1) if s >= 2 else 0))
                            act.activation(v[:, r, 0:2, :, 0:HD],
                                           JOB[0][0:KB, :].rearrange("p (c h e) -> p c h e", c=2, e=HD),
                                           ACT.Copy).then_inc(v01_ready, 1)

                    def exp(i):
                        act.wait_ge(max_done, ONE + g * NH + i + 1)
                        act.wait_ge(pT_ps, ONE + g * NH + (i - 3 if i >= 4 else 0))
                        act.activation(prob[:, i % 4, :], SCORE[i % 3][0:T, 0:NKV], ACT.Exp,
                                       bias=mx[:, i % 4:i % 4 + 1]).then_inc(exp_done, 1)

                    def copy_probT(i):
                        act.wait_ge(pT_ps, ONE + g * NH + i + 1)
                        act.wait_ge(pv_ps, ONE + g * NH + (i - 3 if i >= 4 else 0))
                        act.activation(probT[:, i % 4].rearrange("k c t -> k (c t)"), PT[0][0:KB, 0:NJ * T],
                                       ACT.Copy).then_inc(pT_act, 1)

                    def copy_oT(s):
                        act.wait_ge(oT_ps, ONE + g * GROUP + s + 1)
                        act.wait_ge(y_ps, ONE + g * GROUP + max(s - 1, 0))
                        act.activation(oT[:, s % 2].rearrange("p k t -> p (k t)"), bank[0][:, 0:KD * T],
                                       ACT.Copy).then_inc(oT_ready, 1)

                    for j in range(8):
                        copies(0, j)
                    for i in range(NH + AHEAD + 1):
                        if i < NH:
                            exp(i)
                        if 0 <= i - AHEAD < NH and (i - AHEAD) % 2 == 0:
                            copy_probT(i - AHEAD)
                        s, h = divmod(i, H)
                        if layer == 0 and h == 4 and s >= 1:
                            copy_oT(s - 1)
                        if s < GROUP - 1 and 7 <= h < 15:
                            copies(s + 1, h - 7)
                    if layer == 0:
                        copy_oT(GROUP - 1)

            @block.vector
            def _(dve):
                chain = Chain(dve, pre)
                e.make_rstd_dve(dve, chain, std_ready, std_asked, mv, rstd[:], e.norm_tmp, layer == 1, e.stat6)
                chain(dve.memset(v[:, :, :, :, HD:HD + 1], 1.0))
                n_tail = 1
                with dve.Fori(0, NG) as g:
                    link = Chain(dve, tail, g * GROUP * n_tail, GROUP * n_tail)

                    def norm_context(s):
                        b = g * GROUP + s
                        r = s % 2
                        dve.wait_ge(ctx_loaded[r], g * (8 * GROUP) + 16 * (s // 2 + 1))
                        for c in range(NJ):
                            row = b * NJ + c
                            last = dve.tensor_scalar(cnat[:, r, c, :], cnat[:, r, c, :], cmv[:, row, 0:1],
                                                     crstd[:, bass.ds(row, 1)], ALU.subtract, ALU.mult)
                        last.then_inc(cn_ready, 1)

                    def copies(s, j):
                        b = g * GROUP + s
                        r = s % 2
                        if j == 1:
                            dve.wait_ge(xT_ps, ONE + g * GROUP + max(s - 1, 0))
                            dve.tensor_scalar(xn[:, r, :], x[:, b, :], mv[:, b, 0:1], rstd[:, bass.ds(b, 1)],
                                              ALU.subtract, ALU.mult).then_inc(xn_ready, 1)
                            if layer == 1:
                                dve.wait_ge(cT_ps, ONE + g * (2 * GROUP) + 2 * s + 2)
                                dve.wait_ge(v_ps, ONE + g * (2 * GROUP) + (2 * (s - 1) if s >= 2 else 0))
                                dve.tensor_copy(ctxT[0:C1, r, 1, :], JOB[1][0:C1, 0:NKV]).then_inc(cT1_ready, 1)
                        if j == 3:
                            dve.wait_ge(q_ps, ONE + b + 1)
                            dve.wait_ge(s_ps, ONE + g * NH + (H * (s - 1) if s >= 2 else 0))
                            for m in range(KD):
                                for h in range(P // HD):
                                    last = dve.tensor_scalar(qT[:, r, m * (P // HD) + h, :],
                                                             JOB[1][:, m * T:(m + 1) * T], a.bq[:, 0, m:m + 1],
                                                             e.head_mask[:, h:h + 1], ALU.add, ALU.mult)
                            last.then_inc(q_ready, 1)
                        if j == 5:
                            dve.wait_ge(k_ps, ONE + g * (2 * GROUP) + 2 * s + 2)
                            dve.wait_ge(s_ps, ONE + g * NH + (H * (s - 1) if s >= 2 else 0))
                            dve.tensor_scalar(kT[:, r, 1, :], JOB[1][:, 0:NKV], a.bk[:, 1:2], None,
                                              ALU.add).then_inc(k1_ready, 1)
                        if j == 7:
                            dve.wait_ge(v_ps, ONE + g * (2 * GROUP) + 2 * s + 2)
                            dve.wait_ge(pv_ps, ONE + g * NH + (H * (s - 1) if s >= 2 else 0))
                            dve.tensor_copy(v[:, r, 2, :, 0:HD],
                                            JOB[1][0:KB, 0:D].rearrange("p (h e) -> p h e", e=HD))\
                               .then_inc(v2_ready, 1)

                    def neg_max(i):
                        dve.wait_ge(s_ps, ONE + g * NH + i + 1)
                        dve.wait_ge(exp_done, ONE + g * NH + (i - 3 if i >= 4 else 0))
                        dve.tensor_reduce(mx[:, i % 4:i % 4 + 1], SCORE[i % 3][0:T, 0:NKV], AX_X, ALU.max,
                                          negate=True).then_inc(max_done, 1)

                    def copy_probT(i):
                        dve.wait_ge(pT_ps, ONE + g * NH + i + 1)
                        dve.wait_ge(pv_ps, ONE + g * NH + (i - 3 if i >= 4 else 0))
                        dve.tensor_copy(probT[:, i % 4].rearrange("k c t -> k (c t)"), PT[1][0:KB, 0:NJ * T])\
                           .then_inc(pT_dve, 1)

                    def normalise(s):
                        b = g * GROUP + s
                        pv = PV[0:T, 0:H * (HD + 1)].rearrange("t (h e) -> t h e", e=HD + 1)
                        dve.wait_ge(pv_ps, ONE + g * NH + H * (s + 1))
                        dve.reciprocal(rinv[:, s % 2, :], pv[:, :, HD]).then_inc(rinv_done, 1)
                        dve.wait_ge(rinv_done, ONE + b + 1)
                        if layer == 0:
                            dve.wait_ge(oT_ps, ONE + g * GROUP + max(s - 1, 0))
                        dve.tensor_tensor(o[:, s % 2], pv[:, :, 0:HD], wide(rinv[:, s % 2, :].unsqueeze(2), 2, HD),
                                          ALU.mult).then_inc(o_ready, 1)
                        dve.wait_ge(o_ready, ONE + b + 1)
                        ov = o[:, s % 2].rearrange("t h e -> t (h e)")
                        dve.tensor_tensor(ov, ov, a.bv[0:T, :], ALU.add).then_inc(o_biased, 1)
                        if layer == 1:
                            dve.wait_ge(o_biased, ONE + b + 1)
                            link(dve.tensor_tensor(x[:, b, :], x[:, b, :], ov, ALU.add))
                            e.residual_stats(dve, b, s)

                    def add_y(s):
                        b = g * GROUP + s
                        dve.wait_ge(y_ps, ONE + b + 1)
                        dve.tensor_tensor(y[:, s % 2, :], bank[4][0:T, 0:D], a.bo[:], ALU.add).then_inc(y_read, 1)
                        dve.wait_ge(y_read, ONE + b + 1)
                        link(dve.tensor_tensor(x[:, b, :], x[:, b, :], y[:, s % 2, :], ALU.add))
                        e.residual_stats(dve, b, s)

                    if layer == 1:
                        norm_context(0)
                    for j in range(8):
                        copies(0, j)
                    neg_max(0)
                    for i in range(NH + AHEAD + 1):
                        if i + 1 < NH:
                            neg_max(i + 1)
                        if 0 <= i - AHEAD < NH and (i - AHEAD) % 2 == 1:
                            copy_probT(i - AHEAD)
                        s, h = divmod(i, H)
                        if h == AHEAD and s >= 1:
                            normalise(s - 1)
                        if layer == 0 and h == 5 and s >= 1:
                            add_y(s - 1)
                        if layer == 1 and h == 5 and s < GROUP - 1:
                            norm_context(s + 1)
                        if s < GROUP - 1 and 7 <= h < 15:
                            copies(s + 1, h - 7)
                    if layer == 0:
                        add_y(GROUP - 1)
                    link.close()


def experts(e, layer):
    nc, sem, bank, x, mv, rstd, ident, d = e.nc, e.sem, e.bank, e.x, e.mv, e.rstd, e.ident, e.d
    T, D, B, NG, GT, KD, E = e.T, e.D, e.B, e.NG, e.GT, e.KD, e.E
    n_ = f"f{layer}_"
    w1_d, w2_d = d[f"L{layer}_ffn_w1"], d[f"L{layer}_ffn_w2"]
    FF = w1_d.shape[2]
    NF = FF // P
    BIG = 3.0e38
    SLOTS = e.SLOTS
    NS = SLOTS // P
    NT = e.NT
    STEPS = -(-B * T // SLOTS)
    NI = max(NT, STEPS, E)
    with ExitStack() as st:
        def sb(name, shape, dt=F32):
            return st.enter_context(nc.sbuf_tensor(n_ + name, shape, dt))

        def count(name, start=ONE):
            return e.count(n_ + name, start)

        def flag(name):
            return sem(n_ + name)

        xn = sb("xn", [T, B, D])
        where = sb("where", [T, 2, B], mybir.dt.uint32)
        share = sb("share", [T, 2, B])
        owner = sb("owner", [1, NT], mybir.dt.int32)

        gate_loads, std_asked, std_ready, pre = flag("gate_loads"), flag("std_asked"), flag("std_ready"), flag("pre")
        xn_ready, xT_ps, xT_ready = count("xn_ready"), count("xT_ps"), count("xT_ready")
        logit_ps, logit_read = count("logit_ps"), count("logit_read")
        kept = count("kept")
        const_made, exp_asked, exp_done = flag("const_made"), flag("exp_asked"), flag("exp_done")
        top_chain, chosen, rank_ps = flag("top_chain"), flag("chosen"), flag("rank_ps")
        cleared = flag("cleared")

        with ExitStack() as inner:
            def tmp(name, shape, dt=F32):
                return inner.enter_context(nc.sbuf_tensor(n_ + name, shape, dt))

            xTg = tmp("xTg", [P, KD, GT])
            xnG = tmp("xnG", [T, GROUP, D])
            gw = tmp("gate_w", [P, KD, E])
            gb = tmp("gate_b", [T, E])
            logit = tmp("logit", [T, B, E])
            iota_i = tmp("iota_i", [T, NI], mybir.dt.int32)
            iota = tmp("iota", [T, NI])
            before = tmp("before", [T, T])
            ones = tmp("ones", [T, T])
            t0, one1, one2 = tmp("t0", [T, B, E]), tmp("one1", [T, B, E]), tmp("one2", [T, B, E])
            both = tmp("both", [T, B, E])
            num = tmp("num", [T, B, E])
            run = tmp("run", [T, 2, B, E])
            top = tmp("top", [T, 6, B])
            steps = tmp("steps", [T, E, STEPS])
            tiles = tmp("tiles", [T, E])
            tend = tmp("tend", [T, 2, E])
            own = tmp("own", [1, NT, E])
            own1 = tmp("own1", [1, NT])
            zero = tmp("zero", [P, 7 * D]) if layer == 0 else None
            with_bias = layer == 0
            gate_dmas = 2 if with_bias else 1

            e.start_counts()
            with nc.Block() as block:
                @block.sync
                def _(sp):
                    gate = d["L0_ffn_gate_w"] if layer == 0 else d["router_T"]
                    with nc.allow_non_contiguous_dma(reason="eight columns of the gate"):
                        sp.dma_start(gw[:], gate.rearrange("(k p) n -> p k n", p=P)).then_inc(gate_loads, 16)
                    if with_bias:
                        sp.dma_start(gb[:], d["L0_ffn_gate_b"].partition_broadcast(T)).then_inc(gate_loads, 16)
                    if layer == 0:
                        sp.wait_ge(const_made, 5)
                        rows_ = e.slot_x.rearrange("(p r) c -> p (r c)", p=P)
                        width = NT * NS * D
                        n = 0
                        for at in range(0, width, 7 * D):
                            w_ = min(7 * D, width - at)
                            sp.dma_start(rows_[:, at:at + w_], zero[:, 0:w_]).then_inc(cleared, 16)
                            n += 1
                        sp.wait_ge(cleared, 16 * n)

                @block.gpsimd
                def _(pool):
                    made = Chain(pool, const_made)
                    made(pool.iota(iota_i[:], pattern=[[1, NI]], base=0, channel_multiplier=0))
                    made(pool.memset(ones[:], 1.0))
                    made(pool.memset(before[:], 1.0))
                    made(pool.affine_select(out=before[:], in_=before[:], compare_op=ALU.is_gt, fill=0.0,
                                            base=0, pattern=[[1, T]], channel_multiplier=-1))
                    if layer == 0:
                        made(pool.memset(zero[:], 0.0))

                @block.tensor
                def _(pe):
                    pe.wait_ge(gate_loads, 16 * gate_dmas)
                    with pe.Fori(0, NG) as g:
                        pe.wait_ge(xn_ready, ONE + g * GROUP + GROUP)
                        pe.wait_ge(logit_read, ONE + g)
                        for k in range(KD):
                            for s in range(GROUP):
                                last = pe.transpose(bank[k][:, s * T:(s + 1) * T], xnG[:, s, k * P:(k + 1) * P],
                                                    ident[0:T, 0:T])
                            last.then_inc(xT_ps, 1)
                        pe.wait_ge(xT_ready, ONE + g * 2 + 2)
                        for s in range(GROUP):
                            for k in range(KD):
                                last = pe.matmul(bank[2][0:T, s * E:(s + 1) * E], xTg[:, k, s * T:(s + 1) * T],
                                                 gw[:, k, :], start=(k == 0), stop=(k == KD - 1))
                        last.then_inc(logit_ps, 1)
                    pe.wait_ge(chosen, 1)
                    pe.wait_ge(const_made, 4)
                    marks = both[:].rearrange("t b n -> t (b n)")
                    pe.matmul(bank[3][0:T, 0:B * E], before[:], marks, start=True, stop=True)
                    pe.matmul(bank[4][0:T, 0:B * E], ones[:], marks, start=True, stop=True).then_inc(rank_ps, 1)

                @block.scalar
                def _(act):
                    e.make_rstd_act(act, std_ready, std_asked, e.norm_tmp)
                    with act.Fori(0, NG) as g:
                        for k in range(KD):
                            act.wait_ge(xT_ps, ONE + g * 2 + k + 1)
                            act.wait_ge(logit_ps, ONE + g)
                            act.activation(xTg[:, k, :], bank[k][:, 0:GT], ACT.Copy).then_inc(xT_ready, 1)
                    act.wait_ge(exp_asked, 1)
                    act.activation(top[:, 2, :], top[:, 2, :], ACT.Exp).then_inc(exp_done, 1)

                @block.vector
                def _(dve):
                    chain = Chain(dve, pre)
                    e.make_rstd_dve(dve, chain, std_ready, std_asked, mv, rstd[:], e.norm_tmp, False, e.stat6)
                    dve.wait_ge(gate_loads, 16 * gate_dmas)
                    with dve.Fori(0, NG) as g:
                        dve.wait_ge(xT_ps, ONE + g * 2)
                        dve.wait_ge(kept, ONE + g)
                        for s in range(GROUP):
                            b = g * GROUP + s
                            dve.tensor_scalar(xnG[:, s, :], x[:, b, :], mv[:, b, 0:1], rstd[:, bass.ds(b, 1)],
                                              ALU.subtract, ALU.mult).then_inc(xn_ready, 1)
                        dve.wait_ge(xn_ready, ONE + g * GROUP + GROUP)
                        dve.tensor_scalar(xn[:, bass.ds(g * GROUP, GROUP), :], xnG[:], 1.0, None,
                                          ALU.mult).then_inc(kept, 1)
                        dve.wait_ge(logit_ps, ONE + g + 1)
                        lg = logit[:, bass.ds(g * GROUP, GROUP), :]
                        ps = bank[2][0:T, 0:GROUP * E].rearrange("t (s n) -> t s n", n=E)
                        if with_bias:
                            dve.tensor_tensor(lg, ps, wide(gb[:].unsqueeze(1), 1, GROUP), ALU.add)\
                               .then_inc(logit_read, 1)
                        else:
                            dve.tensor_copy(lg, ps).then_inc(logit_read, 1)
                    dve.wait_ge(logit_read, ONE + NG)
                    dve.wait_ge(const_made, 4)
                    link = Chain(dve, top_chain)
                    link(dve.tensor_copy(iota[:], iota_i[:]))
                    iw = wide(iota[:, 0:E].unsqueeze(1), 1, B)

                    def over_experts(row):
                        return wide(top[:, row, :].unsqueeze(2), 2, E)

                    def first_of_max(values, value, index, onehot):
                        link(dve.tensor_reduce(top[:, value, :], values, AX_X, ALU.max))
                        link(dve.tensor_tensor(t0[:], values, over_experts(value), ALU.is_equal))
                        link(dve.tensor_scalar(t0[:], t0[:], -float(E), float(E), ALU.mult, ALU.add))
                        link(dve.tensor_tensor(t0[:], t0[:], iw, ALU.add))
                        link(dve.tensor_reduce(top[:, index, :], t0[:], AX_X, ALU.min))
                        link(dve.tensor_tensor(onehot[:], iw, over_experts(index), ALU.is_equal))

                    first_of_max(logit[:], 0, 1, one1)
                    link(dve.scalar_tensor_tensor(out=logit[:], in0=one1[:], scalar=-BIG, in1=logit[:],
                                                  op0=ALU.mult, op1=ALU.add))
                    first_of_max(logit[:], 3, 4, one2)
                    link(dve.tensor_tensor(both[:], one1[:], one2[:], ALU.add))
                    dve.sem_inc(chosen, 1)
                    link(dve.tensor_tensor(top[:, 2, :], top[:, 3, :], top[:, 0, :], ALU.subtract))
                    dve.sem_inc(exp_asked, 1)
                    dve.wait_ge(exp_done, 1)
                    link(dve.tensor_scalar(top[:, 5, :], top[:, 2, :], 1.0, None, ALU.add))
                    link(dve.reciprocal(share[:, 0, :], top[:, 5, :]))
                    link(dve.tensor_tensor(share[:, 1, :], share[:, 0, :], top[:, 2, :], ALU.mult))

                    dve.wait_ge(rank_ps, 1)
                    link(dve.tensor_copy(num[:].rearrange("t b n -> t (b n)"), bank[4][0:T, 0:B * E]))
                    link(dve.tensor_copy(run[:, 0], num[:]))
                    at, step = 0, 1
                    while step < B:
                        link(dve.tensor_tensor(run[:, 1 - at, step:B], run[:, at, step:B], run[:, at, 0:B - step],
                                               ALU.add))
                        link(dve.tensor_copy(run[:, 1 - at, 0:step], run[:, at, 0:step]))
                        at, step = 1 - at, 2 * step
                    link(dve.tensor_scalar(steps[:], wide(iota[:, 0:STEPS].unsqueeze(1), 1, E), float(SLOTS), None,
                                           ALU.mult))
                    link(dve.tensor_tensor(steps[:], wide(run[:, at, B - 1, :].unsqueeze(2), 2, STEPS), steps[:],
                                           ALU.is_gt))
                    link(dve.tensor_reduce(tiles[:], steps[:], AX_X, ALU.add))
                    link(dve.tensor_copy(tend[:, 0], tiles[:]))
                    to, step = 0, 1
                    while step < E:
                        link(dve.tensor_tensor(tend[:, 1 - to, step:E], tend[:, to, step:E],
                                               tend[:, to, 0:E - step], ALU.add))
                        link(dve.tensor_copy(tend[:, 1 - to, 0:step], tend[:, to, 0:step]))
                        to, step = 1 - to, 2 * step
                    link(dve.tensor_tensor(own[:], wide(iota[0:1, 0:NT].unsqueeze(2), 2, E),
                                           wide(tend[0:1, to, :].unsqueeze(1), 1, NT), ALU.is_ge))
                    link(dve.tensor_reduce(own1[:], own[:], AX_X, ALU.add))
                    link(dve.tensor_scalar(own1[:], own1[:], float(E - 1), None, ALU.min))
                    link(dve.tensor_copy(owner[:], own1[:]))
                    link(dve.tensor_tensor(tiles[:], tend[:, to], tiles[:], ALU.subtract))
                    link(dve.tensor_scalar(tiles[:], tiles[:], float(SLOTS), None, ALU.mult))
                    link(dve.tensor_tensor(num[:], run[:, at], num[:], ALU.subtract))
                    link(dve.tensor_tensor(num[:], num[:], wide(tiles[:].unsqueeze(1), 1, B), ALU.add))
                    nf = num[:].rearrange("t b n -> t (b n)")
                    link(dve.tensor_tensor(nf, nf, bank[3][0:T, 0:B * E], ALU.add))
                    for c, onehot in enumerate((one1, one2)):
                        link(dve.tensor_tensor(t0[:], num[:], onehot[:], ALU.mult))
                        link(dve.tensor_reduce(top[:, c, :], t0[:], AX_X, ALU.add))
                        link(dve.tensor_copy(where[:, c, :], top[:, c, :]))

        x_slots = sb("x_slots", [P, 2, NS, D])
        xT = sb("xT", [P, 2, KD, SLOTS])
        w1 = sb("w1", [P, 2, KD, FF])
        w2 = sb("w2", [P, 2, NF, D])
        b1 = sb("b1", [P, 2, NF])
        b2 = sb("b2", [P, 2, D])
        hT = sb("hT", [P, NF, SLOTS])
        y = sb("y", [P, 2, NS, D])

        scattered = flag("scattered")
        w_loaded = [flag("w_even"), flag("w_odd")]
        x_loaded = [flag("x_even"), flag("x_odd")]
        y_stored, y_free = flag("y_stored"), count("y_free", TWO)
        turned, y_ready = count("turned", TWO), count("y_ready", TWO)
        xT_copied = count("xT_copied")
        up_ps, h_raw, h_ready = count("up_ps"), count("h_raw"), count("h_ready")
        down_ps = count("down_ps")
        W_DMAS = 4 if layer == 0 else 2
        e.start_counts()

        def all_tiles(eng, tile):
            with eng.Fori(0, NT // 2) as i:
                for r in range(2):
                    tile(i * 2 + r, i, r)
            if NT % 2:
                tile(NT - 1, NT // 2, 0)

        with nc.Block() as block:
            @block.gpsimd
            def _(pool):
                for b in range(B):
                    for c in range(2):
                        pool.indirect_dma_start(
                            out=e.slot_x, out_offset=bass.IndirectOffsetOnAxis(ap=where[:, c, b:b + 1], axis=0),
                            in_=xn[:, b, :], in_offset=None).then_inc(scattered, 16)
                pool.wait_ge(scattered, 16 * 2 * B)

                def tile(n, i, r):
                    pool.wait_ge(y_ready, TWO + n + 1)
                    pool.dma_start(e.slot_y[bass.ds(n * SLOTS, SLOTS), :].rearrange("(j p) c -> p j c", p=P),
                                   y[:, r]).then_inc(y_stored, 16)
                    pool.wait_ge(y_stored, n * 16 + 16)
                    pool.sem_inc(y_free, 1)

                all_tiles(pool, tile)

            @block.sync
            def _(sp):
                def weights(n, i, r):
                    sp.wait_ge(y_ready, TWO + n - 1)
                    expert = sp.value_load(owner[0:1, bass.ds(n, 1)], min_val=0, max_val=E - 1)
                    one = bass.ds(expert, 1)
                    sp.dma_start(w1[:, r], w1_d[one].rearrange("o (k p) f -> p (o k) f", p=P))\
                      .then_inc(w_loaded[r], 16)
                    sp.dma_start(w2[:, r], w2_d[one].rearrange("o (k p) n -> p (o k) n", p=P))\
                      .then_inc(w_loaded[r], 16)
                    if layer == 0:
                        sp.dma_start(b1[:, r], d["L0_b1_cols"][one].rearrange("o p f -> p (o f)"))\
                          .then_inc(w_loaded[r], 16)
                        sp.dma_start(b2[:, r], wide(d["L0_ffn_b2"][one], 0, P)).then_inc(w_loaded[r], 16)

                def tile(n, i, r):
                    weights(n, i, r)
                    sp.wait_ge(turned, TWO + n - 1)
                    sp.dma_start(x_slots[:, r], e.slot_x[bass.ds(n * SLOTS, SLOTS), :].rearrange(
                        "(j p) c -> p j c", p=P)).then_inc(x_loaded[r], 16)

                sp.wait_ge(scattered, 16 * 2 * B)
                all_tiles(sp, tile)

            @block.tensor
            def _(pe):
                def turn(n, i, r):
                    pe.wait_ge(x_loaded[r], i * 16 + 16)
                    pe.wait_ge(xT_copied, ONE + n)
                    for k in range(KD):
                        for j in range(NS):
                            at = (k * NS + j) * P
                            last = pe.transpose(bank[0][:, at:at + P], x_slots[:, r, j, k * P:(k + 1) * P],
                                                ident[:])
                    last.then_inc(turned, 1)

                def tile(n, i, r):
                    turn(n, i, r)
                    pe.wait_ge(w_loaded[r], (i + 1) * (16 * W_DMAS))
                    pe.wait_ge(xT_copied, ONE + n + 1)
                    for f in range(NF):
                        pe.wait_ge(h_raw, ONE + n * NF + (f - 2 if f >= 3 else 0))
                        for k in range(KD):
                            last = pe.matmul(bank[1 + f % 3][:, 0:SLOTS], w1[:, r, k, f * P:(f + 1) * P],
                                             xT[:, r, k, :], start=(k == 0), stop=(k == KD - 1))
                        last.then_inc(up_ps, 1)
                    pe.wait_ge(y_ready, TWO + n - 1)
                    for j in range(NS):
                        for f in range(NF):
                            if j == 0:
                                pe.wait_ge(h_raw if layer == 0 else h_ready, ONE + n * NF + f + 1)
                            last = pe.matmul(bank[4 + 2 * r + j][:, 0:D], hT[:, f, j * P:(j + 1) * P],
                                             w2[:, r, f, :], start=(f == 0), stop=(f == NF - 1))
                    last.then_inc(down_ps, 1)

                all_tiles(pe, tile)

            @block.scalar
            def _(act):
                def tile(n, i, r):
                    act.wait_ge(turned, TWO + n + 1)
                    act.activation(xT[:, r].rearrange("p k s -> p (k s)"), bank[0][:, 0:KD * SLOTS],
                                   ACT.Copy).then_inc(xT_copied, 1)
                    for f in range(NF):
                        act.wait_ge(up_ps, ONE + n * NF + f + 1)
                        act.wait_ge(down_ps, ONE + n)
                        if layer == 0:
                            act.activation(hT[:, f, :], bank[1 + f % 3][:, 0:SLOTS], ACT.Gelu,
                                           bias=b1[:, r, f:f + 1]).then_inc(h_raw, 1)
                        else:
                            act.activation(hT[:, f, :], bank[1 + f % 3][:, 0:SLOTS], ACT.Relu).then_inc(h_raw, 1)

                all_tiles(act, tile)

            @block.vector
            def _(dve):
                def tile(n, i, r):
                    if layer == 1:
                        for f in range(NF):
                            dve.wait_ge(h_raw, ONE + n * NF + f + 1)
                            dve.tensor_tensor(hT[:, f, :], hT[:, f, :], hT[:, f, :], ALU.mult)\
                               .then_inc(h_ready, 1)
                    dve.wait_ge(down_ps, ONE + n + 1)
                    dve.wait_ge(y_free, TWO + n - 1)
                    for j in range(NS):
                        ps = bank[4 + 2 * r + j][:, 0:D]
                        if layer == 0:
                            last = dve.tensor_tensor(y[:, r, j, :], ps, b2[:, r, :], ALU.add)
                        else:
                            last = dve.tensor_copy(y[:, r, j, :], ps)
                    last.then_inc(y_ready, 1)

                all_tiles(dve, tile)

        RING = 4
        near = sb("near", [T, RING, 2, D])
        collected = [flag(f"collected{i}") for i in range(RING)]
        added = flag("added")
        with nc.Block() as block:
            @block.gpsimd
            def _(pool):
                for b in range(B):
                    if b >= RING:
                        pool.wait_ge(added, 2 * (b - RING + 1))
                    for c in range(2):
                        pool.indirect_dma_start(
                            out=near[:, b % RING, c, :], out_offset=None, in_=e.slot_y,
                            in_offset=bass.IndirectOffsetOnAxis(ap=where[:, c, b:b + 1], axis=0))\
                            .then_inc(collected[b % RING], 16)

            @block.vector
            def _(dve):
                link = Chain(dve, added)
                for b in range(B):
                    dve.wait_ge(collected[b % RING], 32 * (b // RING + 1))
                    for c in range(2):
                        link(dve.scalar_tensor_tensor(out=x[:, b, :], in0=near[:, b % RING, c, :],
                                                      scalar=share[:, c, b:b + 1], in1=x[:, b, :], op0=ALU.mult,
                                                      op1=ALU.add))
                    if layer == 0:
                        e.residual_stats(dve, b)


def gated_attention(e):
    nc, sem, bank, x, mv, rstd, ident, w = e.nc, e.sem, e.bank, e.x, e.mv, e.rstd, e.ident, e.w
    T, D, B, NG, GT, KD = e.T, e.D, e.B, e.NG, e.GT, e.KD
    EE = 512
    NE = EE // P
    with ExitStack() as st:
        def sb(name, shape):
            return st.enter_context(nc.sbuf_tensor("ga_" + name, shape, F32))

        def count(name):
            return e.count("ga_" + name)

        def flag(name):
            return sem("ga_" + name)

        rstd1 = sb("rstd1", [T, B])
        xn = sb("xn", [T, GROUP, D])
        xn1 = sb("xn1", [T, GROUP, D])
        xnT = sb("xnT", [P, KD, GT])
        uT = sb("uT", [P, NE, GT])
        zT = sb("zT", [P, GT])
        qT, kT = sb("qT", [P, GT]), sb("kT", [P, GT])
        v = sb("v", [T, GROUP, EE])
        aT = sb("aT", [T, GT])
        hT = sb("hT", [P, NE, GT])

        asked1, std1, asked2, std2, pre = flag("asked1"), flag("std1"), flag("asked2"), flag("std2"), flag("pre")
        xn_ready, xT_ps, xT_ready = count("xn_ready"), count("xT_ps"), count("xT_ready")
        xn1_ready, xn1_based = count("xn1_ready"), count("xn1_based")
        uz_ps, z_ready, u_ready = count("uz_ps"), count("z_ready"), count("u_ready")
        qk_ready = count("qk_ready")
        v_ps, v_biased, v_ready = count("v_ps"), count("v_biased"), count("v_ready")
        a_ps, a_relu, a_ready = count("a_ps"), count("a_relu"), count("a_ready")
        av_ps, h_ready, y_ps = count("av_ps"), count("h_ready"), count("y_ps")
        tail = flag("tail")

        e.start_counts()
        with nc.Block() as block:
            @block.tensor
            def _(pe):
                with pe.Fori(0, NG) as g:
                    pe.wait_ge(xn_ready, ONE + g * GROUP + GROUP)
                    for k in range(KD):
                        for s in range(GROUP):
                            last = pe.transpose(bank[k][:, s * T:(s + 1) * T], xn[:, s, k * P:(k + 1) * P],
                                                ident[0:T, 0:T])
                        last.then_inc(xT_ps, 1)
                    pe.wait_ge(xT_ready, ONE + g * 2 + 2)
                    def up(to, m):
                        for k in range(KD):
                            last = pe.matmul(to[:, 0:GT], w.in_[:, k, m * P:(m + 1) * P], xnT[:, k, :],
                                             start=(k == 0), stop=(k == KD - 1))
                        last.then_inc(uz_ps, 1)
                    up(bank[2], 2 * NE)
                    for s in range(GROUP):
                        if s >= 2:
                            pe.wait_ge(v_biased, ONE + g * GROUP + s - 1)
                        for k in range(KD):
                            last = pe.matmul(bank[4 + s % 2][0:T, :], xnT[:, k, s * T:(s + 1) * T],
                                             w.in_[:, k, EE:2 * EE], start=(k == 0), stop=(k == KD - 1))
                        last.then_inc(v_ps, 1)
                        if s >= 2:
                            pe.wait_ge(u_ready, ONE + g * NE + s - 1)
                        up(bank[6 + s % 2], s)
                    pe.wait_ge(qk_ready, ONE + g * 2 + 2)
                    for s in range(GROUP):
                        at = slice(s * T, (s + 1) * T)
                        last = pe.matmul(bank[3][0:T, at], kT[:, at], qT[:, at], start=True, stop=True)
                    last.then_inc(a_ps, 1)
                    pe.wait_ge(a_ready, ONE + g + 1)
                    pe.wait_ge(v_ready, ONE + g * GROUP + GROUP)
                    pe.wait_ge(v_biased, ONE + g * GROUP + GROUP)
                    pe.wait_ge(u_ready, ONE + g * NE + NE)
                    for m in range(NE):
                        for s in range(GROUP):
                            at = slice(s * T, (s + 1) * T)
                            last = pe.matmul(bank[4 + m][:, at], v[:, s, m * P:(m + 1) * P], aT[:, at],
                                             start=True, stop=True)
                        last.then_inc(av_ps, 1)
                    for s in range(GROUP):
                        if s >= 2:
                            pe.wait_ge(tail, g * (2 * GROUP) + 2 * (s - 2) + 1)
                        for m in range(NE):
                            if s == 0:
                                pe.wait_ge(h_ready, ONE + g * NE + m + 1)
                            last = pe.matmul(bank[s % 2][0:T, 0:D], hT[:, m, s * T:(s + 1) * T], w.out[:, m, :],
                                             start=(m == 0), stop=(m == NE - 1))
                        last.then_inc(y_ps, 1)
                    pe.wait_ge(tail, g * (2 * GROUP) + 2 * (GROUP - 1) + 1)

            @block.scalar
            def _(act):
                e.make_rstd_act(act, std1, asked1, e.norm_tmp)
                e.make_rstd_act(act, std2, asked2, e.norm_tmp)
                with act.Fori(0, NG) as g:
                    for k in range(KD):
                        act.wait_ge(xT_ps, ONE + g * 2 + k + 1)
                        act.wait_ge(uz_ps, ONE + g * (NE + 1))
                        act.activation(xnT[:, k, :], bank[k][:, 0:GT], ACT.Copy).then_inc(xT_ready, 1)
                    act.wait_ge(uz_ps, ONE + g * (NE + 1) + 1)
                    act.wait_ge(qk_ready, ONE + g * 2)
                    act.activation(zT[:], bank[2][:, 0:GT], ACT.Silu, bias=w.b_in_u[:, 8:9]).then_inc(z_ready, 1)
                    for s in range(GROUP):
                        act.wait_ge(v_biased, ONE + g * GROUP + s + 1)
                        act.activation(v[:, s, :], v[:, s, :], ACT.Silu).then_inc(v_ready, 1)
                        act.wait_ge(uz_ps, ONE + g * (NE + 1) + s + 2)
                        act.wait_ge(h_ready, ONE + g * NE)
                        act.activation(uT[:, s, :], bank[6 + s % 2][:, 0:GT], ACT.Silu,
                                       bias=w.b_in_u[:, s:s + 1]).then_inc(u_ready, 1)
                    act.wait_ge(a_ps, ONE + g + 1)
                    act.activation(aT[:], bank[3][0:T, 0:GT], ACT.Relu, scale=1.0 / T).then_inc(a_relu, 1)

            @block.gpsimd
            def _(pool):
                with pool.Fori(0, NG) as g:
                    pool.wait_ge(xn1_ready, ONE + g * GROUP + GROUP)
                    pool.tensor_tensor(xn1[:], xn1[:], wide(w.b_out[:].unsqueeze(1), 1, GROUP), ALU.add)\
                        .then_inc(xn1_based, 1)

            @block.vector
            def _(dve):
                chain = Chain(dve, pre)
                e.make_rstd_dve(dve, chain, std1, asked1, mv, rstd1[:], e.norm_tmp, False, e.stat6)
                e.make_rstd_dve(dve, chain, std2, asked2, mv, rstd[:], e.norm_tmp, True)
                with dve.Fori(0, NG) as g:
                    dve.wait_ge(xT_ps, ONE + g * 2)
                    for s in range(GROUP):
                        b = g * GROUP + s
                        dve.tensor_scalar(xn[:, s, :], x[:, b, :], mv[:, b, 0:1], rstd[:, bass.ds(b, 1)],
                                          ALU.subtract, ALU.mult).then_inc(xn_ready, 1)
                    for s in range(GROUP):
                        b = g * GROUP + s
                        dve.tensor_scalar(xn1[:, s, :], x[:, b, :], mv[:, b, 0:1], rstd1[:, bass.ds(b, 1)],
                                          ALU.subtract, ALU.mult).then_inc(xn1_ready, 1)
                    for s in range(GROUP):
                        dve.wait_ge(v_ps, ONE + g * GROUP + s + 1)
                        dve.wait_ge(av_ps, ONE + g * NE)
                        dve.tensor_tensor(v[:, s, :], bank[4 + s % 2][0:T, :], w.b_in_v[:], ALU.add)\
                           .then_inc(v_biased, 1)
                        if s == 1:
                            dve.wait_ge(z_ready, ONE + g + 1)
                            dve.wait_ge(a_ps, ONE + g)
                            dve.tensor_scalar(qT[:], zT[:], w.gq[:, 0:1], w.gq[:, 1:2], ALU.mult,
                                              ALU.add).then_inc(qk_ready, 1)
                            dve.tensor_scalar(kT[:], zT[:], w.gq[:, 2:3], w.gq[:, 3:4], ALU.mult,
                                              ALU.add).then_inc(qk_ready, 1)
                    dve.wait_ge(a_relu, ONE + g + 1)
                    dve.tensor_tensor(aT[:], aT[:], aT[:], ALU.mult).then_inc(a_ready, 1)
                    for m in range(NE):
                        dve.wait_ge(av_ps, ONE + g * NE + m + 1)
                        dve.wait_ge(u_ready, ONE + g * NE + m + 1)
                        dve.tensor_tensor(hT[:, m, :], bank[4 + m][:, 0:GT], uT[:, m, :], ALU.mult)\
                           .then_inc(h_ready, 1)
                    dve.wait_ge(xn1_based, ONE + g + 1)
                    link = Chain(dve, tail, g * (2 * GROUP), 2 * GROUP)
                    for s in range(GROUP):
                        b = g * GROUP + s
                        dve.wait_ge(y_ps, ONE + b + 1)
                        link(dve.tensor_tensor(xn1[:, s, :], xn1[:, s, :], bank[s % 2][0:T, 0:D], ALU.add))
                        link(dve.tensor_tensor(x[:, b, :], x[:, b, :], xn1[:, s, :], ALU.add))
                        e.residual_stats(dve, b, s)
                    link.close()


def kernel(**inputs):
    import concourse.bacc as bacc
    from concourse.bass_utils import run_bass_kernel_spmd

    a = {k: np.asarray(v) for k, v in inputs.items()}
    a["L0_Wq"], a["L0_Wk"] = a["L0_attn_W_qk"][:, 0::2], a["L0_attn_W_qk"][:, 1::2]
    a["L0_bq"], a["L0_bk"] = a["L0_attn_b_qk"][0::2], a["L0_attn_b_qk"][1::2]
    for n in "qkvo":
        a[f"L0_xW{n}_T"] = a.pop(f"L0_xattn_W{n}").T
    a["router_T"] = a.pop("L1_ffn_router_w").T
    a["ctx_T"] = a["ctx_768"].transpose(2, 0, 1)
    del a["L0_attn_W_qk"], a["L0_attn_b_qk"]
    for name in ("L0_bq", "L0_bk", "L0_attn_b_v", "L1_attn_ln_g", "L1_attn_ln_b", "L0_xattn_bq", "L0_xattn_bk",
                 "L1_xattn_bq", "L1_xattn_bk", "L1_xattn_norm_g", "L1_xattn_norm_b"):
        a[name] = a[name].reshape(-1, P).T
    a["L0_b1_cols"] = a["L0_ffn_b1"].reshape(8, -1, P).transpose(0, 2, 1)
    a["L1_b_in_cols"] = a["L1_attn_b_in"].reshape(-1, P).T
    a = {k: np.ascontiguousarray(v) for k, v in a.items()}

    nc = bacc.Bacc("TRN2", target_bir_lowering=False, num_devices=1)
    d = {k: nc.dram_tensor(f"in_{k}", v.shape, mybir.dt.from_np(v.dtype), kind="ExternalInput").ap()
         for k, v in a.items()}
    out = nc.dram_tensor("out_x", a["x"].shape, F32, kind="ExternalOutput").ap()
    decoder(nc, d, out)
    r = run_bass_kernel_spmd(nc, [{f"in_{k}": v for k, v in a.items()}], core_ids=[0])
    return r.results[0]["out_x"]
```

```python
from contextlib import ExitStack

import numpy as np

import concourse.bass as bass
from concourse import mybir

ALU = mybir.AluOpType
ACT = mybir.ActivationFunctionType
F32 = mybir.dt.float32
AX_X = mybir.AxisListType.X

P = 128
EPS = 1e-5
GROUP = 4
ONE = 1
TWO = 2
LAST_STAGE = 6


def wide(ap, axis, n):
    shape = list(ap.shape)
    shape[axis] = n
    return ap.broadcast_to(shape)


class Parts:
    pass


class Chain:

    def __init__(self, eng, sem, before=0, length=None):
        self.eng, self.sem, self.before, self.length, self.n = eng, sem, before, length, 0

    def __call__(self, ins):
        self.n += 1
        ins.then_inc(self.sem, 1)
        self.eng.wait_ge(self.sem, self.before + self.n)

    def close(self):
        assert self.length == self.n, (self.length, self.n)


def decoder(nc, d, out):
    B, T, D = d["x"].shape
    NG = B // GROUP
    GT = GROUP * T
    KD = D // P
    NKV = d["ctx_768"].shape[1]
    DC = d["ctx_768"].shape[2]
    KB = 125
    NJ = NKV // KB
    C1 = DC - P
    XH, XD = 16, D // 16
    AH, AD = 8, 64
    E = 8
    SLOTS = 2 * P
    NT = (2 * B * T - E) // SLOTS + E

    ctx = ExitStack()
    with ctx:
        def sb(name, shape, dt=F32):
            return ctx.enter_context(nc.sbuf_tensor(name, shape, dt))

        stage_sems = []

        def sem(name):
            stage_sems.append(nc.alloc_semaphore(name=name))
            return stage_sems[-1]

        counts = []

        def count(name, start=ONE):
            counts.append((sem(name), start))
            return counts[-1][0]

        def start_counts():
            for s, start in counts:
                nc.gpsimd.sem_inc(s, start)
            counts.clear()
            nc.all_engine_barrier()

        def end_stage():
            nc.clear_and_free_semaphores(list(stage_sems))
            nc.all_engine_barrier()
            stage_sems.clear()

        bank = [ctx.enter_context(nc.psum_tensor(f"bank{i}", [P, 512], F32)) for i in range(8)]

        x = sb("x_res", [T, B, D])
        mv = sb("x_mean_var", [T, B, 2])
        rstd = sb("x_rstd", [T, B])
        ident = sb("ident", [P, P])
        norm_tmp = sb("norm_tmp", [T, 3, B])
        stat6 = sb("stat6", [T, B, 6])
        cstat = sb("context_stat6", [KB, B * NJ, 6])
        scratch = sb("scratch", [P, GROUP])

        w = Parts()
        w.q = sb("w_q", [P, KD, AH * AD])
        w.k = sb("w_k", [P, KD, AH * AD])
        w.v = sb("w_v", [P, KD, AH * AD])
        w.o = sb("w_o", [P, 4, D])
        w.bq = sb("w_bq", [P, 4])
        w.bk = sb("w_bk", [P, 4])
        w.bv = sb("w_bv", [P, 4])
        w.bo = sb("w_bo", [T, D])
        w.ln_g = sb("w_ln_g", [T, D])
        w.ln_b = sb("w_ln_b", [T, D])
        w.in_ = sb("w_in", [P, KD, 1152])
        w.out = sb("w_out", [P, 4, D])
        w.b_in_u = sb("w_b_in_u", [P, 9])
        w.b_in_v = sb("w_b_in_v", [T, 512])
        w.b_out = sb("w_b_out", [T, D])
        w.gq = sb("w_gq", [P, 4])
        w.ln_gb = sb("w_ln_gb", [P, 2 * KD])
        w.ln_b_wide = sb("w_ln_b_wide", [P, KD, T])
        xa = []
        for n in range(2):
            a = Parts()
            a.wq = sb(f"x{n}_wq", [P, KD, D])
            a.wk = sb(f"x{n}_wk", [P, 2, D])
            a.wv = sb(f"x{n}_wv", [P, 2, D])
            a.bq = sb(f"x{n}_bq", [P, 1, KD])
            a.bk = sb(f"x{n}_bk", [P, KD])
            a.bv = sb(f"x{n}_bv", [P, D])
            xa.append(a)
        xa[0].wo = sb("x0_wo", [P, KD, D])
        xa[0].bo = sb("x0_bo", [T, D])
        xa[1].gb = sb("x1_gb", [P, 8])
        xa[1].b_wide = sb("x1_b_wide", [P, 4, P])
        head_mask = sb("head_mask", [P, P // XD])

        FOLD_WIDE = KD + 2
        loads = sem("setup_loads")
        const_ready = sem("const_ready")
        fold_chain = sem("fold_chain")
        fold_ps = sem("fold_ps")

        def cols(ap, k):
            return ap if k > 1 else ap.rearrange("(p k) -> p k", k=1)

        def rows(ap, parts):
            return ap.partition_broadcast(parts)

        setup_loads = [
            (w.q[:], d["L0_Wq"].rearrange("(k p) n -> p k n", p=P)),
            (w.k[:], d["L0_Wk"].rearrange("(k p) n -> p k n", p=P)),
            (w.v[:], d["L0_attn_W_v"].rearrange("(k p) n -> p k n", p=P)),
            (w.o[:], d["L0_attn_W_out"].rearrange("(k p) n -> p k n", p=P)),
            (w.bq[:], cols(d["L0_bq"], 4)),
            (w.bk[:], cols(d["L0_bk"], 4)),
            (w.bv[:], cols(d["L0_attn_b_v"], 4)),
            (w.bo[:], rows(d["L0_attn_b_out"], T)),
            (w.ln_g[:], rows(d["L0_attn_ln_gamma"], T)),
            (w.ln_b[:], rows(d["L0_attn_ln_beta"], T)),
            (w.in_[:], d["L1_attn_W_in"].rearrange("(k p) n -> p k n", p=P)),
            (w.out[:], d["L1_attn_W_out"].rearrange("(k p) n -> p k n", p=P)),
            (w.b_in_u[:], cols(d["L1_b_in_cols"], 9)),
            (w.b_in_v[:], rows(d["L1_attn_b_in"][512:1024], T)),
            (w.b_out[:], rows(d["L1_attn_b_out"], T)),
            (w.gq[:, 0:1], cols(d["L1_attn_gamma_q"], 1)),
            (w.gq[:, 1:2], cols(d["L1_attn_beta_q"], 1)),
            (w.gq[:, 2:3], cols(d["L1_attn_gamma_k"], 1)),
            (w.gq[:, 3:4], cols(d["L1_attn_beta_k"], 1)),
            (w.ln_gb[:, 0:KD], cols(d["L1_attn_ln_g"], KD)),
            (w.ln_gb[:, KD:2 * KD], cols(d["L1_attn_ln_b"], KD)),
            (xa[0].wq[:], d["L0_xWq_T"].rearrange("(k p) n -> p k n", p=P)),
            (xa[0].wk[:, 0, :], d["L0_xWk_T"][0:P, :]),
            (xa[0].wk[0:C1, 1, :], d["L0_xWk_T"][P:DC, :]),
            (xa[0].wv[:, 0, :], d["L0_xWv_T"][0:P, :]),
            (xa[0].wv[0:C1, 1, :], d["L0_xWv_T"][P:DC, :]),
            (xa[0].wo[:], d["L0_xWo_T"].rearrange("(k p) n -> p k n", p=P)),
            (xa[0].bq[:, 0, :], cols(d["L0_xattn_bq"], KD)),
            (xa[0].bk[:], cols(d["L0_xattn_bk"], KD)),
            (xa[0].bv[:], rows(d["L0_xattn_bv"], P)),
            (xa[0].bo[:], rows(d["L0_xattn_bo"], T)),
            (xa[1].wq[:], d["L1_xattn_Wq"].rearrange("(k p) n -> p k n", p=P)),
            (xa[1].wk[:, 0, :], d["L1_xattn_Wk"][0:P, :]),
            (xa[1].wk[0:C1, 1, :], d["L1_xattn_Wk"][P:DC, :]),
            (xa[1].wv[:, 0, :], d["L1_xattn_Wv"][0:P, :]),
            (xa[1].wv[0:C1, 1, :], d["L1_xattn_Wv"][P:DC, :]),
            (xa[1].bq[:, 0, :], cols(d["L1_xattn_bq"], KD)),
            (xa[1].bk[:], cols(d["L1_xattn_bk"], KD)),
            (xa[1].bv[:], rows(d["L1_xattn_bv"], P)),
            (xa[1].gb[:, 0:KD], cols(d["L1_xattn_norm_g"], KD)),
            (xa[1].gb[:, KD:2 * KD], cols(d["L1_xattn_norm_b"], KD)),
            (xa[1].gb[:, 4:5], cols(d["L1_xattn_tnorm_g"][0:P], 1)),
            (xa[1].gb[0:C1, 5:6], d["L1_xattn_tnorm_g"][P:DC].rearrange("(p a) -> p a", a=1)),
            (xa[1].gb[:, 6:7], cols(d["L1_xattn_tnorm_b"][0:P], 1)),
            (xa[1].gb[0:C1, 7:8], d["L1_xattn_tnorm_b"][P:DC].rearrange("(p a) -> p a", a=1)),
            (x[:], d["x"].rearrange("b t d -> t b d")),
        ]

        def residual_stats(dve, b, col=None):
            if col is not None:
                dve.memset(scratch[0:T, col:col + 1], 0.0)
            dve.bn_stats(stat6[:, b, :], x[:, b, :])

        with nc.Block() as block:
            @block.sync
            def _(sp):
                for dst, src in setup_loads:
                    sp.dma_start(dst, src).then_inc(loads, 16)

            @block.gpsimd
            def _(pool):
                made = Chain(pool, const_ready)
                made(pool.memset(ident[:], 0.0))
                made(pool.affine_select(out=ident[:], in_=ident[:], compare_op=ALU.not_equal, fill=1.0,
                                        base=0, pattern=[[-1, P]], channel_multiplier=1))
                made(pool.memset(head_mask[:], XD ** -0.5))
                made(pool.affine_select(out=head_mask[:], in_=head_mask[:], compare_op=ALU.is_ge, fill=0.0,
                                        base=0, pattern=[[-XD, P // XD]], channel_multiplier=1))
                made(pool.affine_select(out=head_mask[:], in_=head_mask[:], compare_op=ALU.is_ge, fill=0.0,
                                        base=XD - 1, pattern=[[XD, P // XD]], channel_multiplier=-1))

            @block.vector
            def _(dve):
                fold = Chain(dve, fold_chain)
                dve.wait_ge(loads, 16 * len(setup_loads))
                dve.wait_ge(const_ready, 5)
                for k in range(KD):
                    fold(dve.tensor_scalar(w.ln_b_wide[:, k, :], ident[:, 0:T], 0.0,
                                           w.ln_gb[:, KD + k:KD + k + 1], ALU.mult, ALU.add))
                for k in range(2):
                    n = P if k == 0 else C1
                    fold(dve.tensor_scalar(xa[1].b_wide[0:n, 2 + k, :], ident[0:n, :], 0.0,
                                           xa[1].gb[0:n, 6 + k:7 + k], ALU.mult, ALU.add))
                assert fold.n == FOLD_WIDE
                dve.wait_ge(fold_ps, 1)
                fold(dve.tensor_tensor(w.bo[:], w.bo[:], bank[0][0:T, 0:D], ALU.add))
                fold(dve.tensor_tensor(w.b_in_v[:], w.b_in_v[:], bank[1][0:T, :], ALU.add))
                fold(dve.tensor_tensor(w.b_in_u[:], w.b_in_u[:], bank[2][:, 0:9], ALU.add))
                fold(dve.tensor_tensor(xa[1].bq[:, 0, :], xa[1].bq[:, 0, :], bank[2][:, 16:16 + KD], ALU.add))
                fold(dve.tensor_tensor(xa[1].bk[:], xa[1].bk[:], bank[2][:, 32:32 + KD], ALU.add))
                fold(dve.tensor_tensor(xa[1].bv[:], xa[1].bv[:], bank[3][:, 0:D], ALU.add))
                for k in range(KD):
                    fold(dve.tensor_scalar(w.in_[:, k, :], w.in_[:, k, :], w.ln_gb[:, k:k + 1], None, ALU.mult))
                    fold(dve.tensor_scalar(xa[1].wq[:, k, :], xa[1].wq[:, k, :], xa[1].gb[:, k:k + 1], None,
                                           ALU.mult))
                    n = P if k == 0 else C1
                    for wt in (xa[1].wk, xa[1].wv):
                        fold(dve.tensor_scalar(wt[0:n, k, :], wt[0:n, k, :], xa[1].gb[0:n, 4 + k:5 + k], None,
                                               ALU.mult))
                for b in range(B):
                    residual_stats(dve, b)

            @block.tensor
            def _(pe):
                pe.wait_ge(loads, 16 * len(setup_loads))
                pe.wait_ge(fold_chain, FOLD_WIDE)
                for k in range(4):
                    pe.matmul(bank[0][0:T, 0:D], wide(w.bv[:, k:k + 1], 1, T), w.o[:, k, :],
                              start=(k == 0), stop=(k == 3))
                for k in range(KD):
                    pe.matmul(bank[1][0:T, :], w.ln_b_wide[:, k, :], w.in_[:, k, 512:1024],
                              start=(k == 0), stop=(k == KD - 1))
                for m in range(9):
                    for k in range(KD):
                        pe.matmul(bank[2][:, m:m + 1], w.in_[:, k, m * P:(m + 1) * P],
                                  w.ln_gb[:, KD + k:KD + k + 1], start=(k == 0), stop=(k == KD - 1))
                for m in range(KD):
                    for k in range(KD):
                        pe.matmul(bank[2][:, 16 + m:17 + m], xa[1].wq[:, k, m * P:(m + 1) * P],
                                  xa[1].gb[:, KD + k:KD + k + 1], start=(k == 0), stop=(k == KD - 1))
                    for k in range(2):
                        n = P if k == 0 else C1
                        pe.matmul(bank[2][:, 32 + m:33 + m], xa[1].wk[0:n, k, m * P:(m + 1) * P],
                                  xa[1].gb[0:n, 6 + k:7 + k], start=(k == 0), stop=(k == 1))
                for k in range(2):
                    n = P if k == 0 else C1
                    last = pe.matmul(bank[3][:, 0:D], xa[1].b_wide[0:n, 2 + k, :], xa[1].wv[0:n, k, :],
                                     start=(k == 0), stop=(k == 1))
                last.then_inc(fold_ps, 1)

        def mean_var(dve, chain, six, stats, tmp, width):
            chain(dve.tensor_tensor(tmp[:, 0, :], six[:, :, 1], six[:, :, 4], ALU.add))
            chain(dve.tensor_tensor(tmp[:, 1, :], six[:, :, 1], six[:, :, 4], ALU.subtract))
            chain(dve.tensor_tensor(tmp[:, 2, :], six[:, :, 2], six[:, :, 5], ALU.add))
            chain(dve.tensor_scalar(stats[:, :, 0], tmp[:, 0, :], 0.5, None, ALU.mult))
            chain(dve.tensor_tensor(tmp[:, 1, :], tmp[:, 1, :], tmp[:, 1, :], ALU.mult))
            chain(dve.tensor_scalar(tmp[:, 1, :], tmp[:, 1, :], 0.25, None, ALU.mult))
            chain(dve.tensor_scalar(tmp[:, 2, :], tmp[:, 2, :], 1.0 / width, None, ALU.mult))
            chain(dve.tensor_tensor(stats[:, :, 1], tmp[:, 1, :], tmp[:, 2, :], ALU.add))

        def make_rstd_dve(dve, chain, std_ready, std_asked, stats, rs, tmp, double, six=None, width=D):
            if six is not None:
                mean_var(dve, chain, six, stats, tmp, width)
            chain(dve.tensor_scalar(tmp[:, 0, :], stats[:, :, 1], 1.0 + EPS if double else 1.0,
                                    EPS * EPS if double else EPS, ALU.mult, ALU.add))
            dve.sem_inc(std_asked, 1)
            dve.wait_ge(std_ready, 1)
            chain(dve.reciprocal(tmp[:, 2, :], tmp[:, 1, :]))
            chain(dve.tensor_tensor(tmp[:, 1, :], tmp[:, 2, :], tmp[:, 2, :], ALU.mult))
            chain(dve.tensor_tensor(tmp[:, 1, :], tmp[:, 1, :], tmp[:, 0, :], ALU.mult))
            chain(dve.tensor_scalar(tmp[:, 1, :], tmp[:, 1, :], -0.5, 1.5, ALU.mult, ALU.add))
            chain(dve.tensor_tensor(rs, tmp[:, 2, :], tmp[:, 1, :], ALU.mult))

        def make_rstd_act(act, std_ready, std_asked, tmp):
            act.wait_ge(std_asked, 1)
            act.activation(tmp[:, 1, :], tmp[:, 0, :], ACT.Sqrt).then_inc(std_ready, 1)

        env = Parts()
        env.nc, env.d, env.B, env.T, env.D, env.NG, env.GT, env.KD = (
            nc, d, B, T, D, NG, GT, KD)
        env.NKV, env.DC, env.KB, env.NJ, env.C1, env.XH, env.XD, env.AH = (
            NKV, DC, KB, NJ, C1, XH, XD, AH)
        env.AD, env.E, env.bank, env.x, env.mv, env.rstd, env.ident, env.norm_tmp = (
            AD, E, bank, x, mv, rstd, ident, norm_tmp)
        env.stat6, env.scratch, env.head_mask, env.w, env.xa, env.sem, env.count, env.start_counts = (
            stat6, scratch, head_mask, w, xa, sem, count, start_counts)
        env.residual_stats, env.make_rstd_dve, env.make_rstd_act = (
            residual_stats, make_rstd_dve, make_rstd_act)
        slot_x = nc.dram_tensor("slot_x", [NT * SLOTS, D], F32, kind="Internal").ap()
        slot_y = nc.dram_tensor("slot_y", [NT * SLOTS, D], F32, kind="Internal").ap()
        env.cstat = cstat
        env.slot_x, env.slot_y, env.SLOTS, env.NT = slot_x, slot_y, SLOTS, NT
        end_stage()
        stages = [self_attention, lambda e: cross_attention(e, 0), lambda e: experts(e, 0),
                  gated_attention, lambda e: cross_attention(e, 1), lambda e: experts(e, 1)]
        for stage in stages[:LAST_STAGE]:
            stage(env)
            end_stage()

        stored = sem("out_stored")
        with nc.Block() as block:
            @block.sync
            def _(sp):
                sp.dma_start(out.rearrange("b t d -> t b d"), x[:]).then_inc(stored, 16)
                sp.wait_ge(stored, 16)


def self_attention(e):
    nc, sem, bank, x, mv, rstd, ident, w = e.nc, e.sem, e.bank, e.x, e.mv, e.rstd, e.ident, e.w
    T, D, B, NG, GT, KD, H, HD = e.T, e.D, e.B, e.NG, e.GT, e.KD, e.AH, e.AD
    UNITS = GROUP * 2
    HU = H // 2
    with ExitStack() as st:
        def sb(name, shape):
            return st.enter_context(nc.sbuf_tensor(name, shape, F32))

        y_all = sb("sa_y", [T, B, D])
        y_mv = sb("sa_y_mv", [T, B, 2])
        y_rstd = sb("sa_y_rstd", [T, B])
        y_tmp = sb("sa_y_tmp", [T, 3, B])
        y_stat = sb("sa_y_stat", [T, B, 6])
        xn = sb("sa_xn", [T, GROUP, D])
        xnT = sb("sa_xnT", [P, KD, GT])
        qT = sb("sa_qT", [P, 4, GT])
        kT = sb("sa_kT", [P, 4, GT])
        v = sb("sa_v", [T, GROUP, H, HD + 1])
        mx = sb("sa_max", [T, 2, HU])
        prob = sb("sa_prob", [T, 2, HU, T])
        probT = sb("sa_probT", [T, 2, HU, T])
        rinv = sb("sa_rinv", [T, 2, HU])
        o = sb("sa_o", [T, 2, H, HD])
        oT = sb("sa_oT", [P, 2, 4, T])

        count, flag = e.count, sem
        std_asked, std_ready = flag("sa_std_asked"), flag("sa_std_ready")
        pre = flag("sa_pre")
        xn_ready = count("sa_xn_ready")
        xT_ps = count("sa_xT_ps")
        xT_ready = count("sa_xT_ready")
        qk_ps = count("sa_qk_ps")
        q_ready, k_ready = count("sa_q_ready"), count("sa_k_ready")
        v_ps, v_ready = count("sa_v_ps"), count("sa_v_ready")
        s_ps = count("sa_scores_ps")
        mx_done = count("sa_max_done")
        shifted = count("sa_shifted")
        exp_done = count("sa_exp_done")
        pT_ps, pT_ready = count("sa_probT_ps"), count("sa_probT_ready")
        pv_ps = count("sa_pv_ps")
        rinv_done = count("sa_rinv_done")
        o_ready = count("sa_o_ready")
        oT_ps, oT_ready = count("sa_oT_ps"), count("sa_oT_ready")
        y_ps, y_done = count("sa_y_ps"), count("sa_y_done")

        e.start_counts()
        with nc.Block() as block:
            @block.tensor
            def _(pe):
                with pe.Fori(0, NG) as g:
                    pe.wait_ge(xn_ready, ONE + g * GROUP + GROUP)
                    for k in range(KD):
                        for s in range(GROUP):
                            last = pe.transpose(bank[k][:, s * T:(s + 1) * T], xn[:, s, k * P:(k + 1) * P],
                                                ident[0:T, 0:T])
                        last.then_inc(xT_ps, 1)
                    for m in range(4):
                        for side, (wt, ready) in enumerate(((w.q, q_ready), (w.k, k_ready))):
                            if m == 0 and side == 0:
                                pe.wait_ge(xT_ready, ONE + g * 2 + 2)
                            if m > 0:
                                pe.wait_ge(ready, ONE + g * 4 + m)
                            for k in range(KD):
                                last = pe.matmul(bank[2 + side][:, 0:GT], wt[:, k, m * P:(m + 1) * P],
                                                 xnT[:, k, :], start=(k == 0), stop=(k == KD - 1))
                            last.then_inc(qk_ps, 1)
                    for s in range(GROUP):
                        if s >= 2:
                            pe.wait_ge(v_ready, ONE + g * GROUP + s - 1)
                        for k in range(KD):
                            last = pe.matmul(bank[s % 2][0:T, :], xnT[:, k, s * T:(s + 1) * T], w.v[:, k, :],
                                             start=(k == 0), stop=(k == KD - 1))
                        last.then_inc(v_ps, 1)
                    pe.wait_ge(q_ready, ONE + g * 4 + 4)
                    pe.wait_ge(k_ready, ONE + g * 4 + 4)

                    def scores(u):
                        s = u // 2
                        if u >= 2:
                            pe.wait_ge(shifted, ONE + g * UNITS + u - 1)
                        for i in range(HU):
                            h = 2 * i + u % 2
                            p0 = HD * (h % 2)
                            last = pe.matmul(bank[4 + u % 2][0:T, i * T:(i + 1) * T],
                                             qT[p0:p0 + HD, h // 2, s * T:(s + 1) * T],
                                             kT[p0:p0 + HD, h // 2, s * T:(s + 1) * T], start=True, stop=True)
                        last.then_inc(s_ps, 1)

                    def turn_prob(u):
                        pe.wait_ge(exp_done, ONE + g * UNITS + u + 1)
                        if u < 2:
                            pe.wait_ge(v_ready, ONE + g * GROUP + 4)
                        for i in range(HU):
                            last = pe.transpose(bank[u % 2][0:T, i * T:(i + 1) * T], prob[:, u % 2, i, :],
                                                ident[0:T, 0:T])
                        last.then_inc(pT_ps, 1)

                    def values(u):
                        s = u // 2
                        pe.wait_ge(pT_ready, ONE + g * UNITS + u + 1)
                        if u >= 2:
                            pe.wait_ge(o_ready, ONE + g * UNITS + u - 1)
                        for i in range(HU):
                            h = 2 * i + u % 2
                            last = pe.matmul(bank[2 + u % 2][0:T, i * (HD + 1):(i + 1) * (HD + 1)],
                                             probT[:, u % 2, i, :], v[:, s, h, :], start=True, stop=True)
                        last.then_inc(pv_ps, 1)

                    def turn_out(s):
                        pe.wait_ge(o_ready, ONE + g * UNITS + 2 * s + 2)
                        ov = o[:, s % 2].rearrange("t h e -> t (h e)")
                        for k in range(4):
                            last = pe.transpose(bank[6][:, k * T:(k + 1) * T], ov[:, k * P:(k + 1) * P],
                                                ident[0:T, 0:T])
                        last.then_inc(oT_ps, 1)

                    def project(s):
                        pe.wait_ge(oT_ready, ONE + g * GROUP + s + 1)
                        pe.wait_ge(y_done, ONE + g * GROUP + s)
                        for k in range(4):
                            last = pe.matmul(bank[7][0:T, 0:D], oT[:, s % 2, k, :], w.o[:, k, :],
                                             start=(k == 0), stop=(k == 3))
                        last.then_inc(y_ps, 1)

                    scores(0)
                    scores(1)
                    for u in range(UNITS):
                        turn_prob(u)
                        if u + 2 < UNITS:
                            scores(u + 2)
                        values(u)
                        if u % 2 == 1 and u >= 3:
                            turn_out((u - 3) // 2)
                        if u % 2 == 0 and u >= 4:
                            project((u - 4) // 2)
                    project(GROUP - 2)
                    turn_out(GROUP - 1)
                    project(GROUP - 1)

            @block.scalar
            def _(act):
                e.make_rstd_act(act, std_ready, std_asked, e.norm_tmp)
                with act.Fori(0, NG) as g:
                    for k in range(KD):
                        act.wait_ge(xT_ps, ONE + g * 2 + k + 1)
                        act.wait_ge(v_ps, ONE + g * GROUP)
                        act.activation(xnT[:, k, :], bank[k][:, 0:GT], ACT.Copy).then_inc(xT_ready, 1)
                    for m in range(4):
                        act.wait_ge(qk_ps, ONE + g * 8 + 2 * m + 1)
                        act.wait_ge(s_ps, ONE + g * UNITS)
                        act.activation(qT[:, m, :], bank[2][:, 0:GT], ACT.Identity,
                                       bias=w.bq[:, m:m + 1]).then_inc(q_ready, 1)

                    def exp(u):
                        act.wait_ge(shifted, ONE + g * UNITS + u + 1)
                        act.activation(prob[:, u % 2], prob[:, u % 2], ACT.Exp,
                                       scale=HD ** -0.5).then_inc(exp_done, 1)

                    def copy_probT(u):
                        act.wait_ge(pT_ps, ONE + g * UNITS + u + 1)
                        if u >= 2:
                            act.wait_ge(pv_ps, ONE + g * UNITS + u - 1)
                        else:
                            act.wait_ge(pv_ps, ONE + g * UNITS)
                        act.activation(probT[:, u % 2].rearrange("t a b -> t (a b)"), bank[u % 2][0:T, 0:HU * T],
                                       ACT.Copy).then_inc(pT_ready, 1)

                    def copy_oT(s):
                        act.wait_ge(oT_ps, ONE + g * GROUP + s + 1)
                        if s >= 2:
                            act.wait_ge(y_ps, ONE + g * GROUP + s - 1)
                        else:
                            act.wait_ge(y_ps, ONE + g * GROUP)
                        act.activation(oT[:, s % 2].rearrange("p a b -> p (a b)"), bank[6][:, 0:4 * T],
                                       ACT.Copy).then_inc(oT_ready, 1)

                    exp(0)
                    for u in range(UNITS):
                        if u + 1 < UNITS:
                            exp(u + 1)
                        copy_probT(u)
                        if u % 2 == 1 and u >= 3:
                            copy_oT((u - 3) // 2)
                    copy_oT(GROUP - 1)

            @block.vector
            def _(dve):
                chain = Chain(dve, pre)
                e.make_rstd_dve(dve, chain, std_ready, std_asked, mv, rstd[:], e.norm_tmp, False, e.stat6)
                chain(dve.memset(v[:, :, :, HD:HD + 1], 1.0))
                with dve.Fori(0, NG) as g:
                    dve.wait_ge(xT_ps, ONE + g * 2)
                    for s in range(GROUP):
                        b = g * GROUP + s
                        dve.tensor_scalar(xn[:, s, :], x[:, b, :], mv[:, b, 0:1], rstd[:, bass.ds(b, 1)],
                                          ALU.subtract, ALU.mult).then_inc(xn_ready, 1)
                    for m in range(4):
                        dve.wait_ge(qk_ps, ONE + g * 8 + 2 * m + 2)
                        dve.wait_ge(s_ps, ONE + g * UNITS)
                        dve.tensor_scalar(kT[:, m, :], bank[3][:, 0:GT], w.bk[:, m:m + 1], None,
                                          ALU.add).then_inc(k_ready, 1)
                    for s in range(GROUP):
                        dve.wait_ge(v_ps, ONE + g * GROUP + s + 1)
                        dve.wait_ge(pv_ps, ONE + g * UNITS)
                        dve.tensor_copy(v[:, s, :, 0:HD],
                                        bank[s % 2][0:T, :].rearrange("t (h e) -> t h e", e=HD))\
                           .then_inc(v_ready, 1)

                    def shift(u):
                        dve.wait_ge(s_ps, ONE + g * UNITS + u + 1)
                        sc = bank[4 + u % 2][0:T, 0:HU * T].rearrange("t (h k) -> t h k", k=T)
                        dve.tensor_reduce(mx[:, u % 2, :], sc, AX_X, ALU.max).then_inc(mx_done, 1)
                        dve.wait_ge(mx_done, ONE + g * UNITS + u + 1)
                        if u >= 2:
                            dve.wait_ge(pT_ps, ONE + g * UNITS + u - 1)
                        else:
                            dve.wait_ge(pT_ps, ONE + g * UNITS)
                        dve.tensor_tensor(prob[:, u % 2], sc, wide(mx[:, u % 2, :].unsqueeze(2), 2, T),
                                          ALU.subtract).then_inc(shifted, 1)

                    def normalise(u):
                        s = u // 2
                        pv = bank[2 + u % 2][0:T, 0:HU * (HD + 1)].rearrange("t (h e) -> t h e", e=HD + 1)
                        dve.wait_ge(pv_ps, ONE + g * UNITS + u + 1)
                        dve.reciprocal(rinv[:, u % 2, :], pv[:, :, HD]).then_inc(rinv_done, 1)
                        dve.wait_ge(rinv_done, ONE + g * UNITS + u + 1)
                        if s >= 2:
                            dve.wait_ge(oT_ps, ONE + g * GROUP + s - 1)
                        else:
                            dve.wait_ge(oT_ps, ONE + g * GROUP)
                        dve.tensor_tensor(o[:, s % 2, u % 2::2, :], pv[:, :, 0:HD],
                                          wide(rinv[:, u % 2, :].unsqueeze(2), 2, HD), ALU.mult)\
                           .then_inc(o_ready, 1)

                    def keep_y(s):
                        dve.wait_ge(y_ps, ONE + g * GROUP + s + 1)
                        dve.tensor_tensor(y_all[:, g * GROUP + s, :], bank[7][0:T, 0:D], w.bo[:],
                                          ALU.add).then_inc(y_done, 1)
                        dve.wait_ge(y_done, ONE + g * GROUP + s + 1)
                        dve.memset(e.scratch[0:T, s:s + 1], 0.0)
                        dve.bn_stats(y_stat[:, g * GROUP + s, :], y_all[:, g * GROUP + s, :])

                    shift(0)
                    shift(1)
                    for u in range(UNITS):
                        if u + 2 < UNITS:
                            shift(u + 2)
                        normalise(u)
                        if u % 2 == 0 and u >= 4:
                            keep_y((u - 4) // 2)
                    keep_y(GROUP - 2)
                    keep_y(GROUP - 1)

        y_asked, y_std = flag("sa_y_std_asked"), flag("sa_y_std")
        ychain = flag("sa_y_chain")
        loop_chain = flag("sa_fin_chain")
        factors_ready, moved = flag("sa_factors_ready"), count("sa_moved")
        coef = sb("sa_coef", [T, 3, B])
        HALF = 2.0 ** -0.5
        e.start_counts()
        with nc.Block() as block:
            @block.scalar
            def _(act):
                e.make_rstd_act(act, y_std, y_asked, y_tmp)
                act.wait_ge(factors_ready, 1)
                with act.Fori(0, NG) as g:
                    for s in range(GROUP):
                        b = g * GROUP + s
                        one = bass.ds(b, 1)
                        act.activation(y_all[:, b, :], y_all[:, b, :], ACT.Identity, bias=coef[:, 2, one],
                                       scale=y_rstd[:, one]).then_inc(moved, 1)
                        act.activation(x[:, b, :], x[:, b, :], ACT.Identity, bias=coef[:, 1, one],
                                       scale=coef[:, 0, one]).then_inc(moved, 1)

            @block.vector
            def _(dve):
                chain = Chain(dve, ychain)
                e.make_rstd_dve(dve, chain, y_std, y_asked, y_mv, y_rstd[:], y_tmp, False, y_stat)
                chain(dve.scalar_tensor_tensor(out=coef[:, 2, :], in0=y_mv[:, :, 0], scalar=-1.0, in1=y_rstd[:],
                                               op0=ALU.mult, op1=ALU.mult))
                chain(dve.scalar_tensor_tensor(out=coef[:, 1, :], in0=mv[:, :, 0], scalar=-HALF, in1=rstd[:],
                                               op0=ALU.mult, op1=ALU.mult))
                chain(dve.tensor_scalar(coef[:, 0, :], rstd[:], HALF, 1.0, ALU.mult, ALU.add))
                dve.sem_inc(factors_ready, 1)
                chain(dve.tensor_scalar(w.ln_g[:], w.ln_g[:], HALF, None, ALU.mult))
                chain(dve.tensor_scalar(w.ln_b[:], w.ln_b[:], HALF, None, ALU.mult))
                with dve.Fori(0, NG) as g:
                    n = 3
                    link = Chain(dve, loop_chain, g * n, n)
                    yg = y_all[:, bass.ds(g * GROUP, GROUP), :]
                    xg = x[:, bass.ds(g * GROUP, GROUP), :]
                    dve.wait_ge(moved, ONE + g * (2 * GROUP) + 2 * GROUP)
                    link(dve.tensor_tensor(yg, yg, wide(w.ln_g[:].unsqueeze(1), 1, GROUP), ALU.mult))
                    link(dve.tensor_tensor(xg, xg, yg, ALU.add))
                    link(dve.tensor_tensor(xg, xg, wide(w.ln_b[:].unsqueeze(1), 1, GROUP), ALU.add))
                    for s in range(GROUP):
                        e.residual_stats(dve, g * GROUP + s, s)
                    link.close()


def load_context(e, sp, rows, loaded, read):
    with sp.Fori(0, e.B // 2) as i:
        for r in range(2):
            sp.wait_ge(read, ONE + i * 2)
            sp.dma_start(rows[:, r], e.d["ctx_768"][bass.ds(i * 2 + r, 1)].rearrange(
                "b (j p) c -> p (b j) c", p=e.KB)).then_inc(loaded[r], 16)


def context_stats(e, dve, rows, loaded, read):
    with dve.Fori(0, e.B // 2) as i:
        for r in range(2):
            dve.wait_ge(read, ONE + i * 2)
            dve.wait_ge(loaded[r], i * 16 + 16)
            dve.memset(e.scratch[:, r:r + 1], 0.0)
            for j in range(e.NJ):
                last = dve.bn_stats(e.cstat[:, (i * 2 + r) * e.NJ + j, :], rows[:, r, j, :])
            last.then_inc(read, 1)


def cross_attention(e, layer):
    nc, sem, bank, x, mv, rstd, ident, d = e.nc, e.sem, e.bank, e.x, e.mv, e.rstd, e.ident, e.d
    T, D, B, NG, KD, H, HD = e.T, e.D, e.B, e.NG, e.KD, e.XH, e.XD
    KB, NJ, NKV, DC, C1 = e.KB, e.NJ, e.NKV, e.DC, e.C1
    a = e.xa[layer]
    n_ = f"x{layer}_"
    JOB = (bank[0], bank[4])
    SCORE = (bank[5], bank[6])
    ST = (bank[2], bank[3])
    PV, BACK = bank[1], bank[7]
    HU = 4
    NU = GROUP * H // HU
    SU = H // HU
    SS = SU * NJ
    VW = P // HU
    HALF = P // 2
    F32R = mybir.dt.float32r
    with ExitStack() as st:
        def sb(name, shape, dt=F32):
            return st.enter_context(nc.sbuf_tensor(n_ + name, shape, dt))

        def count(name):
            return e.count(n_ + name)

        def flag(name):
            return sem(n_ + name)

        ctxT = sb("ctxT", [P, 2, 2, NKV])
        xn = sb("xn", [T, 2, D])
        xnT = sb("xnT", [P, 2, KD, T])
        q_all = sb("q_all", [P, 2, KD, T])
        q_high = sb("q_high", [P, 2, KD, T], F32R)
        q_low = sb("q_low", [P, 2, KD, T])
        kT = sb("kT", [P, 2, KD, NKV])
        k_high = sb("k_high", [P, 2, KD, NKV], F32R)
        qH = sb("qH", [P, 2, H, T], F32R)
        qL = sb("qL", [HALF, 2, H, T], F32R)
        kS = sb("kS", [P, 2, SU, NKV + 1], F32R)
        v = sb("v", [KB, 2, NJ, H, VW])
        mx = sb("neg_max", [T, 2, HU])
        diag = sb("diag", [T, 2, HU, T], F32R)
        ones = sb("ones", [T, KB], F32R)
        probT = sb("probT", [KB, 3, HU, T])
        o4T = sb("o4T", [P, 2, T])
        rinv = sb("rinv", [T, 2, H])
        o = sb("o", [T, 2, H, HD])
        oT = sb("oT", [P, 2, KD, T])
        y = sb("y", [T, 2, D])
        if layer == 1:
            cnat = sb("cnat", [KB, 2, NJ, DC])
            cmv = sb("cmv", [KB, B * NJ, 2])
            crstd = sb("crstd", [KB, B * NJ])
            ctmp = sb("ctmp", [KB, 3, B * NJ])

        std_asked, std_ready, pre = flag("std_asked"), flag("std_ready"), flag("pre")
        ctx_loaded = [flag("ctx_even"), flag("ctx_odd")]
        cn_ready, cT_ps, cT0_ready, cT1_ready = count("cn_ready"), count("cT_ps"), count("cT0_ready"), count("cT1_ready")
        xn_ready, xT_ps, xT_ready = count("xn_ready"), count("xT_ps"), count("xT_ready")
        q_ps, q_ready = count("q_ps"), count("q_ready")
        k_ps, k0_ready, k1_ready = count("k_ps"), count("k0_ready"), count("k1_ready")
        v_ps, v01_ready, v2_ready = count("v_ps"), count("v01_ready"), count("v2_ready")
        q_cut, qH_ready, qL_ready = count("q_cut"), count("qH_ready"), count("qL_ready")
        kh_ready, kS_high, kS_low = count("k_high_ready"), count("kS_high"), count("kS_low")
        s_ps, max_done, diag_ready = (
            count("scores_ps"), count("max_done"), count("diag_ready"))
        st_ps, exp_done, o4_ready, back_ps = count("exponent_ps"), count("exp_done"), count("o4_ready"), count("back_ps")
        pv_ps, rinv_done, o_ready, o_biased = count("pv_ps"), count("rinv_done"), count("o_ready"), count("o_biased")
        oT_ps, oT_ready, y_ps, y_read = count("oT_ps"), count("oT_ready"), count("y_ps"), count("y_read")
        tail = flag("tail")

        if layer == 1:
            c_asked, c_std, c_chain = flag("c_std_asked"), flag("c_std"), flag("c_chain")
            with nc.Block() as block:
                @block.scalar
                def _(act):
                    e.make_rstd_act(act, c_std, c_asked, ctmp)

                @block.vector
                def _(dve):
                    chain = Chain(dve, c_chain)
                    e.make_rstd_dve(dve, chain, c_std, c_asked, cmv, crstd[:], ctmp, False, e.cstat, DC)

        OUT_AT = 2
        JOBS = 10

        def masks(rows, q):
            at = q % 2 * HU
            return wide(e.head_mask[rows, at:at + HU].unsqueeze(2), 2, T)

        def half_of(q):
            return slice(q % 2 * HALF, (q % 2 + 1) * HALF), q // 2

        def job_at(at):
            j = at - 1 if layer == 1 else at - 2
            return j if 0 <= j < JOBS else None

        def since(g, per_group, n):
            return max(g * per_group + n, 0) if type(g) is int else g * per_group + n

        def all_groups(eng, group):
            group(0, True, False)
            with eng.Fori(1, NG - 1) as g:
                group(g, False, False)
            group(NG - 1, False, True)

        e.start_counts()
        with nc.Block() as block:
            @block.sync
            def _(sp):
                with sp.Fori(0, NG) as g:
                    for s in range(GROUP):
                        b = g * GROUP + s
                        r = s % 2
                        if layer == 0:
                            sp.wait_ge(v_ps, ONE + g * (2 * GROUP) + (2 * (s - 1) if s >= 2 else 0))
                            sp.dma_start(ctxT[:, r, 0, :], d["ctx_T"][0:P, bass.ds(b, 1), :].rearrange(
                                "c b k -> c (b k)")).then_inc(ctx_loaded[r], 16)
                            sp.dma_start(ctxT[0:C1, r, 1, :], d["ctx_T"][P:DC, bass.ds(b, 1), :].rearrange(
                                "c b k -> c (b k)")).then_inc(ctx_loaded[r], 16)
                        else:
                            sp.wait_ge(cT_ps, ONE + g * (2 * GROUP) + (2 * (s - 1) if s >= 2 else 0))
                            sp.dma_start(cnat[:, r], d["ctx_768"][bass.ds(b, 1)].rearrange(
                                "b (j p) c -> p (b j) c", p=KB)).then_inc(ctx_loaded[r], 16)

            @block.tensor
            def _(pe):
                def job(g, s, j):
                    b = g * GROUP + s
                    r = s % 2
                    to = JOB[j % 2]
                    if j in (0, 1) and layer == 1:
                        if j == 0:
                            pe.wait_ge(cn_ready, ONE + b + 1)
                            pe.wait_ge(v01_ready, ONE + b)
                            pe.wait_ge(v2_ready, ONE + b)
                        n = P if j == 0 else C1
                        for c in range(NJ):
                            last = pe.transpose(to[0:n, c * KB:(c + 1) * KB], cnat[:, r, c, j * P:j * P + n],
                                                ident[0:KB, 0:KB])
                        last.then_inc(cT_ps, 1)
                    if j == 2:
                        pe.wait_ge(xn_ready, ONE + b + 1)
                        if layer == 1:
                            pe.wait_ge(cT0_ready, ONE + b + 1)
                        else:
                            pe.wait_ge(v01_ready, ONE + b)
                        for k in range(KD):
                            last = pe.transpose(to[:, k * T:(k + 1) * T], xn[:, r, k * P:(k + 1) * P],
                                                ident[0:T, 0:T])
                        last.then_inc(xT_ps, 1)
                    if j == 3:
                        pe.wait_ge(xT_ready, ONE + b + 1)
                        if layer == 1:
                            pe.wait_ge(cT1_ready, ONE + b + 1)
                        else:
                            pe.wait_ge(v2_ready, ONE + b)
                        for m in range(KD):
                            for k in range(KD):
                                last = pe.matmul(to[:, m * T:(m + 1) * T], a.wq[:, k, m * P:(m + 1) * P],
                                                 xnT[:, r, k, :], start=(k == 0), stop=(k == KD - 1))
                        last.then_inc(q_ps, 1)
                    if j in (4, 5):
                        m = j - 4
                        if j == 4 and layer == 0:
                            pe.wait_ge(ctx_loaded[r], g * (16 * GROUP) + 32 * (s // 2 + 1))
                        if j == 5:
                            pe.wait_ge(q_ready, ONE + b + 1)
                        for k in range(2):
                            n = P if k == 0 else C1
                            last = pe.matmul(to[:, 0:NKV], a.wk[0:n, k, m * P:(m + 1) * P],
                                             ctxT[0:n, r, k, :], start=(k == 0), stop=(k == 1))
                        last.then_inc(k_ps, 1)
                    if j in (6, 7):
                        pe.wait_ge(k0_ready if j == 6 else k1_ready, ONE + b + 1)
                        for c in (range(2) if j == 6 else range(2, NJ)):
                            for k in range(2):
                                n = P if k == 0 else C1
                                at = c % 2 * D
                                last = pe.matmul(to[0:KB, at:at + D], ctxT[0:n, r, k, c * KB:(c + 1) * KB],
                                                 a.wv[0:n, k, :], start=(k == 0), stop=(k == 1))
                        last.then_inc(v_ps, 1)

                def score(g, u, j):
                    s, q = divmod(u, SU)
                    r = s % 2
                    n = u * HU + j
                    if j == 0:
                        for made in (qH_ready, kS_high, kS_low):
                            pe.wait_ge(made, ONE + g * (SU * GROUP) + SU * s + q + 1)
                    pe.wait_ge(max_done, ONE + since(g, NU * HU, n - 1))
                    pe.matmul(SCORE[n % 2][0:T, 0:NKV + 1], qH[:, r, n % H, :], kS[:, r, q, :],
                              start=True, stop=True).then_inc(s_ps, 1)

                def exponent(g, i):
                    u, c = divmod(i, NJ)
                    s, q = divmod(u, SU)
                    r = s % 2
                    if c == 0:
                        pe.wait_ge(qL_ready, ONE + g * (SU * GROUP) + SU * s + q + 1)
                        pe.wait_ge(diag_ready, ONE + g * NU + u + 1)
                    pe.wait_ge(exp_done, ONE + since(g, NU * NJ, i - 1))
                    to = ST[i % 2][0:KB, 0:HU * T]
                    keys = slice(c * KB, (c + 1) * KB)
                    heads = slice(q * HU, (q + 1) * HU)
                    pe.matmul(to, kS[:, r, q, keys], qH[:, r, heads, :].rearrange("p h t -> p (h t)"),
                              start=True, stop=False)
                    pe.matmul(to, kS[0:HALF, r, q, keys], qL[:, r, heads, :].rearrange("p h t -> p (h t)"),
                              start=False, stop=False)
                    pe.matmul(to, ones[:], diag[:, u % 2].rearrange("t h k -> t (h k)"), start=False, stop=True)\
                      .then_inc(st_ps, 1)

                def values(g, i):
                    u, c = divmod(i, NJ)
                    s, q = divmod(u, SU)
                    if i % SS == 0:
                        pe.wait_ge(v01_ready, ONE + g * GROUP + s + 1)
                        pe.wait_ge(v2_ready, ONE + g * GROUP + s + 1)
                    if c == 0:
                        pe.wait_ge(o4_ready, ONE + g * (NU * HU) + u * HU)
                    pe.wait_ge(exp_done, ONE + g * (NU * NJ) + i + 1)
                    pe.matmul(PV[:, 0:HU * T], v[:, s % 2, c, q * HU:(q + 1) * HU, :].rearrange("k h e -> k (h e)"),
                              probT[:, i % 3].rearrange("k h t -> k (h t)"), start=(c == 0), stop=(c == NJ - 1))\
                      .then_inc(pv_ps, 1)

                def turn_back(g, u):
                    s, q = divmod(u, SU)
                    pe.wait_ge(o4_ready, ONE + g * (NU * HU) + (u + 1) * HU)
                    if q == 0:
                        pe.wait_ge(o_ready, ONE + g * GROUP + s)
                    pe.transpose(BACK[0:T, q * P:(q + 1) * P], o4T[:, u % 2, :], ident[:]).then_inc(back_ps, 1)

                def turn_out(g, s):
                    pe.wait_ge(o_biased, ONE + g * GROUP + s + 1)
                    ov = o[:, s % 2].rearrange("t h e -> t (h e)")
                    for k in range(KD):
                        last = pe.transpose(bank[0][:, k * T:(k + 1) * T], ov[:, k * P:(k + 1) * P],
                                            ident[0:T, 0:T])
                    last.then_inc(oT_ps, 1)

                def project(g, s):
                    pe.wait_ge(oT_ready, ONE + g * GROUP + s + 1)
                    for k in range(KD):
                        last = pe.matmul(bank[4][0:T, 0:D], oT[:, s % 2, k, :], a.wo[:, k, :],
                                         start=(k == 0), stop=(k == KD - 1))
                    last.then_inc(y_ps, 1)

                def group(g, is_first, last):
                    for i in range(NU * NJ):
                        u, c = divmod(i, NJ)
                        s, at = divmod(i, SS)
                        ahead = u + 1 < NU or not last
                        exponent(g, i)
                        if c < 2 and ahead:
                            score(g, u + 1, 2 * c)
                        if c == 1 and (u > 0 or not is_first):
                            turn_back(g, u - 1)
                        if i > 0 or not is_first:
                            values(g, i - 1)
                        if c < 2 and ahead:
                            score(g, u + 1, 2 * c + 1)
                        if layer == 0 and at == OUT_AT and (s >= 1 or not is_first):
                            pe.wait_ge(v01_ready, ONE + g * GROUP + s + 1)
                            turn_out(g, s - 1)
                        if layer == 0 and at == OUT_AT + 1 and (s >= 1 or not is_first):
                            pe.wait_ge(v2_ready, ONE + g * GROUP + s + 1)
                            project(g, s - 1)
                        j = job_at(at)
                        if (s < GROUP - 1 or not last) and j is not None:
                            if layer == 0 and (s >= 1 or not is_first) and j == 2:
                                pe.wait_ge(oT_ready, ONE + g * GROUP + s)
                                pe.wait_ge(y_read, ONE + g * GROUP + s)
                            job(g, s + 1, j)
                    if last:
                        values(g, NU * NJ - 1)
                        turn_back(g, NU - 1)
                        if layer == 0:
                            turn_out(g, GROUP - 1)
                            project(g, GROUP - 1)

                for j in range(JOBS):
                    job(0, 0, j)
                for j in range(HU):
                    score(0, 0, j)
                all_groups(pe, group)

            @block.scalar
            def _(act):
                e.make_rstd_act(act, std_ready, std_asked, e.norm_tmp)

                def copies(g, s, j):
                    b = g * GROUP + s
                    r = s % 2
                    if j == 0 and layer == 1:
                        act.wait_ge(cT_ps, ONE + g * (2 * GROUP) + 2 * s + 1)
                        act.wait_ge(v_ps, ONE + since(g, 2 * GROUP, 2 * (s - 1)))
                        act.activation(ctxT[:, r, 0, :], JOB[0][:, 0:NKV], ACT.Copy).then_inc(cT0_ready, 1)
                    if j == 2:
                        act.wait_ge(xT_ps, ONE + b + 1)
                        act.activation(xnT[:, r].rearrange("p k t -> p (k t)"), JOB[0][:, 0:KD * T],
                                       ACT.Copy).then_inc(xT_ready, 1)
                    if j == 4:
                        act.wait_ge(k_ps, ONE + g * (2 * GROUP) + 2 * s + 1)
                        act.wait_ge(st_ps, ONE + since(g, NU * NJ, SS * (s - 1)))
                        act.activation(kT[:, r, 0, :], JOB[0][:, 0:NKV], ACT.Identity,
                                       bias=a.bk[:, 0:1]).then_inc(k0_ready, 1)
                    if j == 6:
                        act.wait_ge(k0_ready, ONE + b + 1)
                        act.wait_ge(k1_ready, ONE + b + 1)
                        act.activation(k_high[:, r].rearrange("p k t -> p (k t)"),
                                       kT[:, r].rearrange("p k t -> p (k t)"), ACT.Copy).then_inc(kh_ready, 1)
                        act.wait_ge(kh_ready, ONE + b + 1)
                    if j >= 6:
                        rows, tile = half_of(j - 6)
                        act.activation(kS[0:HALF, r, j - 6, 0:NKV], k_high[rows, r, tile, :], ACT.Copy)\
                           .then_inc(kS_high, 1)
                    if j == 6:
                        act.wait_ge(v_ps, ONE + g * (2 * GROUP) + 2 * s + 1)
                        act.wait_ge(pv_ps, ONE + since(g, NU * NJ, SS * (s - 1)))
                        act.activation(v[:, r, 0:2, :, 0:HD],
                                       JOB[0][0:KB, :].rearrange("p (c h e) -> p c h e", c=2, e=HD),
                                       ACT.Copy).then_inc(v01_ready, 1)

                def exp(g, i):
                    act.wait_ge(st_ps, ONE + g * (NU * NJ) + i + 1)
                    act.wait_ge(pv_ps, ONE + since(g, NU * NJ, i - 2))
                    act.activation(probT[:, i % 3].rearrange("k h t -> k (h t)"), ST[i % 2][0:KB, 0:HU * T],
                                   ACT.Exp).then_inc(exp_done, 1)

                def copy_o4(g, u):
                    act.wait_ge(pv_ps, ONE + g * (NU * NJ) + NJ * (u + 1))
                    act.wait_ge(back_ps, ONE + since(g, NU, u - 1))
                    for j in range(HU):
                        rows = slice(j * VW, (j + 1) * VW)
                        act.activation(o4T[rows, u % 2, :], PV[rows, j * T:(j + 1) * T], ACT.Copy)\
                           .then_inc(o4_ready, 1)

                def copy_oT(g, s):
                    act.wait_ge(oT_ps, ONE + g * GROUP + s + 1)
                    act.wait_ge(y_ps, ONE + since(g, GROUP, s - 1))
                    act.activation(oT[:, s % 2].rearrange("p k t -> p (k t)"), bank[0][:, 0:KD * T],
                                   ACT.Copy).then_inc(oT_ready, 1)

                def group(g, is_first, last):
                    for i in range(NU * NJ):
                        s, at = divmod(i, SS)
                        exp(g, i)
                        if i % NJ == 0 and (i > 0 or not is_first):
                            copy_o4(g, i // NJ - 1)
                        if layer == 0 and at == OUT_AT and (s >= 1 or not is_first):
                            copy_oT(g, s - 1)
                        j = job_at(at)
                        if (s < GROUP - 1 or not last) and j is not None:
                            copies(g, s + 1, j)
                    if last:
                        copy_o4(g, NU - 1)
                    if last and layer == 0:
                        copy_oT(g, GROUP - 1)

                for j in range(JOBS):
                    copies(0, 0, j)
                all_groups(act, group)

            @block.gpsimd
            def _(pool):
                def mask_low(g, s):
                    r = s % 2
                    for q in range(SU):
                        rows, tile = half_of(q)
                        pool.wait_ge(q_cut, ONE + g * (2 * GROUP) + 2 * s + 2)
                        pool.wait_ge(st_ps, ONE + since(g, NU * NJ, SS * (s - 1)))
                        pool.tensor_tensor(qL[:, r, q * HU:(q + 1) * HU, :], wide(q_low[rows, r, tile:tile + 1, :], 1, HU),
                                           masks(rows, q), ALU.mult).then_inc(qL_ready, 1)

                def group(g, is_first, last):
                    for s in range(GROUP - 1 if last else GROUP):
                        mask_low(g, s + 1)

                mask_low(0, 0)
                all_groups(pool, group)

            @block.vector
            def _(dve):
                chain = Chain(dve, pre)
                e.make_rstd_dve(dve, chain, std_ready, std_asked, mv, rstd[:], e.norm_tmp, layer == 1, e.stat6)
                chain(dve.memset(v[:, :, :, :, HD:VW], 0.0))
                chain(dve.memset(v[:, :, :, :, HD:HD + 1], 1.0))
                chain(dve.tensor_scalar(kS[:, :, :, NKV], ident[:, 0:2 * SU].rearrange("p (r k) -> p r k", k=SU),
                                        0.0, None, ALU.mult))
                chain(dve.tensor_scalar(ones[:], ident[0:T, 0:KB], 0.0, 1.0, ALU.mult, ALU.add))

                def norm_context(g, s):
                    b = g * GROUP + s
                    r = s % 2
                    dve.wait_ge(ctx_loaded[r], g * (8 * GROUP) + 16 * (s // 2 + 1))
                    for c in range(NJ):
                        row = b * NJ + c
                        last = dve.tensor_scalar(cnat[:, r, c, :], cnat[:, r, c, :], cmv[:, row, 0:1],
                                                 crstd[:, bass.ds(row, 1)], ALU.subtract, ALU.mult)
                    last.then_inc(cn_ready, 1)

                def copies(g, s, j):
                    b = g * GROUP + s
                    r = s % 2
                    if j == 1:
                        dve.wait_ge(xT_ps, ONE + since(g, GROUP, s - 1))
                        dve.tensor_scalar(xn[:, r, :], x[:, b, :], mv[:, b, 0:1], rstd[:, bass.ds(b, 1)],
                                          ALU.subtract, ALU.mult).then_inc(xn_ready, 1)
                        if layer == 1:
                            dve.wait_ge(cT_ps, ONE + g * (2 * GROUP) + 2 * s + 2)
                            dve.wait_ge(v_ps, ONE + since(g, 2 * GROUP, 2 * (s - 1)))
                            dve.tensor_copy(ctxT[0:C1, r, 1, :], JOB[1][0:C1, 0:NKV]).then_inc(cT1_ready, 1)
                    if j == 3:
                        dve.wait_ge(q_ps, ONE + b + 1)
                        dve.wait_ge(st_ps, ONE + since(g, NU * NJ, SS * (s - 1)))
                        for m in range(KD):
                            last = dve.tensor_scalar(q_all[:, r, m, :], JOB[1][:, m * T:(m + 1) * T],
                                                     a.bq[:, 0, m:m + 1], None, ALU.add)
                        last.then_inc(q_ready, 1)
                        dve.wait_ge(q_ready, ONE + b + 1)
                        dve.tensor_copy(q_high[:, r], q_all[:, r]).then_inc(q_cut, 1)
                        dve.wait_ge(q_cut, ONE + g * (2 * GROUP) + 2 * s + 1)
                        dve.tensor_tensor(q_low[:, r], q_all[:, r], q_high[:, r], ALU.subtract).then_inc(q_cut, 1)
                    if 3 <= j < 3 + SU:
                        rows, tile = half_of(j - 3)
                        for half in range(2):
                            last = dve.tensor_tensor(
                                qH[half * HALF:(half + 1) * HALF, r, (j - 3) * HU:(j - 2) * HU, :],
                                wide(q_high[rows, r, tile:tile + 1, :], 1, HU), masks(rows, j - 3), ALU.mult)
                        last.then_inc(qH_ready, 1)
                    if j == 5:
                        dve.wait_ge(k_ps, ONE + g * (2 * GROUP) + 2 * s + 2)
                        dve.wait_ge(st_ps, ONE + since(g, NU * NJ, SS * (s - 1)))
                        dve.tensor_scalar(kT[:, r, 1, :], JOB[1][:, 0:NKV], a.bk[:, 1:2], None,
                                          ALU.add).then_inc(k1_ready, 1)
                    if j >= 6:
                        rows, tile = half_of(j - 6)
                        dve.wait_ge(kh_ready, ONE + b + 1)
                        dve.tensor_tensor(kS[HALF:P, r, j - 6, 0:NKV], kT[rows, r, tile, :],
                                          k_high[rows, r, tile, :], ALU.subtract).then_inc(kS_low, 1)
                    if j == 7:
                        dve.wait_ge(v_ps, ONE + g * (2 * GROUP) + 2 * s + 2)
                        dve.wait_ge(pv_ps, ONE + since(g, NU * NJ, SS * (s - 1)))
                        dve.tensor_copy(v[:, r, 2, :, 0:HD],
                                        JOB[1][0:KB, 0:D].rearrange("p (h e) -> p h e", e=HD))\
                           .then_inc(v2_ready, 1)

                def neg_max(g, u, j):
                    n = u * HU + j
                    dve.wait_ge(s_ps, ONE + g * (NU * HU) + n + 1)
                    dve.tensor_reduce(mx[:, u % 2, j:j + 1], SCORE[n % 2][0:T, 0:NKV], AX_X, ALU.max,
                                      negate=True).then_inc(max_done, 1)

                def make_diag(g, u):
                    dve.wait_ge(max_done, ONE + g * (NU * HU) + (u + 1) * HU)
                    dve.wait_ge(st_ps, ONE + since(g, NU * NJ, NJ * (u - 1)))
                    dve.tensor_tensor(diag[:, u % 2], wide(ident[0:T, 0:T].unsqueeze(1), 1, HU),
                                      wide(mx[:, u % 2, :].unsqueeze(2), 2, T), ALU.mult).then_inc(diag_ready, 1)

                def normalise(g, s, link):
                    b = g * GROUP + s
                    pv = BACK[0:T, :].rearrange("t (h e) -> t h e", e=VW)
                    dve.wait_ge(back_ps, ONE + g * NU + SU * (s + 1))
                    dve.reciprocal(rinv[:, s % 2, :], pv[:, :, HD]).then_inc(rinv_done, 1)
                    dve.wait_ge(rinv_done, ONE + b + 1)
                    if layer == 0:
                        dve.wait_ge(oT_ps, ONE + since(g, GROUP, s - 1))
                    dve.tensor_tensor(o[:, s % 2], pv[:, :, 0:HD], wide(rinv[:, s % 2, :].unsqueeze(2), 2, HD),
                                      ALU.mult).then_inc(o_ready, 1)
                    dve.wait_ge(o_ready, ONE + b + 1)
                    ov = o[:, s % 2].rearrange("t h e -> t (h e)")
                    dve.tensor_tensor(ov, ov, a.bv[0:T, :], ALU.add).then_inc(o_biased, 1)
                    if layer == 1:
                        dve.wait_ge(o_biased, ONE + b + 1)
                        link(dve.tensor_tensor(x[:, b, :], x[:, b, :], ov, ALU.add))
                        e.residual_stats(dve, b, s % GROUP)

                def add_y(g, s, link):
                    b = g * GROUP + s
                    dve.wait_ge(y_ps, ONE + b + 1)
                    dve.tensor_tensor(y[:, s % 2, :], bank[4][0:T, 0:D], a.bo[:], ALU.add).then_inc(y_read, 1)
                    dve.wait_ge(y_read, ONE + b + 1)
                    link(dve.tensor_tensor(x[:, b, :], x[:, b, :], y[:, s % 2, :], ALU.add))
                    e.residual_stats(dve, b, s % GROUP)

                def group(g, is_first, last):
                    link = Chain(dve, tail, g * GROUP - (0 if is_first else 1), GROUP - is_first + last)
                    for i in range(NU * NJ):
                        u, c = divmod(i, NJ)
                        s, at = divmod(i, SS)
                        more = s < GROUP - 1 or not last
                        if layer == 1 and at == 0 and more:
                            norm_context(g, s + 1)
                        if c < 2 and (u + 1 < NU or not last):
                            neg_max(g, u + 1, 2 * c)
                            neg_max(g, u + 1, 2 * c + 1)
                            if c == 1:
                                make_diag(g, u + 1)
                        if at == 1 and (s >= 1 or not is_first):
                            normalise(g, s - 1, link)
                        if layer == 0 and at == OUT_AT + 1 and (s >= 1 or not is_first):
                            add_y(g, s - 1, link)
                        j = job_at(at)
                        if more and j is not None:
                            copies(g, s + 1, j)
                    if last:
                        normalise(g, GROUP - 1, link)
                    if last and layer == 0:
                        add_y(g, GROUP - 1, link)
                    link.close()

                if layer == 1:
                    norm_context(0, 0)
                for j in range(JOBS):
                    copies(0, 0, j)
                for j in range(HU):
                    neg_max(0, 0, j)
                make_diag(0, 0)
                all_groups(dve, group)


def experts(e, layer):
    nc, sem, bank, x, mv, rstd, ident, d = e.nc, e.sem, e.bank, e.x, e.mv, e.rstd, e.ident, e.d
    T, D, B, NG, GT, KD, E = e.T, e.D, e.B, e.NG, e.GT, e.KD, e.E
    n_ = f"f{layer}_"
    w1_d, w2_d = d[f"L{layer}_ffn_w1"], d[f"L{layer}_ffn_w2"]
    FF = w1_d.shape[2]
    NF = FF // P
    BIG = 3.0e38
    SLOTS = e.SLOTS
    NS = SLOTS // P
    NT = e.NT
    STEPS = -(-B * T // SLOTS)
    NI = max(NT, STEPS, E)
    with ExitStack() as st:
        def sb(name, shape, dt=F32):
            return st.enter_context(nc.sbuf_tensor(n_ + name, shape, dt))

        def count(name, start=ONE):
            return e.count(n_ + name, start)

        def flag(name):
            return sem(n_ + name)

        xn = sb("xn", [T, B, D])
        where = sb("where", [T, 2, B], mybir.dt.uint32)
        share = sb("share", [T, 2, B])
        owner = sb("owner", [1, NT], mybir.dt.int32)

        gate_loads, std_asked, std_ready, pre = flag("gate_loads"), flag("std_asked"), flag("std_ready"), flag("pre")
        xn_ready, xT_ps, xT_ready = count("xn_ready"), count("xT_ps"), count("xT_ready")
        logit_ps, logit_read = count("logit_ps"), count("logit_read")
        kept = count("kept")
        const_made, exp_asked, exp_done = flag("const_made"), flag("exp_asked"), flag("exp_done")
        top_chain, chosen, rank_ps = flag("top_chain"), flag("chosen"), flag("rank_ps")
        cleared = flag("cleared")

        with ExitStack() as inner:
            def tmp(name, shape, dt=F32):
                return inner.enter_context(nc.sbuf_tensor(n_ + name, shape, dt))

            xTg = tmp("xTg", [P, KD, GT])
            xnG = tmp("xnG", [T, GROUP, D])
            gw = tmp("gate_w", [P, KD, E])
            gb = tmp("gate_b", [T, E])
            logit = tmp("logit", [T, B, E])
            iota_i = tmp("iota_i", [T, NI], mybir.dt.int32)
            iota = tmp("iota", [T, NI])
            before = tmp("before", [T, T])
            ones = tmp("ones", [T, T])
            t0, one1, one2 = tmp("t0", [T, B, E]), tmp("one1", [T, B, E]), tmp("one2", [T, B, E])
            both = tmp("both", [T, B, E])
            num = tmp("num", [T, B, E])
            run = tmp("run", [T, 2, B, E])
            top = tmp("top", [T, 6, B])
            steps = tmp("steps", [T, E, STEPS])
            tiles = tmp("tiles", [T, E])
            tend = tmp("tend", [T, 2, E])
            own = tmp("own", [1, NT, E])
            own1 = tmp("own1", [1, NT])
            zero = tmp("zero", [P, 7 * D]) if layer == 0 else None
            with_bias = layer == 0
            gate_dmas = 2 if with_bias else 1

            e.start_counts()
            with nc.Block() as block:
                @block.sync
                def _(sp):
                    gate = d["L0_ffn_gate_w"] if layer == 0 else d["router_T"]
                    with nc.allow_non_contiguous_dma(reason="eight columns of the gate"):
                        sp.dma_start(gw[:], gate.rearrange("(k p) n -> p k n", p=P)).then_inc(gate_loads, 16)
                    if with_bias:
                        sp.dma_start(gb[:], d["L0_ffn_gate_b"].partition_broadcast(T)).then_inc(gate_loads, 16)
                    if layer == 0:
                        sp.wait_ge(const_made, 5)
                        rows_ = e.slot_x.rearrange("(p r) c -> p (r c)", p=P)
                        width = NT * NS * D
                        n = 0
                        for at in range(0, width, 7 * D):
                            w_ = min(7 * D, width - at)
                            sp.dma_start(rows_[:, at:at + w_], zero[:, 0:w_]).then_inc(cleared, 16)
                            n += 1
                        sp.wait_ge(cleared, 16 * n)

                @block.gpsimd
                def _(pool):
                    made = Chain(pool, const_made)
                    made(pool.iota(iota_i[:], pattern=[[1, NI]], base=0, channel_multiplier=0))
                    made(pool.memset(ones[:], 1.0))
                    made(pool.memset(before[:], 1.0))
                    made(pool.affine_select(out=before[:], in_=before[:], compare_op=ALU.is_gt, fill=0.0,
                                            base=0, pattern=[[1, T]], channel_multiplier=-1))
                    if layer == 0:
                        made(pool.memset(zero[:], 0.0))

                @block.tensor
                def _(pe):
                    pe.wait_ge(gate_loads, 16 * gate_dmas)
                    with pe.Fori(0, NG) as g:
                        pe.wait_ge(xn_ready, ONE + g * GROUP + GROUP)
                        pe.wait_ge(logit_read, ONE + g)
                        for k in range(KD):
                            for s in range(GROUP):
                                last = pe.transpose(bank[k][:, s * T:(s + 1) * T], xnG[:, s, k * P:(k + 1) * P],
                                                    ident[0:T, 0:T])
                            last.then_inc(xT_ps, 1)
                        pe.wait_ge(xT_ready, ONE + g * 2 + 2)
                        for s in range(GROUP):
                            for k in range(KD):
                                last = pe.matmul(bank[2][0:T, s * E:(s + 1) * E], xTg[:, k, s * T:(s + 1) * T],
                                                 gw[:, k, :], start=(k == 0), stop=(k == KD - 1))
                        last.then_inc(logit_ps, 1)
                    pe.wait_ge(chosen, 1)
                    pe.wait_ge(const_made, 4)
                    marks = both[:].rearrange("t b n -> t (b n)")
                    pe.matmul(bank[3][0:T, 0:B * E], before[:], marks, start=True, stop=True)
                    pe.matmul(bank[4][0:T, 0:B * E], ones[:], marks, start=True, stop=True).then_inc(rank_ps, 1)

                @block.scalar
                def _(act):
                    e.make_rstd_act(act, std_ready, std_asked, e.norm_tmp)
                    with act.Fori(0, NG) as g:
                        for k in range(KD):
                            act.wait_ge(xT_ps, ONE + g * 2 + k + 1)
                            act.wait_ge(logit_ps, ONE + g)
                            act.activation(xTg[:, k, :], bank[k][:, 0:GT], ACT.Copy).then_inc(xT_ready, 1)
                    act.wait_ge(exp_asked, 1)
                    act.activation(top[:, 2, :], top[:, 2, :], ACT.Exp).then_inc(exp_done, 1)

                @block.vector
                def _(dve):
                    chain = Chain(dve, pre)
                    e.make_rstd_dve(dve, chain, std_ready, std_asked, mv, rstd[:], e.norm_tmp, False, e.stat6)
                    dve.wait_ge(gate_loads, 16 * gate_dmas)
                    with dve.Fori(0, NG) as g:
                        dve.wait_ge(xT_ps, ONE + g * 2)
                        dve.wait_ge(kept, ONE + g)
                        for s in range(GROUP):
                            b = g * GROUP + s
                            dve.tensor_scalar(xnG[:, s, :], x[:, b, :], mv[:, b, 0:1], rstd[:, bass.ds(b, 1)],
                                              ALU.subtract, ALU.mult).then_inc(xn_ready, 1)
                        dve.wait_ge(xn_ready, ONE + g * GROUP + GROUP)
                        dve.tensor_scalar(xn[:, bass.ds(g * GROUP, GROUP), :], xnG[:], 1.0, None,
                                          ALU.mult).then_inc(kept, 1)
                        dve.wait_ge(logit_ps, ONE + g + 1)
                        lg = logit[:, bass.ds(g * GROUP, GROUP), :]
                        ps = bank[2][0:T, 0:GROUP * E].rearrange("t (s n) -> t s n", n=E)
                        if with_bias:
                            dve.tensor_tensor(lg, ps, wide(gb[:].unsqueeze(1), 1, GROUP), ALU.add)\
                               .then_inc(logit_read, 1)
                        else:
                            dve.tensor_copy(lg, ps).then_inc(logit_read, 1)
                    dve.wait_ge(logit_read, ONE + NG)
                    dve.wait_ge(const_made, 4)
                    link = Chain(dve, top_chain)
                    link(dve.tensor_copy(iota[:], iota_i[:]))
                    iw = wide(iota[:, 0:E].unsqueeze(1), 1, B)

                    def over_experts(row):
                        return wide(top[:, row, :].unsqueeze(2), 2, E)

                    def first_of_max(values, value, index, onehot):
                        link(dve.tensor_reduce(top[:, value, :], values, AX_X, ALU.max))
                        link(dve.tensor_tensor(t0[:], values, over_experts(value), ALU.is_equal))
                        link(dve.tensor_scalar(t0[:], t0[:], -float(E), float(E), ALU.mult, ALU.add))
                        link(dve.tensor_tensor(t0[:], t0[:], iw, ALU.add))
                        link(dve.tensor_reduce(top[:, index, :], t0[:], AX_X, ALU.min))
                        link(dve.tensor_tensor(onehot[:], iw, over_experts(index), ALU.is_equal))

                    first_of_max(logit[:], 0, 1, one1)
                    link(dve.scalar_tensor_tensor(out=logit[:], in0=one1[:], scalar=-BIG, in1=logit[:],
                                                  op0=ALU.mult, op1=ALU.add))
                    first_of_max(logit[:], 3, 4, one2)
                    link(dve.tensor_tensor(both[:], one1[:], one2[:], ALU.add))
                    dve.sem_inc(chosen, 1)
                    link(dve.tensor_tensor(top[:, 2, :], top[:, 3, :], top[:, 0, :], ALU.subtract))
                    dve.sem_inc(exp_asked, 1)
                    dve.wait_ge(exp_done, 1)
                    link(dve.tensor_scalar(top[:, 5, :], top[:, 2, :], 1.0, None, ALU.add))
                    link(dve.reciprocal(share[:, 0, :], top[:, 5, :]))
                    link(dve.tensor_tensor(share[:, 1, :], share[:, 0, :], top[:, 2, :], ALU.mult))

                    dve.wait_ge(rank_ps, 1)
                    link(dve.tensor_copy(num[:].rearrange("t b n -> t (b n)"), bank[4][0:T, 0:B * E]))
                    link(dve.tensor_copy(run[:, 0], num[:]))
                    at, step = 0, 1
                    while step < B:
                        link(dve.tensor_tensor(run[:, 1 - at, step:B], run[:, at, step:B], run[:, at, 0:B - step],
                                               ALU.add))
                        link(dve.tensor_copy(run[:, 1 - at, 0:step], run[:, at, 0:step]))
                        at, step = 1 - at, 2 * step
                    link(dve.tensor_scalar(steps[:], wide(iota[:, 0:STEPS].unsqueeze(1), 1, E), float(SLOTS), None,
                                           ALU.mult))
                    link(dve.tensor_tensor(steps[:], wide(run[:, at, B - 1, :].unsqueeze(2), 2, STEPS), steps[:],
                                           ALU.is_gt))
                    link(dve.tensor_reduce(tiles[:], steps[:], AX_X, ALU.add))
                    link(dve.tensor_copy(tend[:, 0], tiles[:]))
                    to, step = 0, 1
                    while step < E:
                        link(dve.tensor_tensor(tend[:, 1 - to, step:E], tend[:, to, step:E],
                                               tend[:, to, 0:E - step], ALU.add))
                        link(dve.tensor_copy(tend[:, 1 - to, 0:step], tend[:, to, 0:step]))
                        to, step = 1 - to, 2 * step
                    link(dve.tensor_tensor(own[:], wide(iota[0:1, 0:NT].unsqueeze(2), 2, E),
                                           wide(tend[0:1, to, :].unsqueeze(1), 1, NT), ALU.is_ge))
                    link(dve.tensor_reduce(own1[:], own[:], AX_X, ALU.add))
                    link(dve.tensor_scalar(own1[:], own1[:], float(E - 1), None, ALU.min))
                    link(dve.tensor_copy(owner[:], own1[:]))
                    link(dve.tensor_tensor(tiles[:], tend[:, to], tiles[:], ALU.subtract))
                    link(dve.tensor_scalar(tiles[:], tiles[:], float(SLOTS), None, ALU.mult))
                    link(dve.tensor_tensor(num[:], run[:, at], num[:], ALU.subtract))
                    link(dve.tensor_tensor(num[:], num[:], wide(tiles[:].unsqueeze(1), 1, B), ALU.add))
                    nf = num[:].rearrange("t b n -> t (b n)")
                    link(dve.tensor_tensor(nf, nf, bank[3][0:T, 0:B * E], ALU.add))
                    for c, onehot in enumerate((one1, one2)):
                        link(dve.tensor_tensor(t0[:], num[:], onehot[:], ALU.mult))
                        link(dve.tensor_reduce(top[:, c, :], t0[:], AX_X, ALU.add))
                        link(dve.tensor_copy(where[:, c, :], top[:, c, :]))

        x_slots = sb("x_slots", [P, 2, NS, D])
        xT = sb("xT", [P, 2, KD, SLOTS])
        w1 = sb("w1", [P, 2, KD, FF])
        w2 = sb("w2", [P, 2, NF, D])
        b1 = sb("b1", [P, 2, NF])
        b2 = sb("b2", [P, 2, D])
        hT = sb("hT", [P, NF, SLOTS])
        y = sb("y", [P, 2, NS, D])

        scattered = flag("scattered")
        w_loaded = [flag("w_even"), flag("w_odd")]
        x_loaded = [flag("x_even"), flag("x_odd")]
        y_stored, y_free = flag("y_stored"), count("y_free", TWO)
        turned, y_ready = count("turned", TWO), count("y_ready", TWO)
        xT_copied = count("xT_copied")
        up_ps, h_raw, h_ready = count("up_ps"), count("h_raw"), count("h_ready")
        down_ps = count("down_ps")
        W_DMAS = 4 if layer == 0 else 2
        if layer == 0:
            ctx_rows = sb("ctx_rows", [e.KB, 2, e.NJ, e.DC])
            ctx_loaded, ctx_read = [flag("ctx_even"), flag("ctx_odd")], count("ctx_read")
        e.start_counts()

        def all_tiles(eng, tile):
            with eng.Fori(0, (NT - 1) // 2) as i:
                for r in range(2):
                    tile(i * 2 + r, i, r)
            for n in range((NT - 1) // 2 * 2, NT):
                tile(n, n // 2, n % 2)

        def after(n, i, r):
            return None if type(n) is int and n + 1 == NT else (n + 1, i + r, 1 - r)

        with nc.Block() as block:
            @block.gpsimd
            def _(pool):
                for b in range(B):
                    for c in range(2):
                        pool.indirect_dma_start(
                            out=e.slot_x, out_offset=bass.IndirectOffsetOnAxis(ap=where[:, c, b:b + 1], axis=0),
                            in_=xn[:, b, :], in_offset=None).then_inc(scattered, 16)
                pool.wait_ge(scattered, 16 * 2 * B)

                def tile(n, i, r):
                    pool.wait_ge(y_ready, TWO + n + 1)
                    pool.dma_start(e.slot_y[bass.ds(n * SLOTS, SLOTS), :].rearrange("(j p) c -> p j c", p=P),
                                   y[:, r]).then_inc(y_stored, 16)
                    pool.wait_ge(y_stored, n * 16 + 16)
                    pool.sem_inc(y_free, 1)

                all_tiles(pool, tile)

            @block.sync
            def _(sp):
                def weights(n, i, r):
                    sp.wait_ge(y_ready, TWO + n - 1)
                    expert = sp.value_load(owner[0:1, bass.ds(n, 1)], min_val=0, max_val=E - 1)
                    one = bass.ds(expert, 1)
                    sp.dma_start(w1[:, r], w1_d[one].rearrange("o (k p) f -> p (o k) f", p=P))\
                      .then_inc(w_loaded[r], 16)
                    sp.dma_start(w2[:, r], w2_d[one].rearrange("o (k p) n -> p (o k) n", p=P))\
                      .then_inc(w_loaded[r], 16)
                    if layer == 0:
                        sp.dma_start(b1[:, r], d["L0_b1_cols"][one].rearrange("o p f -> p (o f)"))\
                          .then_inc(w_loaded[r], 16)
                        sp.dma_start(b2[:, r], wide(d["L0_ffn_b2"][one], 0, P)).then_inc(w_loaded[r], 16)

                def rows_in(n, i, r):
                    sp.wait_ge(turned, TWO + n - 1)
                    sp.dma_start(x_slots[:, r], e.slot_x[bass.ds(n * SLOTS, SLOTS), :].rearrange(
                        "(j p) c -> p j c", p=P)).then_inc(x_loaded[r], 16)

                def tile(n, i, r):
                    if after(n, i, r):
                        rows_in(*after(n, i, r))
                        weights(*after(n, i, r))

                if layer == 0:
                    load_context(e, sp, ctx_rows, ctx_loaded, ctx_read)
                weights(0, 0, 0)
                sp.wait_ge(scattered, 16 * 2 * B)
                rows_in(0, 0, 0)
                all_tiles(sp, tile)

            @block.tensor
            def _(pe):
                def turn(n, i, r):
                    pe.wait_ge(x_loaded[r], i * 16 + 16)
                    pe.wait_ge(xT_copied, ONE + n)
                    for k in range(KD):
                        for j in range(NS):
                            at = (k * NS + j) * P
                            last = pe.transpose(bank[0][:, at:at + P], x_slots[:, r, j, k * P:(k + 1) * P],
                                                ident[:])
                    last.then_inc(turned, 1)

                def tile(n, i, r):
                    pe.wait_ge(w_loaded[r], (i + 1) * (16 * W_DMAS))
                    pe.wait_ge(xT_copied, ONE + n + 1)
                    for f in range(NF):
                        pe.wait_ge(h_raw, ONE + n * NF + (f - 2 if f >= 3 else 0))
                        for k in range(KD):
                            last = pe.matmul(bank[1 + f % 3][:, 0:SLOTS], w1[:, r, k, f * P:(f + 1) * P],
                                             xT[:, r, k, :], start=(k == 0), stop=(k == KD - 1))
                        last.then_inc(up_ps, 1)
                    if after(n, i, r):
                        turn(*after(n, i, r))
                    pe.wait_ge(y_ready, TWO + n - 1)
                    for j in range(NS):
                        for f in range(NF):
                            if j == 0:
                                pe.wait_ge(h_raw if layer == 0 else h_ready, ONE + n * NF + f + 1)
                            last = pe.matmul(bank[4 + 2 * r + j][:, 0:D], hT[:, f, j * P:(j + 1) * P],
                                             w2[:, r, f, :], start=(f == 0), stop=(f == NF - 1))
                    last.then_inc(down_ps, 1)

                turn(0, 0, 0)
                all_tiles(pe, tile)

            @block.scalar
            def _(act):
                def copy_xT(n, i, r):
                    act.wait_ge(turned, TWO + n + 1)
                    act.activation(xT[:, r].rearrange("p k s -> p (k s)"), bank[0][:, 0:KD * SLOTS],
                                   ACT.Copy).then_inc(xT_copied, 1)

                def tile(n, i, r):
                    for f in range(NF):
                        act.wait_ge(up_ps, ONE + n * NF + f + 1)
                        act.wait_ge(down_ps, ONE + n)
                        if layer == 0:
                            act.activation(hT[:, f, :], bank[1 + f % 3][:, 0:SLOTS], ACT.Gelu,
                                           bias=b1[:, r, f:f + 1]).then_inc(h_raw, 1)
                        else:
                            act.activation(hT[:, f, :], bank[1 + f % 3][:, 0:SLOTS], ACT.Relu).then_inc(h_raw, 1)
                    if after(n, i, r):
                        copy_xT(*after(n, i, r))

                copy_xT(0, 0, 0)
                all_tiles(act, tile)

            @block.vector
            def _(dve):
                def tile(n, i, r):
                    if layer == 1:
                        for f in range(NF):
                            dve.wait_ge(h_raw, ONE + n * NF + f + 1)
                            dve.tensor_tensor(hT[:, f, :], hT[:, f, :], hT[:, f, :], ALU.mult)\
                               .then_inc(h_ready, 1)
                    dve.wait_ge(down_ps, ONE + n + 1)
                    dve.wait_ge(y_free, TWO + n - 1)
                    for j in range(NS):
                        ps = bank[4 + 2 * r + j][:, 0:D]
                        if layer == 0:
                            last = dve.tensor_tensor(y[:, r, j, :], ps, b2[:, r, :], ALU.add)
                        else:
                            last = dve.tensor_copy(y[:, r, j, :], ps)
                    last.then_inc(y_ready, 1)

                if layer == 0:
                    context_stats(e, dve, ctx_rows, ctx_loaded, ctx_read)
                all_tiles(dve, tile)

        RING = 4
        near = sb("near", [T, RING, 2, D])
        collected = [flag(f"collected{i}") for i in range(RING)]
        added = flag("added")
        with nc.Block() as block:
            @block.gpsimd
            def _(pool):
                for b in range(B):
                    if b >= RING:
                        pool.wait_ge(added, 2 * (b - RING + 1))
                    for c in range(2):
                        pool.indirect_dma_start(
                            out=near[:, b % RING, c, :], out_offset=None, in_=e.slot_y,
                            in_offset=bass.IndirectOffsetOnAxis(ap=where[:, c, b:b + 1], axis=0))\
                            .then_inc(collected[b % RING], 16)

            @block.vector
            def _(dve):
                link = Chain(dve, added)
                for b in range(B):
                    dve.wait_ge(collected[b % RING], 32 * (b // RING + 1))
                    for c in range(2):
                        link(dve.scalar_tensor_tensor(out=x[:, b, :], in0=near[:, b % RING, c, :],
                                                      scalar=share[:, c, b:b + 1], in1=x[:, b, :], op0=ALU.mult,
                                                      op1=ALU.add))
                    if layer == 0:
                        e.residual_stats(dve, b)


def gated_attention(e):
    nc, sem, bank, x, mv, rstd, ident, w = e.nc, e.sem, e.bank, e.x, e.mv, e.rstd, e.ident, e.w
    T, D, B, NG, GT, KD = e.T, e.D, e.B, e.NG, e.GT, e.KD
    EE = 512
    NE = EE // P
    with ExitStack() as st:
        def sb(name, shape):
            return st.enter_context(nc.sbuf_tensor("ga_" + name, shape, F32))

        def count(name):
            return e.count("ga_" + name)

        def flag(name):
            return sem("ga_" + name)

        rstd1 = sb("rstd1", [T, B])
        xn = sb("xn", [T, GROUP, D])
        xn1 = sb("xn1", [T, GROUP, D])
        xnT = sb("xnT", [P, KD, GT])
        uT = sb("uT", [P, NE, GT])
        zT = sb("zT", [P, GT])
        qT, kT = sb("qT", [P, GT]), sb("kT", [P, GT])
        v = sb("v", [T, GROUP, EE])
        aT = sb("aT", [T, GT])
        hT = sb("hT", [P, NE, GT])

        asked1, std1, asked2, std2, pre = flag("asked1"), flag("std1"), flag("asked2"), flag("std2"), flag("pre")
        xn_ready, xT_ps, xT_ready = count("xn_ready"), count("xT_ps"), count("xT_ready")
        xn1_ready, xn1_based = count("xn1_ready"), count("xn1_based")
        uz_ps, z_ready, u_ready = count("uz_ps"), count("z_ready"), count("u_ready")
        qk_ready = count("qk_ready")
        v_ps, v_biased, v_ready = count("v_ps"), count("v_biased"), count("v_ready")
        a_ps, a_relu, a_ready = count("a_ps"), count("a_relu"), count("a_ready")
        av_ps, h_ready, y_ps = count("av_ps"), count("h_ready"), count("y_ps")
        tail = flag("tail")

        e.start_counts()
        with nc.Block() as block:
            @block.tensor
            def _(pe):
                with pe.Fori(0, NG) as g:
                    pe.wait_ge(xn_ready, ONE + g * GROUP + GROUP)
                    for k in range(KD):
                        for s in range(GROUP):
                            last = pe.transpose(bank[k][:, s * T:(s + 1) * T], xn[:, s, k * P:(k + 1) * P],
                                                ident[0:T, 0:T])
                        last.then_inc(xT_ps, 1)
                    pe.wait_ge(xT_ready, ONE + g * 2 + 2)
                    def up(to, m):
                        for k in range(KD):
                            last = pe.matmul(to[:, 0:GT], w.in_[:, k, m * P:(m + 1) * P], xnT[:, k, :],
                                             start=(k == 0), stop=(k == KD - 1))
                        last.then_inc(uz_ps, 1)
                    up(bank[2], 2 * NE)
                    for s in range(GROUP):
                        if s >= 2:
                            pe.wait_ge(v_biased, ONE + g * GROUP + s - 1)
                        for k in range(KD):
                            last = pe.matmul(bank[4 + s % 2][0:T, :], xnT[:, k, s * T:(s + 1) * T],
                                             w.in_[:, k, EE:2 * EE], start=(k == 0), stop=(k == KD - 1))
                        last.then_inc(v_ps, 1)
                        if s >= 2:
                            pe.wait_ge(u_ready, ONE + g * NE + s - 1)
                        up(bank[6 + s % 2], s)
                    pe.wait_ge(qk_ready, ONE + g * 2 + 2)
                    for s in range(GROUP):
                        at = slice(s * T, (s + 1) * T)
                        last = pe.matmul(bank[3][0:T, at], kT[:, at], qT[:, at], start=True, stop=True)
                    last.then_inc(a_ps, 1)
                    pe.wait_ge(a_ready, ONE + g + 1)
                    pe.wait_ge(v_ready, ONE + g * GROUP + GROUP)
                    pe.wait_ge(v_biased, ONE + g * GROUP + GROUP)
                    pe.wait_ge(u_ready, ONE + g * NE + NE)
                    for m in range(NE):
                        for s in range(GROUP):
                            at = slice(s * T, (s + 1) * T)
                            last = pe.matmul(bank[4 + m][:, at], v[:, s, m * P:(m + 1) * P], aT[:, at],
                                             start=True, stop=True)
                        last.then_inc(av_ps, 1)
                    for s in range(GROUP):
                        if s >= 2:
                            pe.wait_ge(tail, g * (2 * GROUP) + 2 * (s - 2) + 1)
                        for m in range(NE):
                            if s == 0:
                                pe.wait_ge(h_ready, ONE + g * NE + m + 1)
                            last = pe.matmul(bank[s % 2][0:T, 0:D], hT[:, m, s * T:(s + 1) * T], w.out[:, m, :],
                                             start=(m == 0), stop=(m == NE - 1))
                        last.then_inc(y_ps, 1)
                    pe.wait_ge(tail, g * (2 * GROUP) + 2 * (GROUP - 1) + 1)

            @block.scalar
            def _(act):
                e.make_rstd_act(act, std1, asked1, e.norm_tmp)
                e.make_rstd_act(act, std2, asked2, e.norm_tmp)
                with act.Fori(0, NG) as g:
                    for k in range(KD):
                        act.wait_ge(xT_ps, ONE + g * 2 + k + 1)
                        act.wait_ge(uz_ps, ONE + g * (NE + 1))
                        act.activation(xnT[:, k, :], bank[k][:, 0:GT], ACT.Copy).then_inc(xT_ready, 1)
                    act.wait_ge(uz_ps, ONE + g * (NE + 1) + 1)
                    act.wait_ge(qk_ready, ONE + g * 2)
                    act.activation(zT[:], bank[2][:, 0:GT], ACT.Silu, bias=w.b_in_u[:, 8:9]).then_inc(z_ready, 1)
                    for s in range(GROUP):
                        act.wait_ge(v_biased, ONE + g * GROUP + s + 1)
                        act.activation(v[:, s, :], v[:, s, :], ACT.Silu).then_inc(v_ready, 1)
                        act.wait_ge(uz_ps, ONE + g * (NE + 1) + s + 2)
                        act.wait_ge(h_ready, ONE + g * NE)
                        act.activation(uT[:, s, :], bank[6 + s % 2][:, 0:GT], ACT.Silu,
                                       bias=w.b_in_u[:, s:s + 1]).then_inc(u_ready, 1)
                    act.wait_ge(a_ps, ONE + g + 1)
                    act.activation(aT[:], bank[3][0:T, 0:GT], ACT.Relu, scale=1.0 / T).then_inc(a_relu, 1)

            @block.gpsimd
            def _(pool):
                with pool.Fori(0, NG) as g:
                    pool.wait_ge(xn1_ready, ONE + g * GROUP + GROUP)
                    pool.tensor_tensor(xn1[:], xn1[:], wide(w.b_out[:].unsqueeze(1), 1, GROUP), ALU.add)\
                        .then_inc(xn1_based, 1)

            @block.vector
            def _(dve):
                chain = Chain(dve, pre)
                e.make_rstd_dve(dve, chain, std1, asked1, mv, rstd1[:], e.norm_tmp, False, e.stat6)
                e.make_rstd_dve(dve, chain, std2, asked2, mv, rstd[:], e.norm_tmp, True)
                with dve.Fori(0, NG) as g:
                    dve.wait_ge(xT_ps, ONE + g * 2)
                    for s in range(GROUP):
                        b = g * GROUP + s
                        dve.tensor_scalar(xn[:, s, :], x[:, b, :], mv[:, b, 0:1], rstd[:, bass.ds(b, 1)],
                                          ALU.subtract, ALU.mult).then_inc(xn_ready, 1)
                    for s in range(GROUP):
                        b = g * GROUP + s
                        dve.tensor_scalar(xn1[:, s, :], x[:, b, :], mv[:, b, 0:1], rstd1[:, bass.ds(b, 1)],
                                          ALU.subtract, ALU.mult).then_inc(xn1_ready, 1)
                    for s in range(GROUP):
                        dve.wait_ge(v_ps, ONE + g * GROUP + s + 1)
                        dve.wait_ge(av_ps, ONE + g * NE)
                        dve.tensor_tensor(v[:, s, :], bank[4 + s % 2][0:T, :], w.b_in_v[:], ALU.add)\
                           .then_inc(v_biased, 1)
                        if s == 1:
                            dve.wait_ge(z_ready, ONE + g + 1)
                            dve.wait_ge(a_ps, ONE + g)
                            dve.tensor_scalar(qT[:], zT[:], w.gq[:, 0:1], w.gq[:, 1:2], ALU.mult,
                                              ALU.add).then_inc(qk_ready, 1)
                            dve.tensor_scalar(kT[:], zT[:], w.gq[:, 2:3], w.gq[:, 3:4], ALU.mult,
                                              ALU.add).then_inc(qk_ready, 1)
                    dve.wait_ge(a_relu, ONE + g + 1)
                    dve.tensor_tensor(aT[:], aT[:], aT[:], ALU.mult).then_inc(a_ready, 1)
                    for m in range(NE):
                        dve.wait_ge(av_ps, ONE + g * NE + m + 1)
                        dve.wait_ge(u_ready, ONE + g * NE + m + 1)
                        dve.tensor_tensor(hT[:, m, :], bank[4 + m][:, 0:GT], uT[:, m, :], ALU.mult)\
                           .then_inc(h_ready, 1)
                    dve.wait_ge(xn1_based, ONE + g + 1)
                    link = Chain(dve, tail, g * (2 * GROUP), 2 * GROUP)
                    for s in range(GROUP):
                        b = g * GROUP + s
                        dve.wait_ge(y_ps, ONE + b + 1)
                        link(dve.tensor_tensor(xn1[:, s, :], xn1[:, s, :], bank[s % 2][0:T, 0:D], ALU.add))
                        link(dve.tensor_tensor(x[:, b, :], x[:, b, :], xn1[:, s, :], ALU.add))
                        e.residual_stats(dve, b, s)
                    link.close()


def kernel(**inputs):
    import concourse.bacc as bacc
    from concourse.bass_utils import run_bass_kernel_spmd

    a = {k: np.asarray(v) for k, v in inputs.items()}
    a["L0_Wq"], a["L0_Wk"] = a["L0_attn_W_qk"][:, 0::2], a["L0_attn_W_qk"][:, 1::2]
    a["L0_bq"], a["L0_bk"] = a["L0_attn_b_qk"][0::2], a["L0_attn_b_qk"][1::2]
    for n in "qkvo":
        a[f"L0_xW{n}_T"] = a.pop(f"L0_xattn_W{n}").T
    a["router_T"] = a.pop("L1_ffn_router_w").T
    a["ctx_T"] = a["ctx_768"].transpose(2, 0, 1)
    del a["L0_attn_W_qk"], a["L0_attn_b_qk"]
    for name in ("L0_bq", "L0_bk", "L0_attn_b_v", "L1_attn_ln_g", "L1_attn_ln_b", "L0_xattn_bq", "L0_xattn_bk",
                 "L1_xattn_bq", "L1_xattn_bk", "L1_xattn_norm_g", "L1_xattn_norm_b"):
        a[name] = a[name].reshape(-1, P).T
    a["L0_b1_cols"] = a["L0_ffn_b1"].reshape(8, -1, P).transpose(0, 2, 1)
    a["L1_b_in_cols"] = a["L1_attn_b_in"].reshape(-1, P).T
    a = {k: np.ascontiguousarray(v) for k, v in a.items()}

    nc = bacc.Bacc("TRN2", target_bir_lowering=False, num_devices=1)
    d = {k: nc.dram_tensor(f"in_{k}", v.shape, mybir.dt.from_np(v.dtype), kind="ExternalInput").ap()
         for k, v in a.items()}
    out = nc.dram_tensor("out_x", a["x"].shape, F32, kind="ExternalOutput").ap()
    decoder(nc, d, out)
    r = run_bass_kernel_spmd(nc, [{f"in_{k}": v for k, v in a.items()}], core_ids=[0])
    return r.results[0]["out_x"]
```
